# Optimizing a Trainium2 kernel written in Bass

```python
import numpy as np
import jax
import jax.numpy as jnp

def _softmax(x, axis=-1):
    return jax.nn.softmax(x, axis=axis)

def _gelu(x):
    return jax.nn.gelu(x, approximate=True)

def _silu(x):
    return jax.nn.silu(x)

def _sigmoid(x):
    return jax.nn.sigmoid(x)

def _layernorm(x, axis=-1, eps=1e-05):
    m = jnp.mean(x, axis=axis, keepdims=True)
    v = jnp.var(x, axis=axis, keepdims=True)
    return (x - m) / jnp.sqrt(v + eps)

def _scatter_add(tgt, idx, src, axis=0):
    return tgt.at[idx].add(src)

def _segment_sum(src, seg, n):
    return jax.ops.segment_sum(src, seg, n)
kernel_name = 'mk_gps_d1_gnn_r8_6d84d8'

def setup_inputs(seed: int=0):
    np.random.seed(seed)
    _w = jnp.asarray

    def _rec_inputs():
        import jax
        import jax.numpy as jnp
        _gk = jax.random.key(seed)
        x = -0.0003713 + 1 * jax.random.normal(jax.random.fold_in(_gk, 1), (6250, 256), jnp.float32)
        src = jax.random.randint(jax.random.fold_in(_gk, 2), (200000,), 0, 6250, jnp.int32)
        dst = jax.random.randint(jax.random.fold_in(_gk, 3), (200000,), 0, 6250, jnp.int32)
        _o = jnp.argsort(dst, stable=True)
        src = src[_o]
        dst = dst[_o]
        return (x, src, dst)
    x, src, dst = _rec_inputs()

    def _L0_gnn_setup():
        import jax, jax.numpy as jnp
        import numpy as np
        N, E = (6250, 100000)
        IN, H, C = (256, 8, 32)
        NEG_SLOPE = 0.2
        EPS = 1e-05
        key = jax.random.key(seed)
        ks = jax.random.split(key, 6)
        x = jax.random.normal(ks[0], (N, IN), jnp.float32)
        edge_index = jax.random.randint(ks[1], (2, E), 0, N, dtype=jnp.int32)
        W = jax.random.normal(ks[2], (IN, H * C), jnp.float32) / np.sqrt(IN).astype(np.float32)
        att_src = jax.random.normal(ks[3], (H, C), jnp.float32) * 0.1
        att_dst = jax.random.normal(ks[4], (H, C), jnp.float32) * 0.1
        bias = jnp.zeros((H * C,), jnp.float32)
        gamma = jnp.ones((H * C,), jnp.float32)
        beta = jnp.zeros((H * C,), jnp.float32)
        return {'x': x, 'edge_index': edge_index, 'W': W, 'att_src': att_src, 'att_dst': att_dst, 'bias': bias, 'gamma': gamma, 'beta': beta}
    _L0_gnn_all = _L0_gnn_setup()
    _L0_gnn_in = {k: v for k, v in _L0_gnn_all.items() if k in ('W', 'att_src', 'att_dst', 'bias', 'gamma', 'beta')}
    del _L0_gnn_all

    def _L0_mix_setup():
        import jax, jax.numpy as jnp
        import numpy as np
        DIM = 256
        HEADS = 4
        DIM_HEAD = 32
        NUM_MEM = 4
        HIDDEN = HEADS * DIM_HEAD
        SCALE = DIM_HEAD ** (-0.5)

        def rmsnorm(x, g):
            n = jnp.linalg.norm(x, axis=-1, keepdims=True)
            return x / jnp.maximum(n, 1e-12) * g * x.shape[-1] ** 0.5
        key = jax.random.key(seed)
        ks = jax.random.split(key, 8)
        B, N = (4, 2048)
        return {'x': jax.random.normal(ks[0], (B, N, DIM), jnp.float32), 't': jax.random.normal(ks[1], (B,), jnp.float32), 'w_qkv': jax.random.normal(ks[2], (DIM, 3 * HIDDEN), jnp.float32) * 0.02, 'mem_kv': jax.random.normal(ks[3], (2, HEADS, DIM_HEAD, NUM_MEM), jnp.float32), 'w_out': jax.random.normal(ks[4], (HIDDEN, DIM), jnp.float32) * 0.02, 'b_out': jnp.zeros((DIM,), jnp.float32), 'g_out': jnp.ones((DIM,), jnp.float32), 'g_pre': jnp.ones((DIM,), jnp.float32)}
    _L0_mix_all = _L0_mix_setup()
    _L0_mix_in = {k: v for k, v in _L0_mix_all.items() if k in ('t', 'w_qkv', 'mem_kv', 'w_out', 'b_out', 'g_out', 'g_pre')}
    del _L0_mix_all

    def _L0_ffn_setup():
        import math
        import jax, jax.numpy as jnp
        import numpy as np
        CAPACITY_FACTOR = 1.25
        TOP_K = 2
        LN_EPS = 1e-05

        def _layer_norm(x, gamma, beta):
            mu = jnp.mean(x, axis=-1, keepdims=True)
            var = jnp.var(x, axis=-1, keepdims=True)
            return (x - mu) * jax.lax.rsqrt(var + LN_EPS) * gamma + beta
        key = jax.random.key(seed)
        ks = jax.random.split(key, 4)
        B, S, D, F, E = (8, 512, 256, 512, 8)
        x = jax.random.normal(ks[0], (B, S, D), dtype=jnp.float32)
        Wr = jax.random.normal(ks[1], (D, E), dtype=jnp.float32) / np.sqrt(D)
        br = jnp.zeros((E,), jnp.float32)
        W1 = jax.random.normal(ks[2], (E, D, F), dtype=jnp.float32) / np.sqrt(D)
        b1 = jnp.zeros((E, F), jnp.float32)
        W2 = jax.random.normal(ks[3], (E, F, D), dtype=jnp.float32) / np.sqrt(F)
        b2 = jnp.zeros((E, D), jnp.float32)
        gamma = jnp.ones((D,), jnp.float32)
        beta = jnp.zeros((D,), jnp.float32)
        return {'x': x, 'Wr': Wr, 'br': br, 'W1': W1, 'b1': b1, 'W2': W2, 'b2': b2, 'gamma': gamma, 'beta': beta}
    _L0_ffn_all = _L0_ffn_setup()
    _L0_ffn_in = {k: v for k, v in _L0_ffn_all.items() if k in ('Wr', 'br', 'W1', 'b1', 'W2', 'b2', 'gamma', 'beta')}
    del _L0_ffn_all
    return {'x': x, 'src': src, 'dst': dst, 'L0_gnn_W': _L0_gnn_in['W'], 'L0_gnn_att_src': _L0_gnn_in['att_src'], 'L0_gnn_att_dst': _L0_gnn_in['att_dst'], 'L0_gnn_bias': _L0_gnn_in['bias'], 'L0_gnn_gamma': _L0_gnn_in['gamma'], 'L0_gnn_beta': _L0_gnn_in['beta'], 'L0_mix_t': _L0_mix_in['t'], 'L0_mix_w_qkv': _L0_mix_in['w_qkv'], 'L0_mix_mem_kv': _L0_mix_in['mem_kv'], 'L0_mix_w_out': _L0_mix_in['w_out'], 'L0_mix_b_out': _L0_mix_in['b_out'], 'L0_mix_g_out': _L0_mix_in['g_out'], 'L0_mix_g_pre': _L0_mix_in['g_pre'], 'L0_ffn_Wr': _L0_ffn_in['Wr'], 'L0_ffn_br': _L0_ffn_in['br'], 'L0_ffn_W1': _L0_ffn_in['W1'], 'L0_ffn_b1': _L0_ffn_in['b1'], 'L0_ffn_W2': _L0_ffn_in['W2'], 'L0_ffn_b2': _L0_ffn_in['b2'], 'L0_ffn_gamma': _L0_ffn_in['gamma'], 'L0_ffn_beta': _L0_ffn_in['beta']}

def reference(x, src, dst, L0_gnn_W, L0_gnn_att_src, L0_gnn_att_dst, L0_gnn_bias, L0_gnn_gamma, L0_gnn_beta, L0_mix_t, L0_mix_w_qkv, L0_mix_mem_kv, L0_mix_w_out, L0_mix_b_out, L0_mix_g_out, L0_mix_g_pre, L0_ffn_Wr, L0_ffn_br, L0_ffn_W1, L0_ffn_b1, L0_ffn_W2, L0_ffn_b2, L0_ffn_gamma, L0_ffn_beta):
    import jax
    import jax.numpy as jnp

    def _L0_gnn_ref(x, edge_index, W, att_src, att_dst, bias, gamma, beta):
        import jax, jax.numpy as jnp
        import numpy as np
        N, E = (6250, 100000)
        IN, H, C = (256, 8, 32)
        NEG_SLOPE = 0.2
        EPS = 1e-05
        n = x.shape[0]
        xl = (x @ W).reshape(n, H, C)
        a_src = jnp.einsum('nhc,hc->nh', xl, att_src)
        a_dst = jnp.einsum('nhc,hc->nh', xl, att_dst)
        loops = jnp.arange(n, dtype=edge_index.dtype)
        src = jnp.concatenate([edge_index[0], loops])
        dst = jnp.concatenate([edge_index[1], loops])
        logits = jax.nn.leaky_relu(a_src[src] + a_dst[dst], NEG_SLOPE)
        seg_max = jax.ops.segment_max(logits, dst, num_segments=n)
        ex = jnp.exp(logits - seg_max[dst])
        denom = jax.ops.segment_sum(ex, dst, num_segments=n)
        alpha = ex / denom[dst]
        msgs = xl[src] * alpha[:, :, None]
        out = jax.ops.segment_sum(msgs, dst, num_segments=n).reshape(n, H * C) + bias
        mu = jnp.mean(out, axis=-1, keepdims=True)
        var = jnp.var(out, axis=-1, keepdims=True)
        return (out - mu) / jnp.sqrt(var + EPS) * gamma + beta

    def _L0_mix_ref(x, t, w_qkv, mem_kv, w_out, b_out, g_out, g_pre):
        import jax, jax.numpy as jnp
        import numpy as np
        DIM = 256
        HEADS = 4
        DIM_HEAD = 32
        NUM_MEM = 4
        HIDDEN = HEADS * DIM_HEAD
        SCALE = DIM_HEAD ** (-0.5)

        def rmsnorm(x, g):
            n = jnp.linalg.norm(x, axis=-1, keepdims=True)
            return x / jnp.maximum(n, 1e-12) * g * x.shape[-1] ** 0.5
        b, n, c = x.shape
        xn = rmsnorm(x, g_pre)
        qkv = xn @ w_qkv
        q, k, v = jnp.split(qkv, 3, axis=-1)

        def to_heads(z):
            return z.reshape(b, n, HEADS, DIM_HEAD).transpose(0, 2, 3, 1)
        q, k, v = map(to_heads, (q, k, v))
        mk = jnp.broadcast_to(mem_kv[0], (b, HEADS, DIM_HEAD, NUM_MEM))
        mv = jnp.broadcast_to(mem_kv[1], (b, HEADS, DIM_HEAD, NUM_MEM))
        k = jnp.concatenate([mk, k], axis=-1)
        v = jnp.concatenate([mv, v], axis=-1)
        q = jax.nn.softmax(q, axis=-2) * SCALE
        k = jax.nn.softmax(k, axis=-1)
        context = jnp.einsum('bhdn,bhen->bhde', k, v)
        out = jnp.einsum('bhde,bhdn->bhen', context, q)
        out = out.transpose(0, 3, 1, 2).reshape(b, n, HIDDEN)
        out = rmsnorm(out @ w_out + b_out, g_out)
        return out + x

    def _L0_ffn_ref(x, Wr, br, W1, b1, W2, b2, gamma, beta):
        import math
        import jax, jax.numpy as jnp
        import numpy as np
        CAPACITY_FACTOR = 1.25
        TOP_K = 2
        LN_EPS = 1e-05

        def _layer_norm(x, gamma, beta):
            mu = jnp.mean(x, axis=-1, keepdims=True)
            var = jnp.var(x, axis=-1, keepdims=True)
            return (x - mu) * jax.lax.rsqrt(var + LN_EPS) * gamma + beta
        B, S, D = x.shape
        E = Wr.shape[1]
        N = B * S
        K = TOP_K
        logits = jnp.mean(x, axis=1) @ Wr + br
        routing_weights = jax.nn.softmax(logits, axis=-1)
        capacity = float(math.ceil(N * CAPACITY_FACTOR / E))
        expected_loads = routing_weights.sum(axis=0) * (N / B)
        scale = jnp.where(expected_loads > capacity, capacity / expected_loads, 1.0)
        routing_weights = jax.nn.softmax(routing_weights * scale, axis=-1)
        rw_tok = jnp.broadcast_to(routing_weights[:, None, :], (B, S, E)).reshape(N, E)
        top_w, top_i = jax.lax.top_k(rw_tok, K)
        top_w = jax.nn.softmax(top_w, axis=-1)
        xf = x.reshape(N, D)
        h = jax.nn.gelu(jnp.einsum('nd,edf->enf', xf, W1) + b1[:, None, :], approximate=False)
        y = jnp.einsum('enf,efd->end', h, W2) + b2[:, None, :]
        w_dense = jnp.zeros((N, E), x.dtype).at[jnp.arange(N)[:, None], top_i].add(top_w)
        out = jnp.einsum('ne,end->nd', w_dense, y).reshape(B, S, D)
        out = _layer_norm(out + x, gamma, beta)
        return out
    edge_index = jnp.stack([src, dst])
    xn = _layernorm(x, axis=-1)
    x = x + _L0_gnn_ref(xn, edge_index, L0_gnn_W, L0_gnn_att_src, L0_gnn_att_dst, L0_gnn_bias, L0_gnn_gamma, L0_gnn_beta) + _L0_mix_ref(xn[None], L0_mix_t, L0_mix_w_qkv, L0_mix_mem_kv, L0_mix_w_out, L0_mix_b_out, L0_mix_g_out, L0_mix_g_pre)[0]
    x = x + _L0_ffn_ref(_layernorm(x, axis=-1)[None], L0_ffn_Wr, L0_ffn_br, L0_ffn_W1, L0_ffn_b1, L0_ffn_W2, L0_ffn_b2, L0_ffn_gamma, L0_ffn_beta)[0]
    return x

_drawn_inputs = setup_inputs


def setup_inputs(seed=0):
    import zlib

    import numpy as np

    out = dict(_drawn_inputs(seed))
    spreads = {'L0_gnn_bias': (0.0, 0.1),
     'L0_gnn_gamma': (1.0, 0.2),
     'L0_gnn_beta': (0.0, 0.1),
     'L0_mix_b_out': (0.0, 0.1),
     'L0_mix_g_out': (1.0, 0.2),
     'L0_mix_g_pre': (1.0, 0.6),
     'L0_ffn_br': (0.0, 0.1),
     'L0_ffn_b1': (0.0, 0.623),
     'L0_ffn_b2': (0.0, 0.424),
     'L0_ffn_gamma': (1.0, 0.2),
     'L0_ffn_beta': (0.0, 0.275)}
    factors = {'L0_mix_w_qkv': 8.0, 'L0_mix_mem_kv': 8.0, 'L0_mix_w_out': 8.0}
    for name, (base, spread) in spreads.items():
        noise = np.random.default_rng([zlib.crc32(name.encode()), seed]).standard_normal(out[name].shape)
        drawn = base * np.exp(spread * noise) if base else spread * noise
        out[name] = jnp.asarray(drawn.astype(out[name].dtype))
    for name, factor in factors.items():
        out[name] = (out[name] * factor).astype(out[name].dtype)
    return out
```

```python
from contextlib import ExitStack

import concourse.bass as bass
from concourse import mybir

ALU = mybir.AluOpType
ACT = mybir.ActivationFunctionType
F32 = mybir.dt.float32
BF16 = mybir.dt.bfloat16
I32 = mybir.dt.int32
U32 = mybir.dt.uint32
X = mybir.AxisListType.X
DVE = mybir.EngineType.DVE
PE = mybir.EngineType.PE
ds = bass.ds

P = 128
N, D, E = 6250, 256, 200000
H, C = 8, 32
T = -(-N // P)
LAST = N - (T - 1) * P
SUP = 7
NS = T // SUP
ROW = H * C + H
GE = 256
GR = -(-E // GE)
PAIRS = GR + T - 1
NOWHERE = T * P
QUADS = -(-PAIRS // 8) * 4
U = 4
PC = -(-(QUADS * 2 + 16) // P)
MH, MD = 4, 32
MHID = MH * MD
NMEM = 4
EX, F = 8, 512
FC = F // P
LN_EPS = 1e-5
SLOPE = 0.2
CAP = float(-(-N * 5 // (4 * EX)))
QKV0 = ROW + H


def flat(ap):
    return ap.rearrange("p a b -> p (a b)")


def gps_layer(nc, x, src, dst, W, att_src, att_dst, gnn_bias, gnn_gamma, gnn_beta, w_qkv, mem_kv, w_out, b_out,
              g_out, g_pre, Wr, br, W1, b1, W2, b2, ffn_gamma, ffn_beta, xl_dram, base_dram, edges_dram,
              pair_dram, out):
    top = ExitStack()

    def alloc(stack):
        return (lambda name, shape, dt=F32: stack.enter_context(nc.sbuf_tensor(name, shape, dt)),
                lambda name: stack.enter_context(nc.semaphore(name)))

    with top:
        top.enter_context(nc.allow_non_contiguous_dma(reason="a few hundred single words, once"))
        sb, _ = alloc(top)
        bank = [top.enter_context(nc.psum_tensor(f"bank{i}", [P, 512], F32)) for i in range(8)]
        acc = sb("acc", [P, T, ROW])
        ident = sb("ident", [P, P])
        iota_row = sb("iota_row", [P, P])
        ones = sb("ones", [P, P])
        ones_bf = sb("ones_bf", [P, P], BF16)
        node_logit = sb("node_logit", [P, T, 2 * H])
        src_idx = sb("src_idx", [P, PC * P, 2], I32)
        dst_loc = sb("dst_loc", [P, PC * P, 2])
        pair_tile = sb("pair_tile", [1, PC * P], I32)
        mix_w = sb("mix_w", [P, D])
        stats = sb("stats", [P, T, 2])
        y_sum = sb("y_sum", [P, 2])
        qstack = ExitStack()
        qsb, _ = alloc(qstack)
        qkv = qsb("qkv", [P, T, 3 * MHID + 1])

        pair_tables(nc, dst, src, edges_dram, pair_dram, ident, iota_row, ones, ones_bf, src_idx, dst_loc,
                    pair_tile, bank)
        project(nc, x, W, att_src, att_dst, w_qkv, g_pre, xl_dram, base_dram, acc, node_logit, qkv, ident, bank)
        contexts(nc, mem_kv, w_out, acc, node_logit, qkv, ident, ones, mix_w, bank)
        edge_phase(nc, xl_dram, acc, node_logit, src_idx, dst_loc, pair_tile, ident, iota_row, bank)
        combine(nc, b_out, g_out, gnn_bias, gnn_gamma, gnn_beta, base_dram, acc, stats, y_sum, qkv, mix_w, ident, ones, bank)
        qstack.close()
        experts(nc, Wr, br, W1, b1, W2, b2, ffn_gamma, ffn_beta, acc, stats, y_sum, ident, ones, bank, out)


def pair_tables(nc, dst, src, edges_dram, pair_dram, ident, iota_row, ones, ones_bf, src_idx, dst_loc, pair_tile,
                bank):
    full = E // GE
    rest = E - full * GE
    with ExitStack() as ctx:
        def sb(name, shape, dt=F32):
            return ctx.enter_context(nc.sbuf_tensor("pt_" + name, shape, dt))

        def sem(name):
            return ctx.enter_context(nc.semaphore(name))

        pad = sb("pad", [1, 4 * GE], I32)
        iota_i = sb("iota_i", [P, P], I32)
        part_i = sb("part_i", [P, 1], I32)
        part_f = sb("part_f", [P, 1])
        first_i = sb("first_i", [P, 2 * PC], I32)
        first_f = sb("first_f", [P, 2 * PC])
        start_i = sb("start_i", [P, T + 1], I32)
        start_f = sb("start_f", [P, T + 1])
        below = sb("below", [P, 2 * PC, T + 1], BF16)
        group_count = sb("group_count", [P, 2, T + 1])
        count = sb("count", [P, T])
        one_t = sb("one_t", [P, T])
        base = sb("base", [P, T + 1])
        shift = sb("shift", [P, T])
        step = sb("step", [P, T])
        pair_i = sb("pair_i", [P, PC], I32)
        pair_f = sb("pair_f", [P, PC])
        reached = sb("reached", [P, PC, T])
        product = sb("product", [P, PC, T])
        tile_f = sb("tile_f", [P, PC])
        tile_i = sb("tile_i", [P, PC], I32)
        tile_node = sb("tile_node", [P, PC])
        row_f = sb("row_f", [P, PC])
        row_i = sb("row_i", [P, PC], I32)
        group = sb("group", [P, PC, 2 * GE], I32)
        group_f = sb("group_f", [P, 2, 2 * GE])
        s_iota, s_pad, s_edges, s_first = sem("s_iota"), sem("s_pad"), sem("s_edges"), sem("s_first")
        s_below, s_counts, s_row, s_group, s_table = (sem("s_below"), sem("s_counts"), sem("s_row"), sem("s_group"),
                                                      sem("s_table"))
        s_pt, s_gf, s_tr, s_idx, s_chain = sem("s_pt"), sem("s_gf"), sem("s_tr"), sem("s_idx"), sem("s_chain")
        block = ctx.enter_context(nc.Block())
        COPIES = 8

        @block.sync
        def _(sp):
            sp.dma_start(edges_dram[0:full, 0:GE], src[0:full * GE].rearrange("(r w) -> r w", w=GE)).then_inc(s_edges, 16)
            sp.dma_start(edges_dram[0:full, GE:2 * GE], dst[0:full * GE].rearrange("(r w) -> r w", w=GE)).then_inc(s_edges, 16)
            sp.dma_start(edges_dram[full:full + 1, 0:rest], src[full * GE:E].rearrange("(r w) -> r w", r=1)).then_inc(s_edges, 16)
            sp.dma_start(edges_dram[full:full + 1, GE:GE + rest], dst[full * GE:E].rearrange("(r w) -> r w", r=1)).then_inc(s_edges, 16)
            sp.wait_ge(s_pad, 2)
            sp.dma_start(edges_dram[full:full + 1, rest:GE], pad[0:1, 0:GE - rest]).then_inc(s_edges, 16)
            sp.dma_start(edges_dram[full:full + 1, GE + rest:2 * GE], pad[0:1, GE:2 * GE - rest]).then_inc(s_edges, 16)
            sp.dma_start(edges_dram[full + 1:full + 2, 0:GE], pad[0:1, 0:GE]).then_inc(s_edges, 16)
            sp.dma_start(edges_dram[full + 1:full + 2, GE:2 * GE], pad[0:1, GE:2 * GE]).then_inc(s_edges, 16)
            sp.wait_ge(s_table, 1)
            sp.dma_start(pair_dram.rearrange("(c p) -> p c", p=P), tile_i[:]).then_inc(s_pt, 16)
            sp.wait_ge(s_pt, 16)
            sp.dma_start(pair_tile[:], pair_dram.rearrange("(a j) -> a j", a=1)).then_inc(s_pt, 16)
            sp.wait_ge(s_pt, 32)
            sp.wait_ge(s_edges, 16 * COPIES)

        @block.scalar
        def _(act):
            act.wait_ge(s_pad, 3)
            for half, (offset, groups) in enumerate(((0, GR), (GE - 1, full))):
                whole = groups // P
                tail = groups - whole * P
                act.dma_start(first_i[:, half * PC:half * PC + whole],
                              dst[0:whole * P * GE].rearrange("(c p w) -> p c w", p=P, w=GE)[:, :, offset]
                              ).then_inc(s_first, 16)
                if offset:
                    tail_ap = dst[whole * P * GE:(whole * P + tail) * GE].rearrange("(p w) -> p w", w=GE)[:, offset:offset + 1]
                    act.dma_start(first_i[0:tail, half * PC + whole:half * PC + whole + 1], tail_ap).then_inc(s_first, 16)
                else:
                    tail_ap = dst[whole * P * GE:(whole * P + tail - 1) * GE].rearrange("(p w) -> p w", w=GE)[:, 0:1]
                    act.dma_start(first_i[0:tail - 1, whole:whole + 1], tail_ap).then_inc(s_first, 16)
                    act.dma_start(first_i[tail - 1:tail, whole:whole + 1],
                                  dst[full * GE:full * GE + 1].rearrange("(p w) -> p w", w=1)).then_inc(s_first, 16)
            for c in range(PC):
                for half in range(2):
                    n = 2 * c + half
                    act.wait_ge(s_tr, n + 1)
                    t = bank[n % 2]
                    nc.scalar.copy(src_idx[:, c * P:(c + 1) * P, half], t[:, 0:P])
                    nc.scalar.copy(dst_loc[:, c * P:(c + 1) * P, half], t[:, P:2 * P]).then_inc(s_idx, 1)

        @block.gpsimd
        def _(pool):
            nc.gpsimd.iota(iota_i[:], pattern=[[1, P]], base=0, channel_multiplier=0)
            nc.gpsimd.iota(part_i[:], pattern=[[0, 1]], base=0, channel_multiplier=1)
            nc.gpsimd.iota(start_i[:], pattern=[[P, T + 1]], base=0, channel_multiplier=0)
            nc.gpsimd.iota(pair_i[:], pattern=[[P, PC]], base=0, channel_multiplier=1).then_inc(s_iota, 1)
            pool.wait_ge(s_row, 1)
            pool.wait_ge(s_edges, 16 * COPIES)
            for c in range(PC):
                nc.gpsimd.indirect_dma_start(out=group[:, c, :], out_offset=None, in_=edges_dram,
                                             in_offset=bass.IndirectOffsetOnAxis(ap=row_i[:, c:c + 1], axis=0)
                                             ).then_inc(s_group, 16)
            pool.wait_ge(s_group, 16 * PC)

        @block.vector
        def _(dve):
            links = [0]

            def link(ins):
                links[0] += 1
                ins.then_inc(s_chain, 1)
                dve.wait_ge(s_chain, links[0])

            nc.vector.memset(pad[:, 0:GE], 0).then_inc(s_pad, 1)
            nc.vector.memset(pad[:, GE:], NOWHERE).then_inc(s_pad, 1)
            nc.vector.memset(first_i[:], NOWHERE).then_inc(s_pad, 1)
            nc.vector.memset(ones[:], 1.0)
            nc.vector.memset(ones_bf[:], 1.0)
            nc.vector.memset(one_t[:], 1.0)
            nc.vector.memset(base[:, 0:1], 0.0)
            dve.wait_ge(s_iota, 1)
            nc.vector.tensor_copy(iota_row[:], iota_i[:])
            nc.vector.tensor_copy(pair_f[:], pair_i[:])
            nc.vector.tensor_copy(start_f[:], start_i[:])
            link(nc.vector.tensor_copy(part_f[:], part_i[:]))
            nc.vector.tensor_scalar(ident[:], iota_row[:], part_f[:, 0:1], None, ALU.is_equal)
            dve.wait_ge(s_first, 16 * 5)
            link(nc.vector.tensor_copy(first_f[:], first_i[:]))
            nc.vector.tensor_tensor(below[:], first_f[:].unsqueeze(2).to_broadcast([P, 2 * PC, T + 1]),
                                    start_f[:].unsqueeze(1).to_broadcast([P, 2 * PC, T + 1]), ALU.is_lt
                                    ).then_inc(s_below, 1)
            dve.wait_ge(s_counts, 1)
            link(nc.vector.tensor_copy(flat(group_count[:]), bank[0][:, 0:2 * (T + 1)]))
            begun, ended = group_count[:, 0, :], group_count[:, 1, :]
            link(nc.vector.tensor_tensor(count[:], begun[:, 1:T + 1], ended[:, 0:T], ALU.subtract))
            link(nc.vector.tensor_tensor_scan(base[:, 1:T + 1], one_t[:], count[:], 0.0, ALU.mult, ALU.add))
            link(nc.vector.tensor_tensor(shift[:], ended[:, 0:T], base[:, 0:T], ALU.subtract))
            link(nc.vector.tensor_copy(step[:, 0:1], shift[:, 0:1]))
            link(nc.vector.tensor_tensor(step[:, 1:T], shift[:, 1:T], shift[:, 0:T - 1], ALU.subtract))
            pairs = pair_f[:].unsqueeze(2).to_broadcast([P, PC, T])
            link(nc.vector.tensor_tensor(reached[:], base[:, 1:T + 1].unsqueeze(1).to_broadcast([P, PC, T]), pairs,
                                         ALU.is_le))
            link(nc.vector.tensor_reduce(tile_f[:], reached[:], X, ALU.add))
            link(nc.vector.tensor_scalar(tile_f[:], tile_f[:], float(T - 1), None, ALU.min))
            nc.vector.tensor_copy(tile_i[:], tile_f[:]).then_inc(s_table, 1)
            nc.vector.tensor_scalar(tile_node[:], tile_f[:], float(P), None, ALU.mult)
            link(nc.vector.tensor_tensor(reached[:], base[:, 0:T].unsqueeze(1).to_broadcast([P, PC, T]), pairs,
                                         ALU.is_le))
            link(nc.vector.tensor_tensor(product[:], reached[:], step[:].unsqueeze(1).to_broadcast([P, PC, T]),
                                         ALU.mult))
            link(nc.vector.tensor_reduce(row_f[:], product[:], X, ALU.add))
            link(nc.vector.tensor_tensor(row_f[:], row_f[:], pair_f[:], ALU.add))
            link(nc.vector.tensor_scalar(row_f[:], row_f[:], float(full + 1), 0.0, ALU.min, ALU.max))
            nc.vector.tensor_copy(row_i[:], row_f[:]).then_inc(s_row, 1)
            dve.wait_ge(s_group, 16 * PC)
            for c in range(PC):
                if c >= 2:
                    dve.wait_ge(s_tr, 2 * (c - 1))
                link(nc.vector.tensor_copy(group_f[:, c % 2, :], group[:, c, :]))
                nc.vector.tensor_scalar(group_f[:, c % 2, GE:], group_f[:, c % 2, GE:], tile_node[:, c:c + 1], None,
                                        ALU.subtract).then_inc(s_gf, 1)

        @block.tensor
        def _(pe):
            pe.wait_ge(s_below, 1)
            for half in range(2):
                for c in range(PC):
                    last = nc.tensor.matmul(bank[0][:, half * (T + 1):(half + 1) * (T + 1)], ones_bf[:],
                                            below[:, half * PC + c, :], start=(c == 0), stop=(c == PC - 1))
            last.then_inc(s_counts, 1)
            for c in range(PC):
                pe.wait_ge(s_gf, c + 1)
                for half in range(2):
                    n = 2 * c + half
                    if n >= 2:
                        pe.wait_ge(s_idx, n - 1)
                    for kind in range(2):
                        last = nc.tensor.transpose(bank[n % 2][:, kind * P:(kind + 1) * P],
                                                   group_f[:, c % 2, kind * GE + half * P:kind * GE + (half + 1) * P],
                                                   ident[:])
                    last.then_inc(s_tr, 1)


def project(nc, x, W, att_src, att_dst, w_qkv, g_pre, xl_dram, base_dram, acc, node_logit, qkv, ident, bank):
    with ExitStack() as ctx:
        def sb(name, shape, dt=F32):
            return ctx.enter_context(nc.sbuf_tensor("pj_" + name, shape, dt))

        def sem(name):
            return ctx.enter_context(nc.semaphore(name))

        w = sb("w", [P, 2, QKV0 + 3 * MHID])
        gp = sb("gp", [P, 2])
        att = sb("att", [P, 2, D])
        att_w = sb("att_w", [P, 4, D])
        xin = sb("xin", [P, 2, SUP, D])
        xn = sb("xn", [P, 2, SUP, D])
        xnT = sb("xnT", [P, 2, 2, P])
        bn = sb("bn", [P, 2, SUP, 6])
        mv = sb("mv", [P, 2, SUP, 2])
        rstd = sb("rstd", [P, 2, SUP])
        junk = sb("junk", [P, SUP, D])
        sumsq = sb("sumsq", [P, 2, SUP])
        rnorm = sb("rnorm", [P, 2, SUP])
        (s_var, s_dev, s_squared) = (sem("pj_" + n) for n in ("var", "dev", "squared"))
        s_w, s_wready, s_chain, s_xn, s_sq, s_rn, s_tp, s_xt, s_mm, s_xl, s_base, s_xls, s_fence = (
            sem(n) for n in ("s_w", "s_wready", "s_chain", "s_xn", "s_sq", "s_rn", "s_tp", "s_xt", "s_mm", "s_xl",
                             "s_base", "s_xls", "s_fence"))
        s_x = [sem("s_x_even"), sem("s_x_odd")]
        s_stored = [sem("s_stored_even"), sem("s_stored_odd")]
        block = ctx.enter_context(nc.Block())
        A0 = 11
        LINKS = 5

        MID = 2

        def supers(eng, body):
            last = (NS - 1) // 2
            with eng.Fori(0, last - 1) as i:
                for b in range(2):
                    body(i, b, P)
            for b in range(2):
                body(last - 1, b, P)
            body(last, 0, LAST)

        def node_rows(dram, s, rows):
            if rows == P:
                return [(dram[ds(s * (SUP * P), SUP * P), :].rearrange("(g p) d -> p g d", p=P), slice(0, SUP), P)]
            whole = s * SUP * P + (SUP - 1) * P
            return [(dram[s * SUP * P:whole, :].rearrange("(g p) d -> p g d", p=P), slice(0, SUP - 1), P),
                    (dram[whole:whole + rows, :].unsqueeze(1), slice(SUP - 1, SUP), rows)]

        @block.sync
        def _(sp):
            sp.dma_start(w[:, :, 0:D], W.rearrange("(k p) n -> p k n", p=P)).then_inc(s_w, 16)
            sp.dma_start(w[:, :, QKV0:], w_qkv.rearrange("(k p) n -> p k n", p=P)).then_inc(s_w, 16)
            sp.dma_start(gp[:], g_pre.rearrange("(k p) -> p k", p=P)).then_inc(s_w, 16)
            for a, v in enumerate((att_src, att_dst)):
                sp.dma_start(att[:, a, :], v.rearrange("h c -> (h c)").partition_broadcast(P)).then_inc(s_w, 16)
            for b in range(2):
                sp.sem_inc(s_stored[b], 16)

            def load(i, b, rows):
                sp.wait_ge(s_stored[b], i * 16 + 16)
                for dram, g, r in node_rows(x, i * 2 + b, rows):
                    sp.dma_start(xin[0:r, b, g, :], dram).then_inc(s_x[b], 16)

            def store(i, b, rows):
                s = i * 2 + b
                sp.wait_ge(s_base, s + 1)
                for dram, g, r in node_rows(base_dram, s, rows):
                    sp.dma_start(dram, xin[0:r, b, g, :]).then_inc(s_stored[b], 16)
                sp.wait_ge(s_xl, s * SUP + SUP)
                for dram, g, r in node_rows(xl_dram, s, rows):
                    sp.dma_start(dram, acc[0:r, ds(s * SUP + g.start, g.stop - g.start), :]).then_inc(s_xls, 16)

            last = (NS - 1) // 2
            load(0, 0, P)
            load(0, 1, P)
            with sp.Fori(0, last - 1) as i:
                for b in range(2):
                    store(i, b, P)
                    load(i + 1, b, P)
            store(last - 1, 0, P)
            load(last, 0, LAST)
            store(last - 1, 1, P)
            store(last, 0, LAST)
            sp.wait_ge(s_stored[0], 16 + 16 * (last + 2))
            sp.wait_ge(s_stored[1], 16 + 16 * last)
            sp.wait_ge(s_xls, 16 * (NS + 1))

        @block.gpsimd
        def _(pool):
            def body(i, b, rows):
                s = i * 2 + b
                pool.wait_ge(s_xn, s + 1)
                pool.sem_inc(s_fence, 1)
                nc.gpsimd.tensor_tensor(flat(xin[:, b, :, :]), flat(xin[:, b, :, :]), flat(xn[:, b, :, :]),
                                        ALU.add).then_inc(s_base, 1)
            supers(pool, body)

        @block.vector
        def _(dve):
            links = [0]

            def link(ins, s=None):
                links[0] += 1
                ins.then_inc(s_chain, 1)
                dve.wait_ge(s_chain, links[0] if s is None else s * LINKS + (A0 + links[0]))

            dve.wait_ge(s_w, 16 * 5)
            for k in range(2):
                for a in range(2):
                    n = 2 * k + a
                    link(nc.vector.tensor_tensor(att_w[:, n, :], w[:, k, 0:D], att[:, a, :], ALU.mult))
                    link(nc.vector.tensor_reduce(w[:, k, D + a * H:D + (a + 1) * H],
                                                 att_w[:, n, :].rearrange("p (h c) -> p h c", c=C), X, ALU.add))
            for k in range(2):
                link(nc.vector.tensor_scalar(w[:, k, QKV0:], w[:, k, QKV0:], gp[:, k:k + 1], None, ALU.mult))
            link(nc.vector.memset(qkv[:, :, 3 * MHID:], 1.0))
            assert links[0] == A0
            dve.sem_inc(s_wready, 1)

            def variance(i, b, full, s_at=None):
                dve.wait_ge(s_x[b], i * 16 + (16 if full else 32))
                for g in range(SUP):
                    last = nc.vector.bn_stats(bn[:, b, g, :], xin[:, b, g, :])
                link(last, s_at)
                dve.sem_inc(s_fence, 1)
                for g in range(SUP):
                    last = nc.vector.bn_aggr(mv[:, b, g, :], bn[:, b, g, :])
                link(last, s_at)
                nc.vector.tensor_scalar(rstd[:, b, :], mv[:, b, :, 1], LN_EPS, None, ALU.add).then_inc(s_var, 1)

            def normalize(i, b, s_at=None):
                dve.wait_ge(s_dev, i * 2 + b + 1)
                link(nc.vector.reciprocal(rstd[:, b, :], rstd[:, b, :]), s_at)
                for g in range(SUP):
                    last = nc.vector.tensor_scalar(xn[:, b, g, :], xin[:, b, g, :], mv[:, b, g, 0:1],
                                                   rstd[:, b, g:g + 1], ALU.subtract, ALU.mult)
                last.then_inc(s_xn, 1)

            variance(0, 0, True)
            normalize(0, 0)
            before = links[0]

            def body(i, b, rows):
                s = i * 2 + b
                links[0] = before - A0
                dve.wait_ge(s_sq, s + 1)
                link(nc.vector.tensor_scalar(rnorm[:, b, :], sumsq[:, b, :], 1e-12, None, ALU.max), s)
                link(nc.vector.reciprocal(rnorm[:, b, :], rnorm[:, b, :]), s)
                nc.vector.tensor_scalar(rnorm[:, b, :], rnorm[:, b, :], float(D) ** 0.5, None, ALU.mult
                                        ).then_inc(s_rn, 1)
                if rows == P:
                    variance(i + b, 1 - b, not (isinstance(i, int) and b == 1), s)
                    normalize(i + b, 1 - b, s)
            supers(dve, body)

        @block.tensor
        def _(pe):
            pe.wait_ge(s_wready, 1)
            pe.sem_inc(s_xt, 2)

            def body(i, b, rows):
                s = i * 2 + b
                pe.wait_ge(s_xn, s + 1)

                def transposes(g):
                    t = bank[(b + g) % 2]
                    pe.wait_ge(s_xt, s * SUP + (g + 1))
                    for k in range(2):
                        last = nc.tensor.transpose(t[:, k * P:(k + 1) * P], xn[:, b, g, k * P:(k + 1) * P], ident[:])
                    last.then_inc(s_tp, 1)

                transposes(0)
                for g in range(SUP):
                    if g + 1 < SUP:
                        transposes(g + 1)
                    a = (b + g) % 2
                    pe.wait_ge(s_xt, s * SUP + (g + 3))
                    for k in range(2):
                        nc.tensor.matmul(bank[2 + a][:, 0:QKV0], xnT[:, a, k, :], w[:, k, 0:QKV0],
                                         start=(k == 0), stop=(k == 1))
                    for k in range(2):
                        last = nc.tensor.matmul(bank[4 + a][:, 0:3 * MHID], xnT[:, a, k, :], w[:, k, QKV0:],
                                                start=(k == 0), stop=(k == 1))
                    last.then_inc(s_mm, 1)
            supers(pe, body)

        @block.scalar
        def _(act):
            def deviations(i, b):
                act.wait_ge(s_var, i * 2 + b + 1)
                nc.scalar.activation(rstd[:, b, :], rstd[:, b, :], ACT.Sqrt).then_inc(s_dev, 1)

            deviations(0, 0)

            def body(i, b, rows):
                s = i * 2 + b
                act.wait_ge(s_xn, s + 1)
                for g in range(SUP):
                    last = nc.scalar.activation(junk[:, g, :], xn[:, b, g, :], ACT.Square,
                                                accum_out=sumsq[:, b, g:g + 1])
                last.then_inc(s_squared, 1)
                act.wait_ge(s_squared, s + 1)
                nc.scalar.activation(sumsq[:, b, :], sumsq[:, b, :], ACT.Sqrt).then_inc(s_sq, 1)

                def copy_xnT(g):
                    a = (b + g) % 2
                    act.wait_ge(s_tp, s * SUP + (g + 1))
                    nc.scalar.copy(flat(xnT[:, a, :, :]), bank[a][:, 0:2 * P]).then_inc(s_xt, 1)

                copy_xnT(0)
                for g in range(SUP):
                    if g + 1 < SUP:
                        copy_xnT(g + 1)
                    if g == 0:
                        act.wait_ge(s_rn, s + 1)
                    if g == MID and rows == P:
                        deviations(i + b, 1 - b)
                    act.wait_ge(s_mm, s * SUP + (g + 1))
                    a = (b + g) % 2
                    nc.scalar.copy(acc[:, ds(s * SUP + g, 1), :].rearrange("p a d -> p (a d)"),
                                   bank[2 + a][:, 0:ROW])
                    nc.scalar.copy(node_logit[:, ds(s * SUP + g, 1), 0:H].rearrange("p a h -> p (a h)"),
                                   bank[2 + a][:, ROW:ROW + H])
                    nc.scalar.activation(qkv[:, ds(s * SUP + g, 1), 0:3 * MHID].rearrange("p a d -> p (a d)"),
                                         bank[4 + a][:, 0:3 * MHID], ACT.Copy, scale=rnorm[:, b, g:g + 1]
                                         ).then_inc(s_xl, 1)
            supers(act, body)


def contexts(nc, mem_kv, w_out, acc, node_logit, qkv, ident, ones, mix_w, bank):
    with ExitStack() as ctx:
        def sb(name, shape, dt=F32):
            return ctx.enter_context(nc.sbuf_tensor("cx_" + name, shape, dt))

        def sem(name):
            return ctx.enter_context(nc.semaphore(name))

        mem = sb("mem", [P, 2, NMEM])
        memT = sb("memT", [NMEM, 2, P])
        wout = sb("wout", [P, D])
        top_logit = sb("top_logit", [P, H])
        top_key = sb("top_key", [P, MHID])
        top_hcol = sb("top_hcol", [P, 1])
        top_kcol = sb("top_kcol", [P, 1])
        neg_kcol = sb("neg_kcol", [P, 1])
        key_max = sb("key_max", [P, MHID])
        mem_e = sb("mem_e", [P, NMEM])
        z = sb("z", [P, T, H])
        qmax = sb("qmax", [P, NS, SUP, MH])
        qsum = sb("qsum", [P, SUP, MH])
        ctx_n = sb("ctx_n", [P, MHID])
        ctx_b = sb("ctx_b", [P, MHID])
        ctx_t = sb("ctx_t", [P, MHID])
        rden = sb("rden", [P, 1])
        names = ("s_in", "s_max", "s_tp", "s_col", "s_bc", "s_memw", "s_mem", "s_chain", "s_self", "s_w", "s_kd",
                 "s_ke", "s_qd", "s_qe", "s_ctx", "s_ctxn", "s_ctxt", "s_ctxT", "s_mw", "s_neg", "s_mt", "s_mc",
                 "s_wd")
        (s_in, s_max, s_tp, s_col, s_bc, s_memw, s_mem, s_chain, s_self, s_w, s_kd, s_ke, s_qd, s_qe, s_ctx, s_ctxn,
         s_ctxt, s_ctxT, s_mw, s_neg, s_mt, s_mc, s_wd) = (sem("c" + n) for n in names)
        keys = qkv[:, :, MHID:2 * MHID]
        block = ctx.enter_context(nc.Block())

        @block.sync
        def _(sp):
            sp.dma_start(mem[:], mem_kv.rearrange("a h d m -> (h d) a m")).then_inc(s_in, 16)
            sp.dma_start(wout[:], w_out).then_inc(s_in, 16)

        @block.vector
        def _(dve):
            links = [0]

            def link(ins):
                links[0] += 1
                ins.then_inc(s_chain, 1)
                dve.wait_ge(s_chain, links[0])

            nc.vector.tensor_reduce(top_logit[:], acc[:, 0:T - 1, D:ROW].rearrange("p t h -> p h t"), X, ALU.max)
            link(nc.vector.tensor_reduce(top_key[:], keys[:, 0:T - 1, :].rearrange("p t d -> p d t"), X, ALU.max))
            nc.vector.tensor_tensor(top_logit[0:LAST, :], top_logit[0:LAST, :], acc[0:LAST, T - 1, D:ROW], ALU.max)
            nc.vector.tensor_tensor(top_key[0:LAST, :], top_key[0:LAST, :], keys[0:LAST, T - 1, :], ALU.max
                                    ).then_inc(s_max, 1)
            dve.wait_ge(s_tp, 1)
            nc.vector.tensor_reduce(top_hcol[0:H, :], bank[0][0:H, 0:P], X, ALU.max)
            dve.wait_ge(s_in, 32)
            link(nc.vector.tensor_reduce(top_kcol[:], mem[:, 0, :], X, ALU.max))
            link(nc.vector.tensor_reduce(neg_kcol[:], bank[1][:, 0:P], X, ALU.max))
            nc.vector.tensor_tensor(top_kcol[:], top_kcol[:], neg_kcol[:], ALU.max).then_inc(s_col, 1)
            dve.wait_ge(s_col, 1)
            nc.vector.tensor_scalar(neg_kcol[:], top_kcol[:], -1.0, None, ALU.mult).then_inc(s_neg, 1)
            dve.wait_ge(s_bc, 1)
            link(nc.vector.tensor_copy(key_max[:], bank[1][:, 0:P]))
            for c in range(NS):
                k = keys[:, c * SUP:(c + 1) * SUP, :]
                nc.vector.tensor_tensor(k, k, key_max[:].unsqueeze(1).to_broadcast([P, SUP, MHID]), ALU.subtract
                                        ).then_inc(s_kd, 1)
            logit = node_logit[:, :, 0:H]
            bound = node_logit[:, :, H:]
            link(nc.vector.tensor_tensor(z[:], logit, bank[0][:, 0:H].unsqueeze(1).to_broadcast([P, T, H]), ALU.add))
            link(nc.vector.scalar_tensor_tensor(out=bound, in0=z[:], scalar=SLOPE, in1=z[:], op0=ALU.mult,
                                                op1=ALU.max))
            link(nc.vector.tensor_tensor(z[:], acc[:, :, D:ROW], logit, ALU.add))
            link(nc.vector.scalar_tensor_tensor(out=z[:], in0=z[:], scalar=SLOPE, in1=z[:], op0=ALU.mult,
                                                op1=ALU.max))
            link(nc.vector.tensor_tensor(z[:], z[:], bound, ALU.subtract))
            nc.vector.tensor_scalar(z[:], z[:], 0.0, None, ALU.min).then_inc(s_self, 1)
            for c in range(NS):
                q = qkv[:, c * SUP:(c + 1) * SUP, 0:MHID].rearrange("p t (h d) -> p t h d", d=MD)
                wide = [P, SUP, MH, MD]
                link(nc.vector.tensor_reduce(qmax[:, c], q, X, ALU.max))
                nc.vector.tensor_tensor(q, q, qmax[:, c].unsqueeze(3).to_broadcast(wide), ALU.subtract).then_inc(s_qd, 1)
            dve.wait_ge(s_w, 1)
            for h in range(H):
                f = acc[:, :, h * C:(h + 1) * C]
                nc.vector.tensor_tensor(f, f, acc[:, :, D + h:D + h + 1].to_broadcast([P, T, C]), ALU.mult)
            for c in range(NS):
                q = qkv[:, c * SUP:(c + 1) * SUP, 0:MHID].rearrange("p t (h d) -> p t h d", d=MD)
                dve.wait_ge(s_qe, c + 1)
                link(nc.vector.tensor_reduce(qsum[:], q, X, ALU.add))
                link(nc.vector.reciprocal(qsum[:], qsum[:]))
                link(nc.vector.tensor_tensor(q, q, qsum[:].unsqueeze(3).to_broadcast([P, SUP, MH, MD]), ALU.mult))
            dve.wait_ge(s_mt, 1)
            nc.vector.tensor_copy(flat(memT[:]), bank[2][0:NMEM, 0:2 * P]).then_inc(s_mc, 1)
            dve.wait_ge(s_ctx, 1)
            link(nc.vector.reciprocal(rden[:], bank[3][:, MHID:MHID + 1]))
            link(nc.vector.memset(ctx_b[:], 0.0))
            link(nc.vector.tensor_scalar(ctx_n[:], bank[3][:, 0:MHID], rden[:, 0:1], float(MD) ** -0.5, ALU.mult,
                                         ALU.mult))
            for h in range(MH):
                blk = slice(h * MD, (h + 1) * MD)
                last = nc.vector.tensor_copy(ctx_b[blk, blk], ctx_n[blk, blk])
            last.then_inc(s_ctxn, 1)
            dve.wait_ge(s_ctxt, 1)
            nc.vector.tensor_copy(ctx_t[:], bank[4][:, 0:P]).then_inc(s_ctxT, 1)
            dve.wait_ge(s_mw, 1)
            nc.vector.tensor_copy(mix_w[:], bank[5][:, 0:D]).then_inc(s_wd, 1)

        @block.scalar
        def _(act):
            act.wait_ge(s_neg, 1)
            nc.scalar.activation(mem_e[:], mem[:, 0, :], ACT.Exp, bias=neg_kcol[:, 0:1]).then_inc(s_mem, 1)
            for c in range(NS):
                act.wait_ge(s_kd, c + 1)
                k = keys[:, c * SUP:(c + 1) * SUP, :]
                nc.scalar.activation(k, k, ACT.Exp).then_inc(s_ke, 1)
            act.wait_ge(s_self, 1)
            nc.scalar.activation(acc[:, :, D:ROW], z[:], ACT.Exp).then_inc(s_w, 1)
            for c in range(NS):
                act.wait_ge(s_qd, c + 1)
                q = qkv[:, c * SUP:(c + 1) * SUP, 0:MHID]
                nc.scalar.activation(q, q, ACT.Exp).then_inc(s_qe, 1)

        @block.tensor
        def _(pe):
            pe.wait_ge(s_max, 1)
            nc.tensor.transpose(bank[0][0:H, 0:P], top_logit[:], ident[:])
            nc.tensor.transpose(bank[1][:, 0:P], top_key[:], ident[:]).then_inc(s_tp, 1)
            pe.wait_ge(s_col, 1)
            nc.tensor.matmul(bank[0][:, 0:H], top_hcol[0:H, 0:1].to_broadcast([H, P]), ident[0:H, 0:H], start=True,
                             stop=True)
            nc.tensor.matmul(bank[1][:, 0:P], top_kcol[:, 0:1].to_broadcast([P, P]), ident[:], start=True, stop=True
                             ).then_inc(s_bc, 1)
            pe.wait_ge(s_mem, 1)
            nc.tensor.transpose(bank[2][0:NMEM, 0:P], mem_e[:], ident[:])
            nc.tensor.transpose(bank[2][0:NMEM, P:2 * P], mem[:, 1, :], ident[:]).then_inc(s_mt, 1)
            for t in range(T):
                if t % SUP == 0:
                    pe.wait_ge(s_ke, t // SUP + 1)
                r = P if t < T - 1 else LAST
                nc.tensor.matmul(bank[3][:, 0:MHID + 1], qkv[0:r, t, MHID:2 * MHID], qkv[0:r, t, 2 * MHID:],
                                 start=(t == 0), stop=False)
            pe.wait_ge(s_mc, 1)
            nc.tensor.matmul(bank[3][:, 0:MHID], memT[:, 0, :], memT[:, 1, :], start=False, stop=False)
            nc.tensor.matmul(bank[3][:, MHID:MHID + 1], memT[:, 0, :], ones[0:NMEM, 0:1], start=False, stop=True
                             ).then_inc(s_ctx, 1)
            pe.wait_ge(s_ctxn, 1)
            nc.tensor.transpose(bank[4][:, 0:P], ctx_b[:], ident[:]).then_inc(s_ctxt, 1)
            pe.wait_ge(s_ctxT, 1)
            nc.tensor.matmul(bank[5][:, 0:D], ctx_t[:], wout[:], start=True, stop=True).then_inc(s_mw, 1)


def edge_phase(nc, xl_dram, acc, node_logit, src_idx, dst_loc, pair_tile, ident, iota_row, bank):
    with ExitStack() as ctx:
        def sb(name, shape, dt=F32):
            return ctx.enter_context(nc.sbuf_tensor("ed_" + name, shape, dt))

        def sem(name):
            return ctx.enter_context(nc.semaphore(name))

        rows = sb("rows", [P, U * 4, ROW])
        hot = sb("hot", [P, U, 4, P])
        hotT = sb("hotT", [P, U, 4 * P])
        idx = sb("idx", [P, U * 4], I32)
        logit = sb("logit", [P, 2, 4, H])
        s_rows = [sem(f"e_rows{u}") for u in range(U)]
        (s_idx, s_hot, s_tr, s_hotT, s_node, s_logit, s_exp, s_scaled, s_sum, s_added, s_chain, s_fence) = (
            sem("e_" + n) for n in ("idx", "hot", "tr", "hotT", "node", "logit", "exp", "scaled", "sum", "added",
                                    "chain", "fence"))
        TURNS = QUADS // U
        LINKS = 3
        block = ctx.enter_context(nc.Block())

        def tiles_of(eng, which, at):
            _, values = nc.values_load_multi_w_load_instructions(
                pair_tile[0:1, ds(at, 2 * U)], engines=(which,), min_val=0, max_val=T - 1,
                skip_runtime_bounds_check_because="pair_tables clamps the tiles")
            return values

        def steps(q, u, k):
            return (q * 4 + k)

        @block.gpsimd
        def _(pool):
            def gather(u):
                for k in range(4):
                    m = 4 * u + k
                    nc.gpsimd.indirect_dma_start(out=rows[:, m, :], out_offset=None, in_=xl_dram,
                                                 in_offset=bass.IndirectOffsetOnAxis(ap=idx[:, m:m + 1], axis=0)
                                                 ).then_inc(s_rows[u], 16)

            pool.wait_ge(s_idx, U)
            for u in range(U):
                gather(u)
            with pool.Fori(0, TURNS - 1) as i:
                for u in range(U):
                    q = i * U + u
                    pool.wait_ge(s_sum, q * 2 + 2)
                    pool.wait_ge(s_idx, q + (U + 1))
                    pool.sem_inc(s_fence, 1)
                    gather(u)

        @block.scalar
        def _(act):
            def copy_indices(q, u):
                nc.scalar.copy(idx[:, 4 * u:4 * u + 4],
                               src_idx[:, ds(q * 2, 2), :].rearrange("p a b -> p (a b)")).then_inc(s_idx, 1)

            def copy_hotT(q, u):
                act.wait_ge(s_tr, q + 1)
                nc.scalar.copy(hotT[:, u, :], bank[2 + u % 2][:]).then_inc(s_hotT, 1)

            def exps(q, u):
                act.wait_ge(s_logit, q + 1)
                nc.scalar.activation(rows[:, 4 * u:4 * u + 4, D:ROW], logit[:, u % 2, :, :], ACT.Exp
                                     ).then_inc(s_exp, 1)

            for u in range(U):
                copy_indices(u, u)
            for u in range(3):
                copy_hotT(u, u)
            exps(0, 0)

            def turn(i, last=False):
                for u in range(U):
                    q = i * U + u
                    if not last:
                        copy_indices(q + U, u)
                    if not (last and u == U - 1):
                        exps(q + 1, (u + 1) % U)
                    if not (last and u > 0):
                        copy_hotT(q + 3, (u + 3) % U)

            with act.Fori(0, TURNS - 1) as i:
                turn(i)
            turn(TURNS - 1, True)

        @block.vector
        def _(dve):
            links = [0]

            def link(ins, i):
                links[0] += 1
                ins.then_inc(s_chain, 1)
                return i * (LINKS * U) + (LINKS + links[0])

            def one_hots(q, u):
                nc.vector.tensor_tensor(hot[:, u, :, :], iota_row[:].unsqueeze(1).to_broadcast([P, 4, P]),
                                        dst_loc[:, ds(q * 2, 2), :].rearrange("p a b -> p (a b)").unsqueeze(2)
                                        .to_broadcast([P, 4, P]), ALU.is_equal).then_inc(s_hot, 1)

            def edge_logits(i, turn, q, u, between):
                own = bank[4 + u % 2][:, 0:8 * H].rearrange("p (k h) -> p k h", k=4)
                z = logit[:, u % 2, :, :]
                dve.wait_ge(s_rows[u], turn * 64 + 64)
                dve.wait_ge(s_node, q + 1)
                at = link(nc.vector.tensor_tensor(z, rows[:, 4 * u:4 * u + 4, D:ROW], own[:, :, 0:H], ALU.add), i)
                between(0)
                dve.wait_ge(s_chain, at)
                at = link(nc.vector.scalar_tensor_tensor(out=z, in0=z, scalar=SLOPE, in1=z, op0=ALU.mult,
                                                         op1=ALU.max), i)
                between(1)
                dve.wait_ge(s_chain, at)
                at = link(nc.vector.tensor_tensor(z, z, own[:, :, H:], ALU.subtract), i)
                between(2)
                dve.wait_ge(s_chain, at)
                nc.vector.tensor_scalar(z, z, 0.0, None, ALU.min).then_inc(s_logit, 1)

            def scale(q, u, a):
                r = rows[:, 4 * u + 2 * a:4 * u + 2 * a + 2, :]
                f = r[:, :, 0:D].rearrange("p k (h c) -> p k h c", c=C)
                nc.vector.tensor_tensor(f, f, r[:, :, D:ROW].unsqueeze(3).to_broadcast([P, 2, H, C]), ALU.mult
                                        ).then_inc(s_scaled, 1)

            def add(q, a, tile):
                dve.wait_ge(s_sum, q * 2 + (a + 1))
                dve.wait_ge(s_added, q * 2 + (a + 1))
                into = acc[:, ds(tile, 1), :].rearrange("p a d -> p (a d)")
                nc.vector.tensor_tensor(into, into, bank[a][:, 0:ROW], ALU.add).then_inc(s_added, 1)

            dve.sem_inc(s_added, 1)
            for u in range(3):
                one_hots(u, u)
            links[0] = -LINKS
            edge_logits(0, 0, 0, 0, lambda n: None)

            def turn(i, last=False):
                links[0] = 0
                tiles = tiles_of(dve, DVE, i * (2 * U))
                for u in range(U):
                    q = i * U + u
                    end = last and u == U - 1

                    def between(n):
                        if n == 0:
                            dve.wait_ge(s_exp, q + 1)
                        if n < 2:
                            scale(q, u, n)
                        elif not (last and u > 0):
                            one_hots(q + 3, (u + 3) % U)

                    if end:
                        for n in range(3):
                            between(n)
                    else:
                        edge_logits(i, i + (u + 1) // U, q + 1, (u + 1) % U, between)
                    for a in range(2):
                        add(q, a, tiles[2 * u + a])

            with dve.Fori(0, TURNS - 1) as i:
                turn(i)
            turn(TURNS - 1, True)

        @block.tensor
        def _(pe):
            def transposes(q, u):
                pe.wait_ge(s_hot, q + 1)
                for k in range(4):
                    last = nc.tensor.transpose(bank[2 + u % 2][:, k * P:(k + 1) * P], hot[:, u, k, :], ident[:])
                last.then_inc(s_tr, 1)

            def node_rows(q, u, tiles):
                pe.wait_ge(s_hotT, q + 1)
                for k in range(4):
                    last = nc.tensor.matmul(bank[4 + u % 2][:, 2 * H * k:2 * H * (k + 1)],
                                            hotT[:, u, k * P:(k + 1) * P],
                                            node_logit[:, ds(tiles[k // 2], 1), :].rearrange("p a h -> p (a h)"),
                                            start=True, stop=True)
                last.then_inc(s_node, 1)

            def sums(q, u, a):
                pe.wait_ge(s_scaled, q * 2 + (a + 1))
                for k in range(2):
                    m = 2 * a + k
                    last = nc.tensor.matmul(bank[a][:, 0:ROW], hot[:, u, m, :], rows[:, 4 * u + m, :],
                                            start=(k == 0), stop=(k == 1))
                last.then_inc(s_sum, 1)

            first = tiles_of(pe, PE, 0)
            transposes(0, 0)
            transposes(1, 1)
            node_rows(0, 0, first[0:2])
            transposes(2, 2)
            node_rows(1, 1, first[2:4])

            def turn(i, last=False):
                tiles = tiles_of(pe, PE, i * (2 * U) + 4)
                for u in range(U):
                    q = i * U + u
                    for a in range(2):
                        sums(q, u, a)
                    if not (last and u > 1):
                        node_rows(q + 2, (u + 2) % U, tiles[2 * u:2 * u + 2])
                    if not (last and u > 0):
                        transposes(q + 3, (u + 3) % U)

            with pe.Fori(0, TURNS - 1) as i:
                turn(i)
            turn(TURNS - 1, True)


def combine(nc, b_out, g_out, gnn_bias, gnn_gamma, gnn_beta, base_dram, acc, stats, y_sum, qkv, mix_w, ident, ones,
            bank):
    with ExitStack() as ctx:
        def sb(name, shape, dt=F32):
            return ctx.enter_context(nc.sbuf_tensor("cb_" + name, shape, dt))

        def sem(name):
            return ctx.enter_context(nc.semaphore("m_" + name))

        gain = sb("gain", [P, 4, D])
        bout = sb("bout", [1, D])
        zero2 = sb("zero2", [P, 2])
        base = sb("base_rows", [P, 2, SUP, D])
        y = sb("y_rows", [P, SUP, D])
        mixed = sb("mixed", [P, SUP, D])
        q = sb("q", [P, SUP, MHID])
        qT = sb("qT", [P, SUP, P])
        junk = sb("junk", [P, SUP, D])
        rden = sb("rden", [P, SUP, H])
        bn = sb("bn", [P, SUP, 6])
        mv = sb("mv", [P, 2, SUP, 2])
        sumsq = sb("sumsq", [P, SUP])
        rnorm = sb("rnorm", [P, SUP])
        (s_par, s_chain, s_fence, s_tp, s_qT, s_mix, s_sq, s_used, s_biased, s_y, s_ysum, s_zero, s_done, s_q,
         s_squared, s_var, s_dev) = (
            sem(n) for n in ("par", "chain", "fence", "tp", "qT", "mix", "sq", "used", "biased", "y", "ysum", "zero",
                             "done", "q", "squared", "var", "dev"))
        s_base = [sem("base_even"), sem("base_odd")]
        block = ctx.enter_context(nc.Block())
        LINKS = 16
        last = (NS - 1) // 2

        def supers(eng, body):
            with eng.Fori(0, last) as i:
                for b in range(2):
                    body(i, b, P)
            body(last, 0, LAST)

        def tiles(t, s, lo, hi):
            return t[:, ds(s * SUP, SUP), lo:hi]

        def mix_bank(g):
            return bank[4 + g // 2][:, (g % 2) * D:(g % 2 + 1) * D]

        @block.sync
        def _(sp):
            for n, v in enumerate((g_out, gnn_bias, gnn_gamma, gnn_beta)):
                sp.dma_start(gain[:, n, :], v.partition_broadcast(P)).then_inc(s_par, 16)
            sp.dma_start(bout[:], b_out.rearrange("(a d) -> a d", a=1)).then_inc(s_par, 16)
            sp.sem_inc(s_done, 2)

            def load(i, b, rows):
                s = i * 2 + b
                sp.wait_ge(s_done, s + 1)
                if rows == P:
                    sp.dma_start(base[:, b, :, :], base_dram[ds(s * (SUP * P), SUP * P), :].rearrange(
                        "(g p) d -> p g d", p=P)).then_inc(s_base[b], 16)
                else:
                    at = (T - 1) * P
                    sp.dma_start(base[:, b, 0:SUP - 1, :], base_dram[s * SUP * P:at, :].rearrange(
                        "(g p) d -> p g d", p=P)).then_inc(s_base[b], 16)
                    sp.dma_start(base[0:rows, b, SUP - 1, :], base_dram[at:at + rows, :]).then_inc(s_base[b], 16)
            supers(sp, load)

        @block.gpsimd
        def _(pool):
            pool.wait_ge(s_par, 16 * 5)

            def body(i, b, rows):
                pool.wait_ge(s_base[b], i * 16 + (16 if rows == P else 32))
                pool.sem_inc(s_fence, 1)
                nc.gpsimd.tensor_tensor(base[:, b, :, :], base[:, b, :, :],
                                        gain[:, 3:4, :].to_broadcast([P, SUP, D]), ALU.add).then_inc(s_biased, 1)
            supers(pool, body)

        @block.scalar
        def _(act):
            def body(i, b, rows):
                s = i * 2 + b
                nc.scalar.copy(q[:], tiles(qkv, s, 0, MHID)).then_inc(s_q, 1)
                for half, (lo, hi) in enumerate(((0, 4), (4, SUP))):
                    act.wait_ge(s_tp, s * 2 + (half + 1))
                    nc.scalar.copy(flat(qT[:, lo:hi, :]), bank[half][:, 0:(hi - lo) * P]).then_inc(s_qT, 1)
                act.wait_ge(s_mix, s + 1)
                for g in range(SUP):
                    done = nc.scalar.activation(junk[:, g, :], mix_bank(g), ACT.Square, accum_out=sumsq[:, g:g + 1])
                done.then_inc(s_squared, 1)
                act.wait_ge(s_squared, s + 1)
                nc.scalar.activation(sumsq[:], sumsq[:], ACT.Sqrt).then_inc(s_sq, 1)
                for n in range(2):
                    act.wait_ge(s_var, s * 2 + (n + 1))
                    nc.scalar.activation(mv[:, n, :, 1], mv[:, n, :, 1], ACT.Sqrt).then_inc(s_dev, 1)
            supers(act, body)

        @block.tensor
        def _(pe):
            pe.wait_ge(s_par, 16 * 5)
            pe.wait_ge(s_zero, 1)
            nc.tensor.matmul(bank[2][:, 0:2], ident[:], zero2[:], start=True, stop=False)
            pe.sem_inc(s_used, 1)

            def body(i, b, rows):
                s = i * 2 + b
                pe.wait_ge(s_q, s + 1)
                for g in range(SUP):
                    t = nc.tensor.transpose(bank[g // 4][:, (g % 4) * P:(g % 4 + 1) * P], q[:, g, :], ident[:])
                    if g in (3, SUP - 1):
                        t.then_inc(s_tp, 1)
                pe.wait_ge(s_qT, s * 2 + 2)
                pe.wait_ge(s_used, s + 1)
                for g in range(SUP):
                    nc.tensor.matmul(mix_bank(g), qT[:, g, :], mix_w[:], start=True, stop=False)
                    t = nc.tensor.matmul(mix_bank(g), ones[0:1, :], bout[:], start=False, stop=True)
                t.then_inc(s_mix, 1)
                pe.wait_ge(s_y, s + 1)
                for g in range(SUP):
                    r = rows if g == SUP - 1 else P
                    end = rows != P and g == SUP - 1
                    for k in range(2):
                        t = nc.tensor.matmul(bank[2][:, k:k + 1], y[0:r, g, k * P:(k + 1) * P], ones[0:r, 0:1],
                                             start=False, stop=end and k == 1)
                t.then_inc(s_ysum, 1)
            supers(pe, body)

        @block.vector
        def _(dve):
            links = [0]

            def link(ins, s):
                links[0] += 1
                ins.then_inc(s_chain, 1)
                dve.wait_ge(s_chain, s * LINKS + links[0])

            nc.vector.memset(zero2[:], 0.0).then_inc(s_zero, 1)
            dve.wait_ge(s_par, 16 * 5)
            dve.sem_inc(s_ysum, 1)

            def norm_stats(view, s, n):
                dve.sem_inc(s_fence, 1)
                for g in range(SUP):
                    done = nc.vector.bn_stats(bn[:, g, :], view[:, g, :])
                link(done, s)
                dve.sem_inc(s_fence, 1)
                for g in range(SUP):
                    done = nc.vector.bn_aggr(mv[:, n, g, :], bn[:, g, :])
                link(done, s)
                nc.vector.tensor_scalar(mv[:, n, :, 1], mv[:, n, :, 1], LN_EPS, None, ALU.add).then_inc(s_var, 1)
                dve.wait_ge(s_dev, s * 2 + (n + 1))
                link(nc.vector.reciprocal(mv[:, n, :, 1], mv[:, n, :, 1]), s)

            def body(i, b, rows):
                s = i * 2 + b
                links[0] = 0
                z = tiles(acc, s, 0, D)
                wide = [P, SUP, H, C]
                z4 = z.rearrange("p t (h c) -> p t h c", c=C)
                link(nc.vector.reciprocal(rden[:], tiles(acc, s, D, ROW)), s)
                link(nc.vector.tensor_tensor(z4, z4, rden[:].unsqueeze(3).to_broadcast(wide), ALU.mult), s)
                link(nc.vector.tensor_tensor(mixed[:], z, gain[:, 1:2, :].to_broadcast([P, SUP, D]), ALU.add), s)
                norm_stats(mixed, s, 0)
                for g in range(SUP):
                    done = nc.vector.tensor_scalar(mixed[:, g, :], mixed[:, g, :], mv[:, 0, g, 0:1], mv[:, 0, g, 1:2],
                                                   ALU.subtract, ALU.mult)
                link(done, s)
                link(nc.vector.tensor_tensor(mixed[:], mixed[:], gain[:, 2:3, :].to_broadcast([P, SUP, D]), ALU.mult),
                     s)
                dve.wait_ge(s_biased, s + 1)
                link(nc.vector.tensor_tensor(z, mixed[:], base[:, b, :, :], ALU.add), s)
                dve.sem_inc(s_done, 1)
                dve.wait_ge(s_sq, s + 1)
                link(nc.vector.tensor_scalar(rnorm[:], sumsq[:], 1e-12, None, ALU.max), s)
                link(nc.vector.reciprocal(rnorm[:], rnorm[:]), s)
                link(nc.vector.tensor_scalar(rnorm[:], rnorm[:], float(D) ** 0.5, None, ALU.mult), s)
                for g in range(SUP):
                    done = nc.vector.scalar_tensor_tensor(out=mixed[:, g, :], in0=mix_bank(g),
                                                          scalar=rnorm[:, g:g + 1], in1=gain[:, 0, :],
                                                          op0=ALU.mult, op1=ALU.mult)
                done.then_inc(s_used, 1)
                dve.wait_ge(s_used, s + 2)
                link(nc.vector.tensor_tensor(z, z, mixed[:], ALU.add), s)
                norm_stats(z, s, 1)
                nc.vector.tensor_copy(stats[:, ds(s * SUP, SUP), :], mv[:, 1, :, :])
                dve.wait_ge(s_ysum, s + 1)
                for g in range(SUP):
                    done = nc.vector.tensor_scalar(y[:, g, :], z[:, g, :], mv[:, 1, g, 0:1], mv[:, 1, g, 1:2],
                                                   ALU.subtract, ALU.mult)
                done.then_inc(s_y, 1)
                assert links[0] == LINKS, links[0]
            supers(dve, body)
            dve.wait_ge(s_ysum, NS + 1)
            nc.vector.tensor_scalar(y_sum[:, 0:2], bank[2][:, 0:2], 1.0 / N, None, ALU.mult).then_inc(s_zero, 1)


def experts(nc, Wr, br, W1, b1, W2, b2, ffn_gamma, ffn_beta, acc, stats, y_sum, ident, ones, bank, out):
    with ExitStack() as ctx:
        def sb(name, shape, dt=F32):
            return ctx.enter_context(nc.sbuf_tensor("ex_" + name, shape, dt))

        def sem(name):
            return ctx.enter_context(nc.semaphore("f_" + name))

        wr = sb("wr", [P, 2, EX])
        brb = sb("brb", [P, EX])
        off_i = sb("off_i", [P, FC], I32)
        off_f = sb("off_f", [P, FC])
        a = sb("a", [P, 8, EX])
        top8 = sb("top8", [P, 8])
        top8_i = sb("top8_i", [P, 8], U32)
        which = sb("which", [P, 2])
        scaled = sb("scaled", [P, 2, 2])
        idx_f = sb("idx_f", [P, 2, 2 + FC])
        idx_i = sb("idx_i", [P, 2, 2 + FC], I32)
        one_i = sb("one_i", [P, 2], I32)
        w1 = sb("w1", [P, 2, 2, F])
        w2 = sb("w2", [P, 2, FC, D])
        b1c = sb("b1c", [P, 2, FC])
        b2r = sb("b2r", [P, 2, D])
        gain = sb("gain", [P, 2, D])
        y = sb("y", [P, 2, SUP, D])
        yT = sb("yT", [P, 2, 2, SUP * P])
        hT = sb("hT", [P, 2 * FC, SUP * P])
        bn = sb("bn", [P, SUP, 6])
        mv = sb("mv", [P, SUP, 2])
        res = sb("res", [P, 2, SUP, D])
        (s_par, s_chain, s_fence, s_lg, s_e, s_ee, s_idx, s_off, s_gath, s_wgt, s_y, s_tp, s_yT, s_h, s_act, s_o,
         s_read, s_yb, s_xb, s_res, s_var, s_dev) = (
            sem(n) for n in ("par", "chain", "fence", "lg", "e", "ee", "idx", "off", "gath", "wgt", "y", "tp", "yT",
                             "h", "act", "o", "read", "yb", "xb", "res", "var", "dev"))
        s_stored = [sem("stored_even"), sem("stored_odd")]
        block = ctx.enter_context(nc.Block())
        last = (NS - 1) // 2
        GATHERS = 2 * (2 + FC + FC + 1)
        A0 = 25
        LINKS = 5

        def supers(eng, body):
            with eng.Fori(0, last) as i:
                for b in range(2):
                    body(i, b, P)
            body(last, 0, LAST)

        halves = ((0, 4), (4, SUP))

        @block.sync
        def _(sp):
            sp.dma_start(wr[:], Wr.rearrange("(k p) e -> p k e", p=P)).then_inc(s_par, 16)
            sp.dma_start(brb[:], br.partition_broadcast(P)).then_inc(s_par, 16)
            sp.dma_start(gain[:, 0, :], ffn_gamma.partition_broadcast(P)).then_inc(s_par, 16)
            sp.dma_start(gain[:, 1, :], ffn_beta.partition_broadcast(P)).then_inc(s_par, 16)
            for b in range(2):
                sp.sem_inc(s_stored[b], 16)

            def body(i, b, rows):
                s = i * 2 + b
                sp.wait_ge(s_res, s + 1)
                if rows == P:
                    sp.dma_start(out[ds(s * (SUP * P), SUP * P), :].rearrange("(g p) d -> p g d", p=P),
                                 res[:, b, :, :]).then_inc(s_stored[b], 16)
                else:
                    at = (T - 1) * P
                    sp.dma_start(out[s * SUP * P:at, :].rearrange("(g p) d -> p g d", p=P),
                                 res[:, b, 0:SUP - 1, :]).then_inc(s_stored[b], 16)
                    sp.dma_start(out[at:at + rows, :], res[0:rows, b, SUP - 1, :]).then_inc(s_stored[b], 16)
            supers(sp, body)
            sp.wait_ge(s_stored[0], 16 * (last + 3))
            sp.wait_ge(s_stored[1], 16 * (last + 1))

        @block.gpsimd
        def _(pool):
            nc.gpsimd.iota(off_i[:], pattern=[[P, FC]], base=0, channel_multiplier=1).then_inc(s_off, 1)
            pool.wait_ge(s_idx, 1)
            w1_rows = W1.rearrange("e d f -> (e d) f")
            w2_rows = W2.rearrange("e f d -> (e f) d")
            b1_rows = b1.rearrange("e (f a) -> (e f) a", a=1)

            def gather(dest, table, index):
                nc.gpsimd.indirect_dma_start(out=dest, out_offset=None, in_=table,
                                             in_offset=bass.IndirectOffsetOnAxis(ap=index, axis=0)
                                             ).then_inc(s_gath, 16)

            for e in range(2):
                for k in range(2):
                    gather(w1[:, e, k, :], w1_rows, idx_i[:, e, k:k + 1])
                for f in range(FC):
                    gather(b1c[:, e, f:f + 1], b1_rows, idx_i[:, e, 2 + f:3 + f])
                for f in range(FC):
                    gather(w2[:, e, f, :], w2_rows, idx_i[:, e, 2 + f:3 + f])
                gather(b2r[:, e, :], b2, one_i[:, e:e + 1])

            def body(i, b, rows):
                s = i * 2 + b
                x2 = acc[:, ds(s * SUP, SUP), 0:D]
                pool.wait_ge(s_y, s + 1)
                pool.wait_ge(s_wgt, 1)
                pool.sem_inc(s_fence, 1)
                nc.gpsimd.tensor_tensor(x2, x2, gain[:, 1:2, :].to_broadcast([P, SUP, D]), ALU.add).then_inc(s_xb, 1)
                pool.wait_ge(s_tp, s * 4 + 4)
                pool.sem_inc(s_fence, 1)
                nc.gpsimd.tensor_tensor(y[:, b, :, :], y[:, b, :, :], b2r[:, 0:1, :].to_broadcast([P, SUP, D]),
                                        ALU.add).then_inc(s_yb, 1)
            supers(pool, body)

        @block.vector
        def _(dve):
            links = [0]

            def link(ins, s=None):
                links[0] += 1
                ins.then_inc(s_chain, 1)
                dve.wait_ge(s_chain, links[0] if s is None else s * LINKS + (A0 + links[0]))

            V = nc.vector
            dve.wait_ge(s_off, 1)
            link(V.tensor_copy(off_f[:], off_i[:]))
            dve.wait_ge(s_par, 64)
            dve.wait_ge(s_lg, 1)
            link(V.tensor_tensor(a[:, 0, :], bank[0][:, 0:EX], brb[:], ALU.add))

            def softmax(src, dst, n):
                link(V.tensor_reduce(top8[:, 0:1], src, X, ALU.max))
                V.tensor_scalar(dst, src, top8[:, 0:1], None, ALU.subtract).then_inc(s_e, 1)
                dve.wait_ge(s_ee, n)
                link(V.tensor_reduce(top8[:, 0:1], dst, X, ALU.add))
                link(V.reciprocal(top8[:, 0:1], top8[:, 0:1]))
                link(V.tensor_scalar(dst, dst, top8[:, 0:1], None, ALU.mult))

            softmax(a[:, 0, :], a[:, 1, :], 1)
            link(V.tensor_scalar(a[:, 2, :], a[:, 1, :], float(N), None, ALU.mult))
            link(V.tensor_scalar(a[:, 3, :], a[:, 2, :], CAP, None, ALU.max))
            link(V.reciprocal(a[:, 4, :], a[:, 3, :]))
            link(V.tensor_scalar(a[:, 4, :], a[:, 4, :], CAP, None, ALU.mult))
            link(V.tensor_tensor(a[:, 5, :], a[:, 1, :], a[:, 4, :], ALU.mult))
            softmax(a[:, 5, :], a[:, 6, :], 2)
            link(V.max(top8[:], a[:, 6, :]))
            link(V.max_index(top8_i[:], top8[:], a[:, 6, :]))
            V.tensor_tensor(a[:, 7, 0:1], top8[:, 1:2], top8[:, 0:1], ALU.subtract).then_inc(s_e, 1)
            link(V.tensor_copy(which[:], top8_i[:, 0:2]))
            V.tensor_copy(one_i[:], which[:])
            V.tensor_scalar(scaled[:, 0, :], which[:], float(D), None, ALU.mult)
            link(V.tensor_scalar(scaled[:, 1, :], which[:], float(F), None, ALU.mult))
            for e in range(2):
                V.tensor_scalar(idx_f[:, e, 0:2], off_f[:, 0:2], scaled[:, 0, e:e + 1], None, ALU.add)
                done = V.tensor_scalar(idx_f[:, e, 2:], off_f[:], scaled[:, 1, e:e + 1], None, ALU.add)
            link(done)
            V.tensor_copy(idx_i[:], idx_f[:]).then_inc(s_idx, 1)
            dve.wait_ge(s_ee, 3)
            link(V.tensor_scalar(a[:, 7, 1:2], a[:, 7, 0:1], 1.0, None, ALU.add))
            link(V.reciprocal(a[:, 7, 2:3], a[:, 7, 1:2]))
            link(V.tensor_tensor(a[:, 7, 3:4], a[:, 7, 0:1], a[:, 7, 2:3], ALU.mult))
            dve.wait_ge(s_gath, 16 * GATHERS)
            for e in range(2):
                weight = a[:, 7, 2 + e:3 + e]
                V.tensor_scalar(flat(w2[:, e, :, :]), flat(w2[:, e, :, :]), weight, None, ALU.mult)
                done = V.tensor_scalar(b2r[:, e, :], b2r[:, e, :], weight, None, ALU.mult)
            link(done)
            link(V.tensor_tensor(b2r[:, 0, :], b2r[:, 0, :], b2r[:, 1, :], ALU.add))
            dve.sem_inc(s_wgt, 1)
            base_links = links[0]
            assert base_links == A0, base_links

            def norm(i, b):
                s = i * 2 + b
                for g in range(SUP):
                    row = acc[:, ds(s * SUP + g, 1), 0:D].rearrange("p a d -> p (a d)")
                    done = V.tensor_scalar(y[:, b, g, :], row, stats[:, ds(s * SUP + g, 1), 0],
                                           stats[:, ds(s * SUP + g, 1), 1], ALU.subtract, ALU.mult)
                done.then_inc(s_y, 1)

            norm(0, 0)

            def body(i, b, rows):
                s = i * 2 + b
                links[0] = 0
                if rows == P:
                    norm(i + b, 1 - b)
                dve.wait_ge(s_yb, s + 1)
                dve.wait_ge(s_stored[b], i * 16 + 16)
                for g in range(SUP):
                    dve.wait_ge(s_o, s * SUP + (g + 1))
                    V.tensor_tensor(res[:, b, g, :], bank[6 + (b + g) % 2][:, 0:D], y[:, b, g, :], ALU.add
                                    ).then_inc(s_read, 1)
                dve.wait_ge(s_read, s * SUP + (SUP + 2))
                for g in range(SUP):
                    done = V.bn_stats(bn[:, g, :], res[:, b, g, :])
                link(done, s)
                dve.sem_inc(s_fence, 1)
                for g in range(SUP):
                    done = V.bn_aggr(mv[:, g, :], bn[:, g, :])
                link(done, s)
                V.tensor_scalar(mv[:, :, 1], mv[:, :, 1], LN_EPS, None, ALU.add).then_inc(s_var, 1)
                dve.wait_ge(s_dev, s + 1)
                link(V.reciprocal(mv[:, :, 1], mv[:, :, 1]), s)
                for g in range(SUP):
                    done = V.tensor_scalar(res[:, b, g, :], res[:, b, g, :], mv[:, g, 0:1], mv[:, g, 1:2],
                                           ALU.subtract, ALU.mult)
                link(done, s)
                link(V.tensor_tensor(res[:, b, :, :], res[:, b, :, :], gain[:, 0:1, :].to_broadcast([P, SUP, D]),
                                     ALU.mult), s)
                dve.wait_ge(s_xb, s + 1)
                V.tensor_tensor(res[:, b, :, :], res[:, b, :, :], acc[:, ds(s * SUP, SUP), 0:D], ALU.add
                                ).then_inc(s_res, 1)
                assert links[0] == LINKS
            supers(dve, body)

        @block.scalar
        def _(act):
            for n, row in enumerate((1, 6)):
                act.wait_ge(s_e, n + 1)
                nc.scalar.activation(a[:, row, :], a[:, row, :], ACT.Exp).then_inc(s_ee, 1)
            act.wait_ge(s_e, 3)
            nc.scalar.activation(a[:, 7, 0:1], a[:, 7, 0:1], ACT.Exp).then_inc(s_ee, 1)
            act.wait_ge(s_gath, 16 * GATHERS)

            def copy_yT(i, b):
                s = i * 2 + b
                for k in range(2):
                    for half, (lo, hi) in enumerate(halves):
                        act.wait_ge(s_tp, s * 4 + (2 * k + half + 1))
                        nc.scalar.copy(yT[:, b, k, lo * P:hi * P], bank[half][:, 0:(hi - lo) * P]).then_inc(s_yT, 1)

            copy_yT(0, 0)

            def body(i, b, rows):
                s = i * 2 + b
                for ef in range(2 * FC):
                    for half, (lo, hi) in enumerate(halves):
                        n = 2 * ef + half
                        act.wait_ge(s_h, s * 16 + (n + 1))
                        nc.scalar.activation(hT[:, ef, lo * P:hi * P], bank[2 + n % 4][:, 0:(hi - lo) * P], ACT.Gelu,
                                             bias=b1c[:, ef // FC, ef % FC:ef % FC + 1]).then_inc(s_act, 1)
                if rows == P:
                    copy_yT(i + b, 1 - b)
                act.wait_ge(s_var, s + 1)
                nc.scalar.activation(mv[:, :, 1], mv[:, :, 1], ACT.Sqrt).then_inc(s_dev, 1)
            supers(act, body)

        @block.tensor
        def _(pe):
            pe.wait_ge(s_par, 64)
            for k in range(2):
                done = nc.tensor.matmul(bank[0][:, 0:EX], y_sum[:, k:k + 1].to_broadcast([P, P]), wr[:, k, :],
                                        start=(k == 0), stop=(k == 1))
            done.then_inc(s_lg, 1)
            pe.sem_inc(s_act, 4)
            pe.sem_inc(s_read, 2)
            pe.sem_inc(s_yT, 2)
            pe.wait_ge(s_wgt, 1)

            def transposes(i, b):
                s = i * 2 + b
                pe.wait_ge(s_y, s + 1)
                for k in range(2):
                    for half, (lo, hi) in enumerate(halves):
                        pe.wait_ge(s_yT, s * 4 + (2 * k + half + 1))
                        for g in range(lo, hi):
                            done = nc.tensor.transpose(bank[half][:, (g - lo) * P:(g - lo + 1) * P],
                                                       y[:, b, g, k * P:(k + 1) * P], ident[:])
                        done.then_inc(s_tp, 1)

            transposes(0, 0)

            def body(i, b, rows):
                s = i * 2 + b
                pe.wait_ge(s_yT, s * 4 + 6)
                for ef in range(2 * FC):
                    for half, (lo, hi) in enumerate(halves):
                        n = 2 * ef + half
                        pe.wait_ge(s_act, s * 16 + (n + 1))
                        for k in range(2):
                            done = nc.tensor.matmul(bank[2 + n % 4][:, 0:(hi - lo) * P],
                                                    w1[:, ef // FC, k, (ef % FC) * P:(ef % FC + 1) * P],
                                                    yT[:, b, k, lo * P:hi * P], start=(k == 0), stop=(k == 1))
                        done.then_inc(s_h, 1)
                if rows == P:
                    transposes(i + b, 1 - b)
                pe.wait_ge(s_act, s * 16 + 20)
                for g in range(SUP):
                    pe.wait_ge(s_read, s * SUP + (g + 1))
                    for ef in range(2 * FC):
                        done = nc.tensor.matmul(bank[6 + (b + g) % 2][:, 0:D], hT[:, ef, g * P:(g + 1) * P],
                                                w2[:, ef // FC, ef % FC, :], start=(ef == 0), stop=(ef == 2 * FC - 1))
                    done.then_inc(s_o, 1)
            supers(pe, body)


INS = ['x', 'src', 'dst', 'L0_gnn_W', 'L0_gnn_att_src', 'L0_gnn_att_dst', 'L0_gnn_bias', 'L0_gnn_gamma',
       'L0_gnn_beta', 'L0_mix_w_qkv', 'L0_mix_mem_kv', 'L0_mix_w_out', 'L0_mix_b_out', 'L0_mix_g_out',
       'L0_mix_g_pre', 'L0_ffn_Wr', 'L0_ffn_br', 'L0_ffn_W1', 'L0_ffn_b1', 'L0_ffn_W2', 'L0_ffn_b2',
       'L0_ffn_gamma', 'L0_ffn_beta']


def kernel(**inputs):
    import numpy as np
    import concourse.bacc as bacc
    from concourse.bass_utils import run_bass_kernel_spmd

    nc = bacc.Bacc("TRN2", target_bir_lowering=False, num_devices=1)
    arrays, args = {}, []
    for name in INS:
        a = np.ascontiguousarray(inputs[name])
        arrays["in_" + name] = a
        args.append(nc.dram_tensor("in_" + name, a.shape, mybir.dt.from_np(a.dtype), kind="ExternalInput").ap())
    xl_dram = nc.dram_tensor("xl_dram", (N, ROW), F32, kind="Internal").ap()
    base_dram = nc.dram_tensor("base_dram", (N, D), F32, kind="Internal").ap()
    edges_dram = nc.dram_tensor("edges_dram", (GR + 1, 2 * GE), I32, kind="Internal").ap()
    pair_dram = nc.dram_tensor("pair_dram", (PC * P,), I32, kind="Internal").ap()
    out = nc.dram_tensor("out_0", (N, D), F32, kind="ExternalOutput").ap()
    gps_layer(nc, *args, xl_dram, base_dram, edges_dram, pair_dram, out)
    r = run_bass_kernel_spmd(nc, [arrays], core_ids=[0])
    return r.results[0]["out_0"]
```

```python
from contextlib import ExitStack

import concourse.bass as bass
from concourse import mybir

ALU = mybir.AluOpType
ACT = mybir.ActivationFunctionType
F32 = mybir.dt.float32
BF16 = mybir.dt.bfloat16
F32R = mybir.dt.float32r
I32 = mybir.dt.int32
U32 = mybir.dt.uint32
X = mybir.AxisListType.X
DVE = mybir.EngineType.DVE
PE = mybir.EngineType.PE
ds = bass.ds

P = 128
N, D, E = 6250, 256, 200000
H, C = 8, 32
T = -(-N // P)
LAST = N - (T - 1) * P
SUP = 7
NS = T // SUP
ROW = H * C + H
GE = 256
GR = -(-E // GE)
PAIRS = GR + T - 1
NOWHERE = T * P
QUADS = -(-PAIRS // 8) * 4
U = 4
PC = -(-(QUADS * 2 + 16) // P)
MH, MD = 4, 32
MHID = MH * MD
NMEM = 4
EX, F = 8, 512
FC = F // P
LN_EPS = 1e-5
SLOPE = 0.2
CAP = float(-(-N * 5 // (4 * EX)))
QKV0 = ROW + H


def flat(ap):
    return ap.rearrange("p a b -> p (a b)")


def gps_layer(nc, x, src, dst, W, att_src, att_dst, gnn_bias, gnn_gamma, gnn_beta, w_qkv, mem_kv, w_out, b_out,
              g_out, g_pre, Wr, br, W1, b1, W2, b2, ffn_gamma, ffn_beta, xl_dram, base_dram, edges_dram,
              pair_dram, out):
    top = ExitStack()

    def alloc(stack):
        return (lambda name, shape, dt=F32: stack.enter_context(nc.sbuf_tensor(name, shape, dt)),
                lambda name: stack.enter_context(nc.semaphore(name)))

    with top:
        top.enter_context(nc.allow_non_contiguous_dma(reason="a few hundred single words, once"))
        sb, _ = alloc(top)
        bank = [top.enter_context(nc.psum_tensor(f"bank{i}", [P, 512], F32)) for i in range(8)]
        acc = sb("acc", [P, T, ROW])
        ident = sb("ident", [P, P])
        stats = sb("stats", [P, T, 2])
        y_sum = sb("y_sum", [P, 2])
        router = sb("router", [P, 3, EX])
        with ExitStack() as attention:
            sa, _ = alloc(attention)
            src_idx = sa("src_idx", [P, PC * P, 2], I32)
            dst_loc = sa("dst_loc", [P, PC * P, 2])
            iota_row = sa("iota_row", [P, P])
            ones = sa("ones", [P, P])
            ones_bf = sa("ones_bf", [P, P], BF16)
            node_logit = sa("node_logit", [P, T, 2 * H])
            pair_tile = sa("pair_tile", [1, PC * P], I32)
            qkv = sa("qkv", [P, T, 3 * MHID + 1])
            with ExitStack() as projection:
                sp, _ = alloc(projection)
                w_part = sp("w_part", [P, 2, 2, QKV0 + 3 * MHID], F32R)
                beta = sp("beta", [P, 1, D])
                xin = sp("xin", [P, 2, SUP, D])
                mv = sp("mv", [P, 2, SUP, 2])
                pair_tables(nc, dst, src, edges_dram, pair_dram, ident, iota_row, ones, ones_bf, src_idx, dst_loc,
                            pair_tile, x, W, att_src, att_dst, w_qkv, g_pre, gnn_beta, w_part, beta, xin, mv, acc,
                            bank)
                project(nc, x, w_part, beta, xin, mv, xl_dram, base_dram, acc, node_logit, qkv, ident, bank)
            edge_phase(nc, mem_kv, w_out, b_out, g_out, xl_dram, base_dram, acc, node_logit, qkv, src_idx, dst_loc,
                       pair_tile, ident, iota_row, ones, bank)
            combine(nc, Wr, br, gnn_bias, gnn_gamma, acc, stats, y_sum, router, qkv, ident, ones, bank)
        experts(nc, W1, b1, W2, b2, ffn_gamma, ffn_beta, acc, stats, y_sum, router, ident, bank, out)


def pair_tables(nc, dst, src, edges_dram, pair_dram, ident, iota_row, ones, ones_bf, src_idx, dst_loc, pair_tile,
                x, W, att_src, att_dst, w_qkv, g_pre, gnn_beta, w_part, beta, xin, mv, acc, bank):
    full = E // GE
    rest = E - full * GE
    with ExitStack() as ctx:
        def sb(name, shape, dt=F32):
            return ctx.enter_context(nc.sbuf_tensor("pt_" + name, shape, dt))

        def sem(name):
            return ctx.enter_context(nc.semaphore(name))

        pad = sb("pad", [1, 4 * GE], I32)
        iota_i = sb("iota_i", [P, P], I32)
        part_i = sb("part_i", [P, 1], I32)
        part_f = sb("part_f", [P, 1])
        first_i = sb("first_i", [P, 2 * PC], I32)
        first_f = sb("first_f", [P, 2 * PC])
        start_i = sb("start_i", [P, T + 1], I32)
        start_f = sb("start_f", [P, T + 1])
        below = sb("below", [P, 2 * PC, T + 1], BF16)
        group_count = sb("group_count", [P, 2, T + 1])
        count = sb("count", [P, T])
        one_t = sb("one_t", [P, T])
        base = sb("base", [P, T + 1])
        shift = sb("shift", [P, T])
        step = sb("step", [P, T])
        pair_i = sb("pair_i", [P, PC], I32)
        pair_f = sb("pair_f", [P, PC])
        reached = sb("reached", [P, PC, T])
        product = sb("product", [P, PC, T])
        tile_f = sb("tile_f", [P, PC])
        tile_i = sb("tile_i", [P, PC], I32)
        tile_node = sb("tile_node", [P, PC])
        row_f = sb("row_f", [P, PC])
        row_i = sb("row_i", [P, PC], I32)
        group = sb("group", [P, PC, 2 * GE], I32)
        whole, taken, buffers = flat(acc[:]), 0, []
        for n, width in ((PC, 2 * GE), (2, QKV0 + 3 * MHID), (2, D), (4, D)):
            buffers.append(whole[:, taken:taken + n * width].rearrange("p (n w) -> p n w", n=n))
            taken += n * width
        group_f, w, att, att_w = buffers
        gp = sb("gp", [P, 2])
        bn = sb("bn", [P, SUP, 6])
        s_w, s_x = sem("s_w"), sem("s_x")
        s_iota, s_pad, s_edges, s_first = sem("s_iota"), sem("s_pad"), sem("s_edges"), sem("s_first")
        s_below, s_counts, s_row, s_group, s_table = (sem("s_below"), sem("s_counts"), sem("s_row"), sem("s_group"),
                                                      sem("s_table"))
        s_pt, s_gf, s_tr, s_idx, s_chain = sem("s_pt"), sem("s_gf"), sem("s_tr"), sem("s_idx"), sem("s_chain")
        block = ctx.enter_context(nc.Block())
        COPIES = 8

        @block.sync
        def _(sp):
            sp.dma_start(edges_dram[0:full, 0:GE], src[0:full * GE].rearrange("(r w) -> r w", w=GE)).then_inc(s_edges, 16)
            sp.dma_start(edges_dram[0:full, GE:2 * GE], dst[0:full * GE].rearrange("(r w) -> r w", w=GE)).then_inc(s_edges, 16)
            sp.dma_start(edges_dram[full:full + 1, 0:rest], src[full * GE:E].rearrange("(r w) -> r w", r=1)).then_inc(s_edges, 16)
            sp.dma_start(edges_dram[full:full + 1, GE:GE + rest], dst[full * GE:E].rearrange("(r w) -> r w", r=1)).then_inc(s_edges, 16)
            sp.wait_ge(s_pad, 2)
            sp.dma_start(edges_dram[full:full + 1, rest:GE], pad[0:1, 0:GE - rest]).then_inc(s_edges, 16)
            sp.dma_start(edges_dram[full:full + 1, GE + rest:2 * GE], pad[0:1, GE:2 * GE - rest]).then_inc(s_edges, 16)
            sp.dma_start(edges_dram[full + 1:full + 2, 0:GE], pad[0:1, 0:GE]).then_inc(s_edges, 16)
            sp.dma_start(edges_dram[full + 1:full + 2, GE:2 * GE], pad[0:1, GE:2 * GE]).then_inc(s_edges, 16)
            sp.wait_ge(s_table, 1)
            sp.dma_start(pair_dram.rearrange("(c p) -> p c", p=P), tile_i[:]).then_inc(s_pt, 16)
            sp.wait_ge(s_pt, 16)
            sp.dma_start(pair_tile[:], pair_dram.rearrange("(a j) -> a j", a=1)).then_inc(s_pt, 16)
            sp.wait_ge(s_pt, 32)
            sp.wait_ge(s_edges, 16 * COPIES)

        @block.scalar
        def _(act):
            act.wait_ge(s_pad, 3)
            for half, (offset, groups) in enumerate(((0, GR), (GE - 1, full))):
                whole = groups // P
                tail = groups - whole * P
                act.dma_start(first_i[:, half * PC:half * PC + whole],
                              dst[0:whole * P * GE].rearrange("(c p w) -> p c w", p=P, w=GE)[:, :, offset]
                              ).then_inc(s_first, 16)
                if offset:
                    tail_ap = dst[whole * P * GE:(whole * P + tail) * GE].rearrange("(p w) -> p w", w=GE)[:, offset:offset + 1]
                    act.dma_start(first_i[0:tail, half * PC + whole:half * PC + whole + 1], tail_ap).then_inc(s_first, 16)
                else:
                    tail_ap = dst[whole * P * GE:(whole * P + tail - 1) * GE].rearrange("(p w) -> p w", w=GE)[:, 0:1]
                    act.dma_start(first_i[0:tail - 1, whole:whole + 1], tail_ap).then_inc(s_first, 16)
                    act.dma_start(first_i[tail - 1:tail, whole:whole + 1],
                                  dst[full * GE:full * GE + 1].rearrange("(p w) -> p w", w=1)).then_inc(s_first, 16)
            act.dma_start(w[:, :, 0:D], W.rearrange("(k p) n -> p k n", p=P)).then_inc(s_w, 16)
            act.dma_start(w[:, :, QKV0:], w_qkv.rearrange("(k p) n -> p k n", p=P)).then_inc(s_w, 16)
            act.dma_start(gp[:], g_pre.rearrange("(k p) -> p k", p=P)).then_inc(s_w, 16)
            for a, v in enumerate((att_src, att_dst)):
                act.dma_start(att[:, a, :], v.rearrange("h c -> (h c)").partition_broadcast(P)).then_inc(s_w, 16)
            for b in range(2):
                act.dma_start(xin[:, b, :, :], x[b * SUP * P:(b + 1) * SUP * P, :].rearrange("(g p) d -> p g d", p=P)
                              ).then_inc(s_x, 16)
            act.dma_start(beta[:, 0, :], gnn_beta.partition_broadcast(P)).then_inc(s_x, 16)
            for c in range(PC):
                for half in range(2):
                    n = 2 * c + half
                    act.wait_ge(s_tr, n + 1)
                    t = bank[n % 4]
                    nc.scalar.copy(src_idx[:, c * P:(c + 1) * P, half], t[:, 0:P])
                    nc.scalar.copy(dst_loc[:, c * P:(c + 1) * P, half], t[:, P:2 * P]).then_inc(s_idx, 1)

        @block.gpsimd
        def _(pool):
            nc.gpsimd.iota(iota_i[:], pattern=[[1, P]], base=0, channel_multiplier=0)
            nc.gpsimd.iota(part_i[:], pattern=[[0, 1]], base=0, channel_multiplier=1)
            nc.gpsimd.iota(start_i[:], pattern=[[P, T + 1]], base=0, channel_multiplier=0)
            nc.gpsimd.iota(pair_i[:], pattern=[[P, PC]], base=0, channel_multiplier=1).then_inc(s_iota, 1)
            pool.wait_ge(s_row, 1)
            pool.wait_ge(s_edges, 16 * COPIES)
            for c in range(PC):
                nc.gpsimd.indirect_dma_start(out=group[:, c, :], out_offset=None, in_=edges_dram,
                                             in_offset=bass.IndirectOffsetOnAxis(ap=row_i[:, c:c + 1], axis=0)
                                             ).then_inc(s_group, 16)
            pool.wait_ge(s_group, 16 * PC)

        @block.vector
        def _(dve):
            links = [0]

            def link(ins):
                links[0] += 1
                ins.then_inc(s_chain, 1)
                dve.wait_ge(s_chain, links[0])

            nc.vector.memset(pad[:, 0:GE], 0).then_inc(s_pad, 1)
            nc.vector.memset(pad[:, GE:], NOWHERE).then_inc(s_pad, 1)
            nc.vector.memset(first_i[:], NOWHERE).then_inc(s_pad, 1)
            nc.vector.memset(ones[:], 1.0)
            nc.vector.memset(ones_bf[:], 1.0)
            nc.vector.memset(one_t[:], 1.0)
            nc.vector.memset(base[:, 0:1], 0.0)
            dve.wait_ge(s_iota, 1)
            nc.vector.tensor_copy(iota_row[:], iota_i[:])
            nc.vector.tensor_copy(pair_f[:], pair_i[:])
            nc.vector.tensor_copy(start_f[:], start_i[:])
            link(nc.vector.tensor_copy(part_f[:], part_i[:]))
            nc.vector.tensor_scalar(ident[:], iota_row[:], part_f[:, 0:1], None, ALU.is_equal)
            dve.wait_ge(s_first, 16 * 5)
            link(nc.vector.tensor_copy(first_f[:], first_i[:]))
            nc.vector.tensor_tensor(below[:], first_f[:].unsqueeze(2).to_broadcast([P, 2 * PC, T + 1]),
                                    start_f[:].unsqueeze(1).to_broadcast([P, 2 * PC, T + 1]), ALU.is_lt
                                    ).then_inc(s_below, 1)
            dve.wait_ge(s_counts, 1)
            link(nc.vector.tensor_copy(flat(group_count[:]), bank[0][:, 0:2 * (T + 1)]))
            begun, ended = group_count[:, 0, :], group_count[:, 1, :]
            link(nc.vector.tensor_tensor(count[:], begun[:, 1:T + 1], ended[:, 0:T], ALU.subtract))
            link(nc.vector.tensor_tensor_scan(base[:, 1:T + 1], one_t[:], count[:], 0.0, ALU.mult, ALU.add))
            link(nc.vector.tensor_tensor(shift[:], ended[:, 0:T], base[:, 0:T], ALU.subtract))
            link(nc.vector.tensor_copy(step[:, 0:1], shift[:, 0:1]))
            link(nc.vector.tensor_tensor(step[:, 1:T], shift[:, 1:T], shift[:, 0:T - 1], ALU.subtract))
            pairs = pair_f[:].unsqueeze(2).to_broadcast([P, PC, T])
            link(nc.vector.tensor_tensor(reached[:], base[:, 1:T + 1].unsqueeze(1).to_broadcast([P, PC, T]), pairs,
                                         ALU.is_le))
            link(nc.vector.tensor_reduce(tile_f[:], reached[:], X, ALU.add))
            link(nc.vector.tensor_scalar(tile_f[:], tile_f[:], float(T - 1), None, ALU.min))
            nc.vector.tensor_copy(tile_i[:], tile_f[:]).then_inc(s_table, 1)
            nc.vector.tensor_scalar(tile_node[:], tile_f[:], float(P), None, ALU.mult)
            link(nc.vector.tensor_tensor(reached[:], base[:, 0:T].unsqueeze(1).to_broadcast([P, PC, T]), pairs,
                                         ALU.is_le))
            link(nc.vector.tensor_tensor(product[:], reached[:], step[:].unsqueeze(1).to_broadcast([P, PC, T]),
                                         ALU.mult))
            link(nc.vector.tensor_reduce(row_f[:], product[:], X, ALU.add))
            link(nc.vector.tensor_tensor(row_f[:], row_f[:], pair_f[:], ALU.add))
            link(nc.vector.tensor_scalar(row_f[:], row_f[:], float(full + 1), 0.0, ALU.min, ALU.max))
            nc.vector.tensor_copy(row_i[:], row_f[:]).then_inc(s_row, 1)

            dve.wait_ge(s_w, 16 * 5)
            for k in range(2):
                for a in range(2):
                    done = nc.vector.tensor_tensor(att_w[:, 2 * k + a, :], w[:, k, 0:D], att[:, a, :], ALU.mult)
            link(done)
            for k in range(2):
                for a in range(2):
                    nc.vector.tensor_reduce(w[:, k, D + a * H:D + (a + 1) * H],
                                            att_w[:, 2 * k + a, :].rearrange("p (h c) -> p h c", c=C), X, ALU.add)
            for k in range(2):
                done = nc.vector.tensor_scalar(w[:, k, QKV0:], w[:, k, QKV0:], gp[:, k:k + 1], None, ALU.mult)
            link(done)
            link(nc.vector.tensor_copy(w_part[:, 0, :, :], w[:]))
            nc.vector.tensor_tensor(w_part[:, 1, :, :], w[:], w_part[:, 0, :, :].bitcast(F32), ALU.subtract)
            dve.wait_ge(s_x, 16 * 3)
            for g in range(SUP):
                done = nc.vector.bn_stats(bn[:, g, :], xin[:, 0, g, :])
            link(done)
            for g in range(SUP):
                done = nc.vector.bn_aggr(mv[:, 0, g, :], bn[:, g, :])
            dve.wait_ge(s_group, 16 * PC)
            for c in range(PC):
                nc.vector.tensor_copy(group_f[:, c, 0:GE], group[:, c, 0:GE])
                nc.vector.tensor_scalar(group_f[:, c, GE:], group[:, c, GE:], tile_node[:, c:c + 1], None,
                                        ALU.subtract).then_inc(s_gf, 1)

        @block.tensor
        def _(pe):
            pe.wait_ge(s_below, 1)
            for half in range(2):
                for c in range(PC):
                    last = nc.tensor.matmul(bank[0][:, half * (T + 1):(half + 1) * (T + 1)], ones_bf[:],
                                            below[:, half * PC + c, :], start=(c == 0), stop=(c == PC - 1))
            last.then_inc(s_counts, 1)
            for c in range(PC):
                pe.wait_ge(s_gf, c + 1)
                for half in range(2):
                    n = 2 * c + half
                    if n >= 4:
                        pe.wait_ge(s_idx, n - 3)
                    for kind in range(2):
                        last = nc.tensor.transpose(bank[n % 4][:, kind * P:(kind + 1) * P],
                                                   group_f[:, c, kind * GE + half * P:kind * GE + (half + 1) * P],
                                                   ident[:])
                    last.then_inc(s_tr, 1)


def project(nc, x, w_part, beta, xin, mv, xl_dram, base_dram, acc, node_logit, qkv, ident, bank):
    with ExitStack() as ctx:
        def sb(name, shape, dt=F32):
            return ctx.enter_context(nc.sbuf_tensor("pj_" + name, shape, dt))

        def sem(name):
            return ctx.enter_context(nc.semaphore(name))

        xn = sb("xn", [P, 2, SUP, D])
        xnT = sb("xnT", [P, SUP, 2, 2, P], F32R)
        bn = sb("bn", [P, 2, SUP, 6])
        rstd = sb("rstd", [P, 2, SUP])
        sumsq = sb("sumsq", [P, 2, SUP])
        rnorm = sb("rnorm", [P, 2, SUP])
        s_var, s_dev, s_squared, s_sum = (sem("pj_" + n) for n in ("var", "dev", "squared", "sum"))
        s_low, s_chain, s_xn, s_sq, s_rn, s_tp, s_xt, s_mm, s_xl, s_base, s_xls, s_fence = (
            sem(n) for n in ("s_low", "s_chain", "s_xn", "s_sq", "s_rn", "s_tp", "s_xt", "s_mm", "s_xl",
                             "s_base", "s_xls", "s_fence"))
        s_x = [sem("s_x_even"), sem("s_x_odd")]
        s_stored = [sem("s_stored_even"), sem("s_stored_odd")]
        block = ctx.enter_context(nc.Block())
        HIGH, LOW = 0, 1
        PARTS = ((LOW, HIGH), (HIGH, LOW), (HIGH, HIGH))
        A0 = 4
        LINKS = 6

        AHEAD = 2

        def ahead(i, b, g, rows):
            if g + AHEAD < SUP:
                return [(i, b, g + AHEAD)]
            return [(i + b, 1 - b, g + AHEAD - SUP)] if rows == P else []

        def supers(eng, body):
            last = (NS - 1) // 2
            with eng.Fori(0, last - 1) as i:
                for b in range(2):
                    body(i, b, P)
            for b in range(2):
                body(last - 1, b, P)
            body(last, 0, LAST)

        def node_rows(dram, s, rows):
            if rows == P:
                return [(dram[ds(s * (SUP * P), SUP * P), :].rearrange("(g p) d -> p g d", p=P), slice(0, SUP), P)]
            whole = s * SUP * P + (SUP - 1) * P
            return [(dram[s * SUP * P:whole, :].rearrange("(g p) d -> p g d", p=P), slice(0, SUP - 1), P),
                    (dram[whole:whole + rows, :].unsqueeze(1), slice(SUP - 1, SUP), rows)]

        @block.sync
        def _(sp):
            for b in range(2):
                sp.sem_inc(s_stored[b], 16)
                sp.sem_inc(s_x[b], 16)

            def load(i, b, rows):
                sp.wait_ge(s_stored[b], i * 16 + 16)
                for dram, g, r in node_rows(x, i * 2 + b, rows):
                    sp.dma_start(xin[0:r, b, g, :], dram).then_inc(s_x[b], 16)

            def store_base(i, b, rows):
                s = i * 2 + b
                sp.wait_ge(s_base, s + 1)
                for dram, g, r in node_rows(base_dram, s, rows):
                    sp.dma_start(dram, xin[0:r, b, g, :]).then_inc(s_stored[b], 16)

            def store_xl(i, b, rows):
                s = i * 2 + b
                sp.wait_ge(s_xl, s * SUP + (SUP + 2))
                for dram, g, r in node_rows(xl_dram, s, rows):
                    sp.dma_start(dram, acc[0:r, ds(s * SUP + g.start, g.stop - g.start), :]).then_inc(s_xls, 16)

            last = (NS - 1) // 2
            with sp.Fori(0, last - 1) as i:
                for b in range(2):
                    store_base(i, b, P)
                    load(i + 1, b, P)
                    store_xl(i, b, P)
            store_base(last - 1, 0, P)
            load(last, 0, LAST)
            store_xl(last - 1, 0, P)
            store_base(last - 1, 1, P)
            store_xl(last - 1, 1, P)
            store_base(last, 0, LAST)
            store_xl(last, 0, LAST)
            sp.wait_ge(s_stored[0], 16 + 16 * (last + 2))
            sp.wait_ge(s_stored[1], 16 + 16 * last)
            sp.wait_ge(s_xls, 16 * (NS + 1))

        @block.gpsimd
        def _(pool):
            def body(i, b, rows):
                s = i * 2 + b
                pool.wait_ge(s_xn, s + 1)
                pool.sem_inc(s_fence, 1)
                nc.gpsimd.tensor_tensor(flat(xin[:, b, :, :]), flat(xin[:, b, :, :]), flat(xn[:, b, :, :]),
                                        ALU.add).then_inc(s_sum, 1)
                pool.wait_ge(s_sum, s + 1)
                pool.sem_inc(s_fence, 1)
                nc.gpsimd.tensor_tensor(xin[:, b, :, :], xin[:, b, :, :], beta[:].to_broadcast([P, SUP, D]), ALU.add
                                        ).then_inc(s_base, 1)
            supers(pool, body)

        @block.vector
        def _(dve):
            links = [0]

            def link(ins, s=None):
                links[0] += 1
                ins.then_inc(s_chain, 1)
                dve.wait_ge(s_chain, links[0] if s is None else s * LINKS + (A0 + links[0]))

            nc.vector.memset(qkv[:, :, 3 * MHID:], 1.0)

            def variance_of(i, b, full, tiles):
                if tiles.start == 0:
                    dve.wait_ge(s_x[b], i * 16 + (16 if full else 32))
                for g in range(tiles.start, tiles.stop):
                    last = nc.vector.bn_stats(bn[:, b, g, :], xin[:, b, g, :])
                return last

            def variance(i, b, s_at):
                if s_at is not None:
                    dve.sem_inc(s_fence, 1)
                    for g in range(SUP):
                        last = nc.vector.bn_aggr(mv[:, b, g, :], bn[:, b, g, :])
                    link(last, s_at)
                nc.vector.tensor_scalar(rstd[:, b, :], mv[:, b, :, 1], LN_EPS, None, ALU.add).then_inc(s_var, 1)

            def scales(i, b, s_at=None):
                dve.wait_ge(s_dev, i * 2 + b + 1)
                link(nc.vector.reciprocal(rstd[:, b, :], rstd[:, b, :]), s_at)
                link(nc.vector.scalar_tensor_tensor(out=sumsq[:, b, :], in0=mv[:, b, :, 1], scalar=float(D),
                                                    in1=rstd[:, b, :], op0=ALU.mult, op1=ALU.mult), s_at)
                nc.vector.tensor_tensor(sumsq[:, b, :], sumsq[:, b, :], rstd[:, b, :], ALU.mult).then_inc(s_squared, 1)

            def norms(i, b, s_at=None):
                dve.wait_ge(s_sq, i * 2 + b + 1)
                link(nc.vector.tensor_scalar(rnorm[:, b, :], sumsq[:, b, :], 1e-12, None, ALU.max), s_at)
                link(nc.vector.reciprocal(rnorm[:, b, :], rnorm[:, b, :]), s_at)
                nc.vector.tensor_scalar(rnorm[:, b, :], rnorm[:, b, :], float(D) ** 0.5, None, ALU.mult
                                        ).then_inc(s_rn, 1)

            def normalize(b, tiles):
                for g in range(tiles.start, tiles.stop):
                    last = nc.vector.tensor_scalar(xn[:, b, g, :], xin[:, b, g, :], mv[:, b, g, 0:1],
                                                   rstd[:, b, g:g + 1], ALU.subtract, ALU.mult)
                return last

            first, rest = slice(0, 4), slice(4, SUP)
            variance(0, 0, None)
            scales(0, 0)
            normalize(0, slice(0, SUP)).then_inc(s_xn, 1)
            norms(0, 0)
            assert links[0] == A0

            def body(i, b, rows):
                s = i * 2 + b
                links[0] = 0
                n = (i + b, 1 - b)
                for g in range(SUP):
                    a = (b + g) % 2
                    dve.wait_ge(s_xt, s * SUP + (g + 1))
                    nc.vector.tensor_tensor(flat(xnT[:, g, LOW, :, :]), bank[a][:, 0:2 * P],
                                            flat(xnT[:, g, HIGH, :, :]).bitcast(F32), ALU.subtract).then_inc(s_low, 1)
                    if rows != P:
                        continue
                    if g == 0:
                        variance_of(*n, not (isinstance(i, int) and b == 1), first)
                    if g == 1:
                        link(variance_of(*n, True, rest), s)
                    if g == 2:
                        variance(*n, s)
                    if g == 3:
                        scales(*n, s)
                        normalize(n[1], first)
                    if g == 4:
                        normalize(n[1], rest).then_inc(s_xn, 1)
                    if g == 5:
                        norms(*n, s)
            supers(dve, body)

        @block.tensor
        def _(pe):
            pe.sem_inc(s_low, 2)
            pe.sem_inc(s_xl, 2)

            def transposes(i, b, g):
                s = i * 2 + b
                t = bank[(b + g) % 2]
                pe.wait_ge(s_xn, s + 1)
                pe.wait_ge(s_low, s * SUP + (g + 1))
                for k in range(2):
                    last = nc.tensor.transpose(t[:, k * P:(k + 1) * P], xn[:, b, g, k * P:(k + 1) * P], ident[:])
                last.then_inc(s_tp, 1)

            for g in range(AHEAD):
                transposes(0, 0, g)

            def body(i, b, rows):
                s = i * 2 + b
                for g in range(SUP):
                    a = (b + g) % 2
                    for tile in ahead(i, b, g, rows):
                        transposes(*tile)
                    pe.wait_ge(s_low, s * SUP + (g + 3))
                    pe.wait_ge(s_xl, s * SUP + (g + 1))
                    for out, columns in ((bank[2 + a], slice(0, QKV0)), (bank[4 + a], slice(QKV0, QKV0 + 3 * MHID))):
                        for k in range(2):
                            for m, (xp, wp) in enumerate(PARTS):
                                last = nc.tensor.matmul(out[:, 0:columns.stop - columns.start], xnT[:, g, xp, k, :],
                                                        w_part[:, wp, k, columns], start=(k == 0 and m == 0),
                                                        stop=(k == 1 and m == 2))
                    last.then_inc(s_mm, 1)
            supers(pe, body)

        @block.scalar
        def _(act):
            def deviations(i, b):
                act.wait_ge(s_var, i * 2 + b + 1)
                nc.scalar.activation(rstd[:, b, :], rstd[:, b, :], ACT.Sqrt).then_inc(s_dev, 1)

            def norms(i, b):
                act.wait_ge(s_squared, i * 2 + b + 1)
                nc.scalar.activation(sumsq[:, b, :], sumsq[:, b, :], ACT.Sqrt).then_inc(s_sq, 1)

            def copy_xnT(i, b, g):
                act.wait_ge(s_tp, (i * 2 + b) * SUP + (g + 1))
                nc.scalar.copy(flat(xnT[:, g, HIGH, :, :]), bank[(b + g) % 2][:, 0:2 * P]).then_inc(s_xt, 1)

            deviations(0, 0)
            norms(0, 0)
            for g in range(AHEAD):
                copy_xnT(0, 0, g)

            def body(i, b, rows):
                s = i * 2 + b
                for g in range(SUP):
                    for tile in ahead(i, b, g, rows):
                        copy_xnT(*tile)
                    if g == 0:
                        act.wait_ge(s_rn, s + 1)
                    if g == 2 and rows == P:
                        deviations(i + b, 1 - b)
                    if g == 4 and rows == P:
                        norms(i + b, 1 - b)
                    act.wait_ge(s_mm, s * SUP + (g + 1))
                    a = (b + g) % 2
                    nc.scalar.copy(acc[:, ds(s * SUP + g, 1), :].rearrange("p a d -> p (a d)"),
                                   bank[2 + a][:, 0:ROW])
                    nc.scalar.copy(node_logit[:, ds(s * SUP + g, 1), 0:H].rearrange("p a h -> p (a h)"),
                                   bank[2 + a][:, ROW:ROW + H])
                    nc.scalar.activation(qkv[:, ds(s * SUP + g, 1), 0:3 * MHID].rearrange("p a d -> p (a d)"),
                                         bank[4 + a][:, 0:3 * MHID], ACT.Copy, scale=rnorm[:, b, g:g + 1]
                                         ).then_inc(s_xl, 1)
            supers(act, body)


def edge_phase(nc, mem_kv, w_out, b_out, g_out, xl_dram, base_dram, acc, node_logit, qkv, src_idx, dst_loc,
               pair_tile, ident, iota_row, ones, bank):
    with ExitStack() as ctx:
        def sb(name, shape, dt=F32):
            return ctx.enter_context(nc.sbuf_tensor("ed_" + name, shape, dt))

        def sem(name):
            return ctx.enter_context(nc.semaphore("e_" + name))

        rows = sb("rows", [P, U * 4, ROW])
        hot = sb("hot", [P, U, 4, P])
        hotT = sb("hotT", [P, U, 4 * P])
        idx = sb("idx", [P, U * 4], I32)
        logit = sb("logit", [P, 2, 4, H])
        s_rows = [sem(f"rows{u}") for u in range(U)]
        (s_idx, s_hot, s_tr, s_hotT, s_node, s_logit, s_exp, s_scaled, s_sum, s_added, s_chain, s_fence) = (
            sem(n) for n in ("idx", "hot", "tr", "hotT", "node", "logit", "exp", "scaled", "sum", "added", "chain",
                             "fence"))

        top_logit = sb("top_logit", [P, H])
        top_col = sb("top_col", [P, 1])
        self_z = sb("self_z", [P, T, H])
        s_lmax, s_ltp, s_lcol, s_lbc, s_bound, s_self, s_self_w = (
            sem(n) for n in ("lmax", "ltp", "lcol", "lbc", "bound", "self", "self_w"))

        mem = sb("mem", [P, 2, NMEM])
        mem_k = sb("mem_k", [NMEM, P])
        mem_v = sb("mem_v", [NMEM, MHID + 1])
        mem_e = sb("mem_e", [P, NMEM])
        wout = sb("wout", [P, D])
        bout = sb("bout", [1, D])
        gout = sb("gout", [P, D])
        top_keys = sb("top_keys", [P, 4, MHID])
        top_key = sb("top_key", [P, MHID])
        kcol = sb("kcol", [P, 3])
        key_max = sb("key_max", [P, MHID])
        key_exp = sb("key_exp", [P, SUP, MHID])
        qmax = sb("qmax", [P, SUP, MH])
        qsum = sb("qsum", [P, SUP, MH])
        ctx_n = sb("ctx_n", [P, MHID])
        ctx_b = sb("ctx_b", [P, MHID])
        ctx_t = sb("ctx_t", [P, MHID])
        rden = sb("rden", [P, 1])
        mix_w = sb("mix_w", [P, D])
        q_two = sb("q_two", [P, 2, MHID])
        qT = sb("qT", [P, 2 * P])
        junk = sb("junk", [P, 2, D])
        sumsq = sb("sumsq", [P, T])
        base = sb("base", [P, 2, D])
        (s_in, s_kmax, s_ktp, s_kcol, s_kneg, s_kbc, s_kready, s_meme, s_memt, s_mem, s_side) = (
            sem(n) for n in ("in", "kmax", "ktp", "kcol", "kneg", "kbc", "kready", "meme", "memt", "mem", "side"))
        (s_kd, s_ke, s_kfree, s_ctx, s_qd, s_qe, s_qchain, s_qs, s_ctxn, s_ctxt, s_ctxT, s_mw, s_wd) = (
            sem(n) for n in ("kd", "ke", "kfree", "ctx", "qd", "qe", "qchain", "qs", "ctxn", "ctxt", "ctxT", "mw",
                             "wd"))
        (s_mq, s_mt, s_mqT, s_mo, s_mread, s_msq, s_rm, s_radd) = (
            sem(n) for n in ("mq", "mt", "mqT", "mo", "mread", "msq", "rm", "radd"))
        s_base = sem("base")
        keys = qkv[:, :, MHID:2 * MHID]

        TURNS = QUADS // U
        LINKS = 3
        TWOS = T // 2
        segments, at = [], 0
        for kind, turns in (("self loops", 1), ("last self loops", 1), ("key parts", 1), ("key maximum", 1), ("keys", NS - 1), ("last keys", 1), ("queries", NS), ("context", 1),
                            ("mix", TWOS), ("last mix", 1), ("norms", 1), ("rest", TWOS), ("last rest", 1)):
            segments.append((kind, at, turns))
            at += turns
        segments.append(("", at, TURNS - 1 - at))
        block = ctx.enter_context(nc.Block())

        def run(eng, turn):
            for kind, first, turns in segments:
                if turns == 1:
                    turn(first, kind, 0)
                else:
                    with eng.Fori(first, first + turns) as i:
                        turn(i, kind, i - first)
            turn(TURNS - 1, "", 0, True)

        def tiles_of(which, at):
            _, values = nc.values_load_multi_w_load_instructions(
                pair_tile[0:1, ds(at, 2 * U)], engines=(which,), min_val=0, max_val=T - 1,
                skip_runtime_bounds_check_because="pair_tables clamps the tiles")
            return values

        @block.sync
        def _(sp):
            sp.dma_start(mem[:], mem_kv.rearrange("a h d m -> (h d) a m")).then_inc(s_in, 16)
            sp.dma_start(wout[:], w_out).then_inc(s_in, 16)
            sp.dma_start(bout[:], b_out.rearrange("(a d) -> a d", a=1)).then_inc(s_in, 16)
            sp.dma_start(gout[:], g_out.partition_broadcast(P)).then_inc(s_in, 16)
            sp.sem_inc(s_radd, 1)
            with sp.Fori(0, TWOS) as j:
                sp.wait_ge(s_radd, j + 1)
                sp.dma_start(base[:], base_dram[ds(j * (2 * P), 2 * P), :].rearrange("(g p) d -> p g d", p=P)
                             ).then_inc(s_base, 16)
            sp.wait_ge(s_radd, TWOS + 1)
            sp.dma_start(base[0:LAST, 0, :], base_dram[(T - 1) * P:N, :]).then_inc(s_base, 16)

        @block.gpsimd
        def _(pool):
            def gather(u):
                for k in range(4):
                    m = 4 * u + k
                    nc.gpsimd.indirect_dma_start(out=rows[:, m, :], out_offset=None, in_=xl_dram,
                                                 in_offset=bass.IndirectOffsetOnAxis(ap=idx[:, m:m + 1], axis=0)
                                                 ).then_inc(s_rows[u], 16)

            pool.wait_ge(s_idx, U)
            for u in range(U):
                gather(u)
            with pool.Fori(0, TURNS - 1) as i:
                for u in range(U):
                    q = i * U + u
                    pool.wait_ge(s_sum, q * 2 + 2)
                    pool.wait_ge(s_idx, q + (U + 1))
                    pool.sem_inc(s_fence, 1)
                    gather(u)

        @block.scalar
        def _(act):
            def side(kind, j, u):
                if kind == "key maximum" and u == 2:
                    act.wait_ge(s_kneg, 1)
                    nc.scalar.activation(mem_e[:], mem[:, 0, :], ACT.Exp, bias=kcol[:, 2:3]).then_inc(s_meme, 1)
                elif kind in ("keys", "last keys") and u == 1:
                    j = j if kind == "keys" else NS - 1
                    act.wait_ge(s_kd, j + 1)
                    act.wait_ge(s_kfree, j + 1)
                    nc.scalar.activation(key_exp[:], keys[:, ds(j * SUP, SUP), :], ACT.Exp).then_inc(s_ke, 1)
                elif kind == "queries" and u == 1:
                    act.wait_ge(s_qd, j + 1)
                    q = qkv[:, ds(j * SUP, SUP), 0:MHID]
                    nc.scalar.activation(q, q, ACT.Exp).then_inc(s_qe, 1)
                elif kind in ("mix", "last mix"):
                    j, n = (j, 2) if kind == "mix" else (TWOS, 1)
                    if u == 0:
                        nc.scalar.copy(q_two[:, 0:n, :], qkv[:, ds(j * 2, n), 0:MHID]).then_inc(s_mq, 1)
                    elif u == 1:
                        act.wait_ge(s_mt, j + 1)
                        nc.scalar.copy(qT[:, 0:n * P], bank[6][:, 0:n * P]).then_inc(s_mqT, 1)
                    elif u == 3:
                        act.wait_ge(s_mo, j + 1)
                        act.wait_ge(s_mread, j + 1)
                        for g in range(n):
                            nc.scalar.activation(junk[:, g, :], bank[7][:, g * D:(g + 1) * D], ACT.Square,
                                                 accum_out=sumsq[:, ds(j * 2 + g, 1)])
                        nc.scalar.copy(qkv[:, ds(j * 2, n), MHID:3 * MHID],
                                       bank[7][:, 0:n * D].rearrange("p (g d) -> p g d", d=D)).then_inc(s_mread, 1)
                elif kind == "norms" and u == 0:
                    act.wait_ge(s_mread, TWOS + 2)
                    nc.scalar.activation(sumsq[:], sumsq[:], ACT.Sqrt).then_inc(s_msq, 1)

            def copy_indices(q, u):
                nc.scalar.copy(idx[:, 4 * u:4 * u + 4],
                               src_idx[:, ds(q * 2, 2), :].rearrange("p a b -> p (a b)")).then_inc(s_idx, 1)

            def copy_hotT(q, u):
                act.wait_ge(s_tr, q + 1)
                nc.scalar.copy(hotT[:, u, :], bank[2 + u % 2][:]).then_inc(s_hotT, 1)

            def exps(q, u):
                act.wait_ge(s_logit, q + 1)
                nc.scalar.activation(rows[:, 4 * u:4 * u + 4, D:ROW], logit[:, u % 2, :, :], ACT.Exp
                                     ).then_inc(s_exp, 1)

            act.sem_inc(s_mread, 1)
            for u in range(U):
                copy_indices(u, u)
            copy_hotT(0, 0)
            act.wait_ge(s_self, 1)
            nc.scalar.activation(acc[:, :, D:ROW], self_z[:], ACT.Exp).then_inc(s_self_w, 1)
            for u in range(1, 3):
                copy_hotT(u, u)
            exps(0, 0)

            def turn(i, kind, j, last=False):
                for u in range(U):
                    q = i * U + u
                    if not last:
                        copy_indices(q + U, u)
                    if not (last and u == U - 1):
                        exps(q + 1, (u + 1) % U)
                    if not (last and u > 0):
                        copy_hotT(q + 3, (u + 3) % U)
                    side(kind, j, u)

            run(act, turn)

        @block.vector
        def _(dve):
            V = nc.vector
            links = [0]
            side_links = [0]

            def link(ins, i):
                links[0] += 1
                ins.then_inc(s_chain, 1)
                return i * (LINKS * U) + (LINKS + links[0])

            def then(ins):
                side_links[0] += 1
                ins.then_inc(s_side, 1)
                dve.wait_ge(s_side, side_links[0])

            SELF = [0, 2 * 2 * U, 3 * 2 * U, 4 * 2 * U, 5 * 2 * U, T]
            QUARTER = (T - 1) // 4

            def scale_self(n):
                part = acc[:, SELF[n]:SELF[n + 1], :]
                f = part[:, :, 0:D].rearrange("p t (h c) -> p t h c", c=C)
                then(V.tensor_tensor(f, f, part[:, :, D:ROW].unsqueeze(3).to_broadcast(
                    [P, SELF[n + 1] - SELF[n], H, C]), ALU.mult))

            def side(kind, j, u):
                if kind in ("self loops", "last self loops"):
                    if u % 2 == 0:
                        scale_self(1 + u // 2 + (2 if kind == "last self loops" else 0))
                elif kind == "key parts":
                    part = keys[:, u * QUARTER:(u + 1) * QUARTER, :]
                    then(V.tensor_reduce(top_keys[:, u, :], part.rearrange("p t d -> p d t"), X, ALU.max))
                elif kind == "key maximum":
                    if u == 0:
                        then(V.tensor_reduce(top_key[:], top_keys[:].rearrange("p t d -> p d t"), X, ALU.max))
                        V.tensor_tensor(top_key[0:LAST, :], top_key[0:LAST, :], keys[0:LAST, T - 1, :], ALU.max
                                        ).then_inc(s_kmax, 1)
                    elif u == 1:
                        dve.wait_ge(s_ktp, 1)
                        V.tensor_reduce(kcol[:, 0:1], bank[6][:, 0:P], X, ALU.max)
                        dve.wait_ge(s_in, 64)
                        then(V.tensor_reduce(kcol[:, 1:2], mem[:, 0, :], X, ALU.max))
                        V.tensor_tensor(kcol[:, 1:2], kcol[:, 0:1], kcol[:, 1:2], ALU.max).then_inc(s_kcol, 1)
                        dve.wait_ge(s_kcol, 1)
                        V.tensor_scalar(kcol[:, 2:3], kcol[:, 1:2], -1.0, None, ALU.mult).then_inc(s_kneg, 1)
                    elif u == 2:
                        dve.wait_ge(s_kbc, 1)
                        V.tensor_copy(key_max[:], bank[7][:, 0:P]).then_inc(s_kready, 1)
                    else:
                        dve.wait_ge(s_memt, 1)
                        V.tensor_copy(mem_k[:], bank[6][0:NMEM, 0:P])
                        V.tensor_copy(mem_v[:, 0:MHID], bank[6][0:NMEM, P:2 * P]).then_inc(s_mem, 1)
                elif kind in ("keys", "last keys") and u == 0:
                    k = keys[:, ds((j if kind == "keys" else NS - 1) * SUP, SUP), :]
                    dve.wait_ge(s_kready, 1)
                    V.tensor_tensor(k, k, key_max[:].unsqueeze(1).to_broadcast([P, SUP, MHID]), ALU.subtract
                                    ).then_inc(s_kd, 1)
                elif kind == "queries":
                    q = qkv[:, ds(j * SUP, SUP), 0:MHID].rearrange("p t (h d) -> p t h d", d=MD)
                    wide = [P, SUP, MH, MD]
                    if u == 0:
                        V.tensor_reduce(qmax[:], q, X, ALU.max).then_inc(s_qchain, 1)
                        dve.wait_ge(s_qchain, j * 3 + 1)
                        V.tensor_tensor(q, q, qmax[:].unsqueeze(3).to_broadcast(wide), ALU.subtract
                                        ).then_inc(s_qd, 1)
                    elif u == 2:
                        dve.wait_ge(s_qe, j + 1)
                        dve.wait_ge(s_qs, j + 1)
                        dve.sem_inc(s_fence, 1)
                        V.tensor_reduce(qsum[:], q, X, ALU.add).then_inc(s_qchain, 1)
                        dve.wait_ge(s_qchain, j * 3 + 2)
                        V.reciprocal(qsum[:], qsum[:]).then_inc(s_qchain, 1)
                    elif u == 3:
                        dve.wait_ge(s_qchain, j * 3 + 3)
                        V.tensor_tensor(q, q, qsum[:].unsqueeze(3).to_broadcast(wide), ALU.mult).then_inc(s_qs, 1)
                elif kind == "context":
                    if u == 0:
                        dve.wait_ge(s_ctx, 1)
                        then(V.reciprocal(rden[:], bank[6][:, MHID:MHID + 1]))
                        then(V.tensor_scalar(ctx_n[:], bank[6][:, 0:MHID], rden[:, 0:1], float(MD) ** -0.5, ALU.mult,
                                             ALU.mult))
                        for h in range(MH):
                            blk = slice(h * MD, (h + 1) * MD)
                            done = V.tensor_copy(ctx_b[blk, blk], ctx_n[blk, blk])
                        done.then_inc(s_ctxn, 1)
                    elif u == 1:
                        dve.wait_ge(s_ctxt, 1)
                        V.tensor_copy(ctx_t[:], bank[7][:, 0:P]).then_inc(s_ctxT, 1)
                    elif u == 3:
                        dve.wait_ge(s_mw, 1)
                        V.tensor_copy(mix_w[:], bank[6][:, 0:D]).then_inc(s_wd, 1)
                elif kind == "norms" and u == 1:
                    dve.wait_ge(s_msq, 1)
                    then(V.tensor_scalar(sumsq[:], sumsq[:], 1e-12, None, ALU.max))
                    then(V.reciprocal(sumsq[:], sumsq[:]))
                    then(V.tensor_scalar(sumsq[:], sumsq[:], float(D) ** 0.5, None, ALU.mult))
                elif kind in ("rest", "last rest"):
                    j, n = (j, 2) if kind == "rest" else (TWOS, 1)
                    if u == 0:
                        for g in range(n):
                            o = qkv[:, ds(j * 2 + g, 1), MHID:3 * MHID].rearrange("p a d -> p (a d)")
                            done = V.scalar_tensor_tensor(out=o, in0=o, scalar=sumsq[:, ds(j * 2 + g, 1)], in1=gout[:],
                                                          op0=ALU.mult, op1=ALU.mult)
                        done.then_inc(s_rm, 1)
                    elif u == 2:
                        dve.wait_ge(s_rm, j + 1)
                        rest = qkv[:, ds(j * 2, n), MHID:3 * MHID]
                        dve.wait_ge(s_base, j * 16 + 16)
                        V.tensor_tensor(rest, rest, base[:, 0:n, :], ALU.add).then_inc(s_radd, 1)

            def one_hots(q, u):
                V.tensor_tensor(hot[:, u, :, :], iota_row[:].unsqueeze(1).to_broadcast([P, 4, P]),
                                dst_loc[:, ds(q * 2, 2), :].rearrange("p a b -> p (a b)").unsqueeze(2)
                                .to_broadcast([P, 4, P]), ALU.is_equal).then_inc(s_hot, 1)

            def edge_logits(i, turn, q, u, between):
                own = bank[4 + u % 2][:, 0:8 * H].rearrange("p (k h) -> p k h", k=4)
                z = logit[:, u % 2, :, :]
                dve.wait_ge(s_rows[u], turn * 64 + 64)
                dve.wait_ge(s_node, q + 1)
                at = link(V.tensor_tensor(z, rows[:, 4 * u:4 * u + 4, D:ROW], own[:, :, 0:H], ALU.add), i)
                between(0)
                dve.wait_ge(s_chain, at)
                at = link(V.scalar_tensor_tensor(out=z, in0=z, scalar=SLOPE, in1=z, op0=ALU.mult, op1=ALU.max), i)
                between(1)
                dve.wait_ge(s_chain, at)
                at = link(V.tensor_tensor(z, z, own[:, :, H:], ALU.subtract), i)
                between(2)
                dve.wait_ge(s_chain, at)
                V.tensor_scalar(z, z, 0.0, None, ALU.min).then_inc(s_logit, 1)

            def scale(q, u, a):
                r = rows[:, 4 * u + 2 * a:4 * u + 2 * a + 2, :]
                f = r[:, :, 0:D].rearrange("p k (h c) -> p k h c", c=C)
                V.tensor_tensor(f, f, r[:, :, D:ROW].unsqueeze(3).to_broadcast([P, 2, H, C]), ALU.mult
                                ).then_inc(s_scaled, 1)

            def add(q, a, tile):
                dve.wait_ge(s_sum, q * 2 + (a + 1))
                dve.wait_ge(s_added, q * 2 + (a + 2))
                into = acc[:, ds(tile, 1), :].rearrange("p a d -> p (a d)")
                V.tensor_tensor(into, into, bank[a][:, 0:ROW], ALU.add).then_inc(s_added, 1)

            then(V.tensor_reduce(top_logit[:], acc[:, 0:T - 1, D:ROW].rearrange("p t h -> p h t"), X, ALU.max))
            V.tensor_tensor(top_logit[0:LAST, :], top_logit[0:LAST, :], acc[0:LAST, T - 1, D:ROW], ALU.max
                            ).then_inc(s_lmax, 1)
            one_hots(0, 0)
            own_logit, bound = node_logit[:, :, 0:H], node_logit[:, :, H:]
            then(V.tensor_tensor(self_z[:], acc[:, :, D:ROW], own_logit, ALU.add))
            then(V.scalar_tensor_tensor(out=self_z[:], in0=self_z[:], scalar=SLOPE, in1=self_z[:], op0=ALU.mult,
                                        op1=ALU.max))
            dve.wait_ge(s_ltp, 1)
            V.tensor_reduce(top_col[0:H, :], bank[6][0:H, 0:P], X, ALU.max).then_inc(s_lcol, 1)
            one_hots(1, 1)
            dve.wait_ge(s_lbc, 1)
            then(V.tensor_tensor(bound, own_logit, bank[6][:, 0:H].unsqueeze(1).to_broadcast([P, T, H]), ALU.add))
            then(V.scalar_tensor_tensor(out=bound, in0=bound, scalar=SLOPE, in1=bound, op0=ALU.mult, op1=ALU.max))
            dve.sem_inc(s_bound, 1)
            then(V.tensor_tensor(self_z[:], self_z[:], bound, ALU.subtract))
            V.tensor_scalar(self_z[:], self_z[:], 0.0, None, ALU.min).then_inc(s_self, 1)
            one_hots(2, 2)
            V.memset(ctx_b[:], 0.0)
            then(V.memset(mem_v[:, MHID:], 1.0))
            dve.sem_inc(s_qs, 1)
            dve.sem_inc(s_added, 2)
            dve.wait_ge(s_self_w, 1)
            scale_self(0)
            links[0] = -LINKS
            edge_logits(0, 0, 0, 0, lambda n: None)

            def turn(i, kind, j, last=False):
                links[0] = 0
                begin = kind == "self loops"
                tiles = tiles_of(DVE, 0 if begin else i * (2 * U) - 2)
                for u in range(U):
                    q = i * U + u
                    end = last and u == U - 1

                    def add_last(a):
                        if not (begin and u == 0):
                            add(q - 1, a, tiles[2 * u + a - (2 if begin else 0)])

                    def between(n):
                        if n == 1:
                            scale(q, u, 1)
                        else:
                            add_last(n // 2)

                    dve.wait_ge(s_exp, q + 1)
                    scale(q, u, 0)
                    if end:
                        for n in range(3):
                            between(n)
                    else:
                        edge_logits(i, i + (u + 1) // U, q + 1, (u + 1) % U, between)
                    if not (last and u > 0):
                        one_hots(q + 3, (u + 3) % U)
                    side(kind, j, u)
                if last:
                    tiles = tiles_of(DVE, (QUADS - 1) * 2)
                    for a in range(2):
                        add(QUADS - 1, a, tiles[a])

            run(dve, turn)

        @block.tensor
        def _(pe):
            def side(kind, j, u):
                if kind == "key maximum":
                    if u == 0:
                        pe.wait_ge(s_kmax, 1)
                        nc.tensor.transpose(bank[6][:, 0:P], top_key[:], ident[:]).then_inc(s_ktp, 1)
                    elif u == 1:
                        pe.wait_ge(s_kcol, 1)
                        nc.tensor.matmul(bank[7][:, 0:P], kcol[:, 1:2].to_broadcast([P, P]), ident[:], start=True,
                                         stop=True).then_inc(s_kbc, 1)
                    elif u == 2:
                        pe.wait_ge(s_meme, 1)
                        nc.tensor.transpose(bank[6][0:NMEM, 0:P], mem_e[:], ident[:])
                        nc.tensor.transpose(bank[6][0:NMEM, P:2 * P], mem[:, 1, :], ident[:]).then_inc(s_memt, 1)
                    else:
                        pe.wait_ge(s_mem, 1)
                        nc.tensor.matmul(bank[6][:, 0:MHID + 1], mem_k[:], mem_v[:], start=True, stop=False)
                        pe.sem_inc(s_kfree, 1)
                elif kind in ("keys", "last keys") and u == 2:
                    end = kind == "last keys"
                    j = NS - 1 if end else j
                    pe.wait_ge(s_ke, j + 1)
                    for g in range(SUP):
                        r = LAST if end and g == SUP - 1 else P
                        done = nc.tensor.matmul(bank[6][:, 0:MHID + 1], key_exp[0:r, g, :],
                                                qkv[0:r, ds(j * SUP + g, 1), 2 * MHID:].rearrange("p a d -> p (a d)"),
                                                start=False, stop=end and g == SUP - 1)
                    done.then_inc(s_ctx if end else s_kfree, 1)
                elif kind == "context":
                    if u == 0:
                        pe.wait_ge(s_ctxn, 1)
                        nc.tensor.transpose(bank[7][:, 0:P], ctx_b[:], ident[:]).then_inc(s_ctxt, 1)
                    elif u == 2:
                        pe.wait_ge(s_ctxT, 1)
                        nc.tensor.matmul(bank[6][:, 0:D], ctx_t[:], wout[:], start=True, stop=True).then_inc(s_mw, 1)
                elif kind in ("mix", "last mix"):
                    j, n = (j, 2) if kind == "mix" else (TWOS, 1)
                    if u == 0:
                        pe.wait_ge(s_wd, 1)
                        pe.wait_ge(s_mq, j + 1)
                        for g in range(n):
                            done = nc.tensor.transpose(bank[6][:, g * P:(g + 1) * P], q_two[:, g, :], ident[:])
                        done.then_inc(s_mt, 1)
                    elif u == 2:
                        pe.wait_ge(s_mqT, j + 1)
                        pe.wait_ge(s_mread, j + 1)
                        for g in range(n):
                            o = bank[7][:, g * D:(g + 1) * D]
                            nc.tensor.matmul(o, qT[:, g * P:(g + 1) * P], mix_w[:], start=True, stop=False)
                            done = nc.tensor.matmul(o, ones[0:1, :], bout[:], start=False, stop=True)
                        done.then_inc(s_mo, 1)

            def transposes(q, u):
                pe.wait_ge(s_hot, q + 1)
                for k in range(4):
                    last = nc.tensor.transpose(bank[2 + u % 2][:, k * P:(k + 1) * P], hot[:, u, k, :], ident[:])
                last.then_inc(s_tr, 1)

            def node_rows(q, u, tiles):
                pe.wait_ge(s_hotT, q + 1)
                for k in range(4):
                    last = nc.tensor.matmul(bank[4 + u % 2][:, 2 * H * k:2 * H * (k + 1)],
                                            hotT[:, u, k * P:(k + 1) * P],
                                            node_logit[:, ds(tiles[k // 2], 1), :].rearrange("p a h -> p (a h)"),
                                            start=True, stop=True)
                last.then_inc(s_node, 1)

            def sums(q, u, a):
                pe.wait_ge(s_scaled, q * 2 + (a + 1))
                pe.wait_ge(s_added, q * 2 + (a + 1))
                for k in range(2):
                    m = 2 * a + k
                    last = nc.tensor.matmul(bank[a][:, 0:ROW], hot[:, u, m, :], rows[:, 4 * u + m, :],
                                            start=(k == 0), stop=(k == 1))
                last.then_inc(s_sum, 1)

            first = tiles_of(PE, 0)
            pe.wait_ge(s_lmax, 1)
            nc.tensor.transpose(bank[6][0:H, 0:P], top_logit[:], ident[:]).then_inc(s_ltp, 1)
            transposes(0, 0)
            pe.wait_ge(s_lcol, 1)
            nc.tensor.matmul(bank[6][:, 0:H], top_col[0:H, 0:1].to_broadcast([H, P]), ident[0:H, 0:H], start=True,
                             stop=True).then_inc(s_lbc, 1)
            transposes(1, 1)
            pe.wait_ge(s_bound, 1)
            node_rows(0, 0, first[0:2])
            transposes(2, 2)
            node_rows(1, 1, first[2:4])

            def turn(i, kind, j, last=False):
                tiles = tiles_of(PE, i * (2 * U) + 4)
                for u in range(U):
                    q = i * U + u
                    for a in range(2):
                        sums(q, u, a)
                    if not (last and u > 1):
                        node_rows(q + 2, (u + 2) % U, tiles[2 * u:2 * u + 2])
                    if not (last and u > 0):
                        transposes(q + 3, (u + 3) % U)
                    side(kind, j, u)

            run(pe, turn)


def combine(nc, Wr, br, gnn_bias, gnn_gamma, acc, stats, y_sum, router, qkv, ident, ones, bank):
    with ExitStack() as ctx:
        def sb(name, shape, dt=F32):
            return ctx.enter_context(nc.sbuf_tensor("cb_" + name, shape, dt))

        def sem(name):
            return ctx.enter_context(nc.semaphore("m_" + name))

        gain = sb("gain", [P, 2, D])
        zero2 = sb("zero2", [P, 2])
        mixed = sb("mixed", [P, 2, SUP, D])
        y = sb("y", [P, 1, SUP, D])
        rden = sb("rden", [P, T, H])
        bn = sb("bn", [P, 2, SUP, 6])
        mv = sb("mv", [P, T, 2, 2])
        shift = sb("shift", [P, T, 2])
        (s_par, s_chain, s_zero, s_den, s_biased, s_var, s_dev, s_shift, s_normed, s_scaled, s_z, s_y, s_ysum,
         s_router) = (
            sem(n) for n in ("par", "chain", "zero", "den", "biased", "var", "dev", "shift", "normed", "scaled", "z",
                             "y", "ysum", "router"))
        block = ctx.enter_context(nc.Block())

        def tiles(s):
            return slice(s * SUP, (s + 1) * SUP)

        turns = [(s, n) for t in range(NS + 1) for s, n in ((t, 0), (t - 1, 1)) if 0 <= s < NS]
        place = {turn: n + 1 for n, turn in enumerate(turns)}

        @block.sync
        def _(sp):
            for n, v in enumerate((gnn_bias, gnn_gamma)):
                sp.dma_start(gain[:, n, :], v.partition_broadcast(P)).then_inc(s_par, 16)
            sp.dma_start(router[:, 0:2, :], Wr.rearrange("(k p) e -> p k e", p=P)).then_inc(s_router, 16)
            sp.dma_start(router[:, 2, :], br.partition_broadcast(P)).then_inc(s_router, 16)
            sp.wait_ge(s_router, 32)

        @block.vector
        def _(dve):
            V = nc.vector
            links = [0]

            def link(ins):
                links[0] += 1
                ins.then_inc(s_chain, 1)
                dve.wait_ge(s_chain, links[0])

            def divide(s):
                z = acc[:, tiles(s), 0:D].rearrange("p t (h c) -> p t h c", c=C)
                V.tensor_tensor(z, z, rden[:, tiles(s), :].unsqueeze(3).to_broadcast([P, SUP, H, C]), ALU.mult
                                ).then_inc(s_den, 1)

            def variance(s, n):
                view = mixed[:, s % 2, :, :] if n == 0 else acc[:, tiles(s), 0:D]
                for g in range(SUP):
                    done = V.bn_stats(bn[:, n, g, :], view[:, g, :])
                link(done)
                for g in range(SUP):
                    done = V.bn_aggr(mv[:, s * SUP + g, n, :], bn[:, n, g, :])
                link(done)
                var = mv[:, tiles(s), n, 1]
                V.tensor_scalar(var, var, LN_EPS, None, ALU.add).then_inc(s_var, 1)

            def scale_shift(s, n):
                m, r = mv[:, tiles(s), n, 0], mv[:, tiles(s), n, 1]
                dve.wait_ge(s_dev, place[s, n])
                link(V.reciprocal(r, r))
                if n == 1:
                    V.tensor_copy(stats[:, tiles(s), :], mv[:, tiles(s), 1, :])
                V.scalar_tensor_tensor(out=shift[:, tiles(s), n], in0=m, scalar=-1.0, in1=r, op0=ALU.mult,
                                       op1=ALU.mult).then_inc(s_shift, 1)

            V.memset(zero2[:], 0.0).then_inc(s_zero, 1)
            link(V.reciprocal(rden[:], acc[:, :, D:ROW]))
            divide(0)
            divide(1)
            dve.wait_ge(s_par, 32)
            for s in range(NS + 1):
                if s < NS:
                    dve.wait_ge(s_biased, s + 1)
                    variance(s, 0)
                    if s + 2 < NS:
                        divide(s + 2)
                    scale_shift(s, 0)
                if s >= 1:
                    dve.wait_ge(s_z, s)
                    variance(s - 1, 1)
                    scale_shift(s - 1, 1)
                if s < NS:
                    dve.wait_ge(s_normed, s + 1)
                    V.tensor_tensor(mixed[:, s % 2, :, :], mixed[:, s % 2, :, :],
                                    gain[:, 1:2, :].to_broadcast([P, SUP, D]), ALU.mult).then_inc(s_scaled, 1)
            dve.wait_ge(s_ysum, NS)
            V.tensor_scalar(y_sum[:, 0:2], bank[2][:, 0:2], 1.0 / N, None, ALU.mult).then_inc(s_zero, 1)

        @block.gpsimd
        def _(pool):
            pool.wait_ge(s_par, 32)

            def bias(s):
                pool.wait_ge(s_den, s + 1)
                nc.gpsimd.tensor_tensor(mixed[:, s % 2, :, :], acc[:, tiles(s), 0:D],
                                        gain[:, 0:1, :].to_broadcast([P, SUP, D]), ALU.add).then_inc(s_biased, 1)

            bias(0)
            bias(1)
            for s in range(NS):
                pool.wait_ge(s_scaled, s + 1)
                nc.gpsimd.tensor_tensor(acc[:, tiles(s), 0:D], mixed[:, s % 2, :, :],
                                        qkv[:, tiles(s), MHID:3 * MHID], ALU.add).then_inc(s_z, 1)
                if s + 2 < NS:
                    pool.wait_ge(s_z, s + 1)
                    bias(s + 2)

        @block.scalar
        def _(act):
            for s, n in turns:
                var = mv[:, tiles(s), n, 1]
                act.wait_ge(s_var, place[s, n])
                nc.scalar.activation(var, var, ACT.Sqrt).then_inc(s_dev, 1)
                act.wait_ge(s_shift, place[s, n])
                if n == 1 and s >= 1:
                    act.wait_ge(s_ysum, s)
                for g in range(SUP):
                    t = s * SUP + g
                    src = mixed[:, s % 2, g, :] if n == 0 else acc[:, t, 0:D]
                    dst = mixed[:, s % 2, g, :] if n == 0 else y[:, 0, g, :]
                    done = nc.scalar.activation(dst, src, ACT.Identity, bias=shift[:, t, n:n + 1],
                                                scale=mv[:, t, n, 1:2])
                done.then_inc(s_y if n else s_normed, 1)

        @block.tensor
        def _(pe):
            pe.wait_ge(s_zero, 1)
            nc.tensor.matmul(bank[2][:, 0:2], ident[:], zero2[:], start=True, stop=False)
            for s in range(NS):
                pe.wait_ge(s_y, s + 1)
                for g in range(SUP):
                    end = s == NS - 1 and g == SUP - 1
                    r = LAST if end else P
                    for k in range(2):
                        t = nc.tensor.matmul(bank[2][:, k:k + 1], y[0:r, 0, g, k * P:(k + 1) * P], ones[0:r, 0:1],
                                             start=False, stop=end and k == 1)
                t.then_inc(s_ysum, 1)


def experts(nc, W1, b1, W2, b2, ffn_gamma, ffn_beta, acc, stats, y_sum, router, ident, bank, out):
    with ExitStack() as ctx:
        def sb(name, shape, dt=F32):
            return ctx.enter_context(nc.sbuf_tensor("ex_" + name, shape, dt))

        def sem(name):
            return ctx.enter_context(nc.semaphore("f_" + name))

        HIGH, LOW = 0, 1
        PARTS = ((LOW, HIGH), (HIGH, LOW), (HIGH, HIGH))
        off_i = sb("off_i", [P, FC], I32)
        off_f = sb("off_f", [P, FC])
        a = sb("a", [P, 8, EX])
        top8 = sb("top8", [P, 8])
        top8_i = sb("top8_i", [P, 8], U32)
        which = sb("which", [P, 2])
        scaled = sb("scaled", [P, 2, 2])
        idx_f = sb("idx_f", [P, 2, 2 + FC])
        idx_i = sb("idx_i", [P, 2, 2 + FC], I32)
        one_i = sb("one_i", [P, 2], I32)
        w1 = sb("w1", [P, 2, 2, 2, F], F32R)
        w2 = sb("w2", [P, 2, 2, FC, D], F32R)
        b1c = sb("b1c", [P, 2, FC])
        b2r = sb("b2r", [P, 1, D])
        gain = sb("gain", [P, 2, D])
        y = sb("y", [P, 2, SUP, D])
        yT = sb("yT", [P, 2, 2, 2, SUP * P], F32R)
        hidden = sb("hidden", [P, 4, 4 * P])
        hT = sb("hT", [P, 2, 2 * FC, SUP * P], F32R)
        bn = sb("bn", [P, SUP, 6])
        mv = sb("mv", [P, SUP, 2])
        res = sb("res", [P, 2, SUP, D])
        w1_in = flat(hidden[:]).rearrange("p (e k f) -> p e k f", e=2, k=2)
        w2_in = res[:].rearrange("p b g d -> p (b g) d")[:, 0:2 * FC, :].rearrange("p (e f) d -> p e f d", e=2)
        b2_in = res[:].rearrange("p b g d -> p (b g) d")[:, 2 * FC:2 * FC + 2, :]
        (s_par, s_chain, s_fence, s_lg, s_e, s_ee, s_idx, s_off, s_w1_in, s_w1, s_b1, s_b2_in, s_b2, s_w2_in, s_w2,
         s_y, s_tp, s_yT, s_yT_low, s_h, s_act, s_low, s_o, s_read, s_yb, s_xb, s_res, s_var, s_dev, s_tail) = (
            sem(n) for n in ("par", "chain", "fence", "lg", "e", "ee", "idx", "off", "w1_in", "w1", "b1", "b2_in",
                             "b2", "w2_in", "w2", "y", "tp", "yT", "yT_low", "h", "act", "low", "o", "read", "yb",
                             "xb", "res", "var", "dev", "tail"))
        s_stored = [sem("stored_even"), sem("stored_odd")]
        block = ctx.enter_context(nc.Block())
        last = (NS - 1) // 2
        UNITS = 4 * FC

        def supers(eng, body):
            with eng.Fori(0, last) as i:
                for b in range(2):
                    body(i, b, P)
            body(last, 0, LAST)

        halves = ((0, 4), (4, SUP))
        EARLY = UNITS - 5

        @block.sync
        def _(sp):
            sp.dma_start(gain[:, 0, :], ffn_gamma.partition_broadcast(P)).then_inc(s_par, 16)
            sp.dma_start(gain[:, 1, :], ffn_beta.partition_broadcast(P)).then_inc(s_par, 16)
            for b in range(2):
                sp.sem_inc(s_stored[b], 16)

            def body(i, b, rows):
                s = i * 2 + b
                sp.wait_ge(s_res, s + 1)
                if rows == P:
                    sp.dma_start(out[ds(s * (SUP * P), SUP * P), :].rearrange("(g p) d -> p g d", p=P),
                                 res[:, b, :, :]).then_inc(s_stored[b], 16)
                else:
                    at = (T - 1) * P
                    sp.dma_start(out[s * SUP * P:at, :].rearrange("(g p) d -> p g d", p=P),
                                 res[:, b, 0:SUP - 1, :]).then_inc(s_stored[b], 16)
                    sp.dma_start(out[at:at + rows, :], res[0:rows, b, SUP - 1, :]).then_inc(s_stored[b], 16)
            supers(sp, body)
            sp.wait_ge(s_stored[0], 16 * (last + 3))
            sp.wait_ge(s_stored[1], 16 * (last + 1))

        @block.gpsimd
        def _(pool):
            nc.gpsimd.iota(off_i[:], pattern=[[P, FC]], base=0, channel_multiplier=1).then_inc(s_off, 1)
            pool.wait_ge(s_idx, 1)
            w1_rows = W1.rearrange("e d f -> (e d) f")
            w2_rows = W2.rearrange("e f d -> (e f) d")
            b1_rows = b1.rearrange("e (f a) -> (e f) a", a=1)

            def gather(dest, table, index, signal):
                nc.gpsimd.indirect_dma_start(out=dest, out_offset=None, in_=table,
                                             in_offset=bass.IndirectOffsetOnAxis(ap=index, axis=0)
                                             ).then_inc(signal, 16)

            for e in range(2):
                for k in range(2):
                    gather(w1_in[:, e, k, :], w1_rows, idx_i[:, e, k:k + 1], s_w1_in)
            for e in range(2):
                for f in range(FC):
                    gather(b1c[:, e, f:f + 1], b1_rows, idx_i[:, e, 2 + f:3 + f], s_b1)
            for e in range(2):
                gather(b2_in[:, e, :], b2, one_i[:, e:e + 1], s_b2_in)
            for e in range(2):
                for f in range(FC):
                    gather(w2_in[:, e, f, :], w2_rows, idx_i[:, e, 2 + f:3 + f], s_w2_in)
            pool.wait_ge(s_par, 32)
            pool.wait_ge(s_b2, 1)

            def body(i, b, rows):
                s = i * 2 + b
                x2 = acc[:, ds(s * SUP, SUP), 0:D]
                pool.wait_ge(s_y, s + 1)
                pool.sem_inc(s_fence, 1)
                nc.gpsimd.tensor_tensor(x2, x2, gain[:, 1:2, :].to_broadcast([P, SUP, D]), ALU.add).then_inc(s_xb, 1)
                pool.wait_ge(s_tp, s * 4 + 4)
                pool.sem_inc(s_fence, 1)
                nc.gpsimd.tensor_tensor(y[:, b, :, :], y[:, b, :, :], b2r[:].to_broadcast([P, SUP, D]),
                                        ALU.add).then_inc(s_yb, 1)
            supers(pool, body)

        @block.vector
        def _(dve):
            links = [0]

            def link(ins):
                links[0] += 1
                ins.then_inc(s_chain, 1)
                dve.wait_ge(s_chain, links[0])

            V = nc.vector
            dve.wait_ge(s_off, 1)
            link(V.tensor_copy(off_f[:], off_i[:]))
            dve.wait_ge(s_lg, 1)
            link(V.tensor_tensor(a[:, 0, :], bank[0][:, 0:EX], router[:, 2, :], ALU.add))

            def softmax(src, dst, n):
                link(V.tensor_reduce(top8[:, 0:1], src, X, ALU.max))
                V.tensor_scalar(dst, src, top8[:, 0:1], None, ALU.subtract).then_inc(s_e, 1)
                dve.wait_ge(s_ee, n)
                link(V.tensor_reduce(top8[:, 0:1], dst, X, ALU.add))
                link(V.reciprocal(top8[:, 0:1], top8[:, 0:1]))
                link(V.tensor_scalar(dst, dst, top8[:, 0:1], None, ALU.mult))

            softmax(a[:, 0, :], a[:, 1, :], 1)
            link(V.tensor_scalar(a[:, 2, :], a[:, 1, :], float(N), None, ALU.mult))
            link(V.tensor_scalar(a[:, 3, :], a[:, 2, :], CAP, None, ALU.max))
            link(V.reciprocal(a[:, 4, :], a[:, 3, :]))
            link(V.tensor_scalar(a[:, 4, :], a[:, 4, :], CAP, None, ALU.mult))
            link(V.tensor_tensor(a[:, 5, :], a[:, 1, :], a[:, 4, :], ALU.mult))
            softmax(a[:, 5, :], a[:, 6, :], 2)
            link(V.max(top8[:], a[:, 6, :]))
            link(V.max_index(top8_i[:], top8[:], a[:, 6, :]))
            V.tensor_tensor(a[:, 7, 0:1], top8[:, 1:2], top8[:, 0:1], ALU.subtract).then_inc(s_e, 1)
            link(V.tensor_copy(which[:], top8_i[:, 0:2]))
            V.tensor_copy(one_i[:], which[:])
            V.tensor_scalar(scaled[:, 0, :], which[:], float(D), None, ALU.mult)
            link(V.tensor_scalar(scaled[:, 1, :], which[:], float(F), None, ALU.mult))
            for e in range(2):
                V.tensor_scalar(idx_f[:, e, 0:2], off_f[:, 0:2], scaled[:, 0, e:e + 1], None, ALU.add)
                done = V.tensor_scalar(idx_f[:, e, 2:], off_f[:], scaled[:, 1, e:e + 1], None, ALU.add)
            link(done)
            V.tensor_copy(idx_i[:], idx_f[:]).then_inc(s_idx, 1)

            def norm(i, b):
                s = i * 2 + b
                for g in range(SUP):
                    row = acc[:, ds(s * SUP + g, 1), 0:D].rearrange("p a d -> p (a d)")
                    done = V.tensor_scalar(y[:, b, g, :], row, stats[:, ds(s * SUP + g, 1), 0],
                                           stats[:, ds(s * SUP + g, 1), 1], ALU.subtract, ALU.mult)
                done.then_inc(s_y, 1)

            def yT_lows(i, b, pieces):
                s = i * 2 + b
                for k, half in pieces:
                    lo, hi = halves[half]
                    dve.wait_ge(s_yT, s * 4 + (2 * k + half + 1))
                    V.tensor_tensor(yT[:, b, LOW, k, lo * P:hi * P], bank[half][:, 0:(hi - lo) * P],
                                    yT[:, b, HIGH, k, lo * P:hi * P].bitcast(F32), ALU.subtract).then_inc(s_yT_low, 1)

            norm(0, 0)
            dve.wait_ge(s_ee, 3)
            link(V.tensor_scalar(a[:, 7, 1:2], a[:, 7, 0:1], 1.0, None, ALU.add))
            link(V.reciprocal(a[:, 7, 2:3], a[:, 7, 1:2]))
            link(V.tensor_tensor(a[:, 7, 3:4], a[:, 7, 0:1], a[:, 7, 2:3], ALU.mult))
            yT_lows(0, 0, ((0, 0), (0, 1), (1, 0), (1, 1)))
            dve.wait_ge(s_w1_in, 16 * 4)
            link(V.tensor_copy(w1[:, HIGH, :, :, :], w1_in))
            V.tensor_tensor(w1[:, LOW, :, :, :], w1_in, w1[:, HIGH, :, :, :].bitcast(F32), ALU.subtract
                            ).then_inc(s_w1, 1)

            def mixture_b2():
                dve.wait_ge(s_b2_in, 16 * 2)
                for e in range(2):
                    done = V.tensor_scalar(b2_in[:, e, :], b2_in[:, e, :], a[:, 7, 2 + e:3 + e], None, ALU.mult)
                link(done)
                V.tensor_tensor(b2r[:, 0, :], b2_in[:, 0, :], b2_in[:, 1, :], ALU.add).then_inc(s_b2, 1)

            def mixture_w2():
                dve.wait_ge(s_w2_in, 16 * 2 * FC)
                for e in range(2):
                    done = V.tensor_scalar(w2_in[:, e, :, :], w2_in[:, e, :, :], a[:, 7, 2 + e:3 + e], None, ALU.mult)
                link(done)
                link(V.tensor_copy(w2[:, HIGH, :, :, :], w2_in))
                done = V.tensor_tensor(w2[:, LOW, :, :, :], w2_in, w2[:, HIGH, :, :, :].bitcast(F32), ALU.subtract)
                link(done)
                dve.sem_inc(s_w2, 1)

            def turn(counted):
                def tail_link(ins):
                    counted[1] += 1
                    ins.then_inc(s_tail, 1)
                    dve.wait_ge(s_tail, counted[0] * TAIL + counted[1])
                return tail_link

            TAIL = 5

            def tail_statistics(i, b, tail_link):
                dve.sem_inc(s_fence, 1)
                for g in range(SUP):
                    done = V.bn_aggr(mv[:, g, :], bn[:, g, :])
                tail_link(done)
                V.tensor_scalar(mv[:, :, 1], mv[:, :, 1], LN_EPS, None, ALU.add).then_inc(s_var, 1)

            def tail_center(i, b, tail_link):
                dve.wait_ge(s_dev, i * 2 + b + 1)
                tail_link(V.reciprocal(mv[:, :, 1], mv[:, :, 1]))
                for g in range(SUP):
                    done = V.scalar_tensor_tensor(out=res[:, b, g, :], in0=res[:, b, g, :], scalar=mv[:, g, 0:1],
                                                  in1=gain[:, 0, :], op0=ALU.subtract, op1=ALU.mult)
                tail_link(done)

            def tail_add(i, b, tail_link):
                s = i * 2 + b
                dve.wait_ge(s_xb, s + 1)
                dve.sem_inc(s_fence, 1)
                for g in range(SUP):
                    row = acc[:, ds(s * SUP + g, 1), 0:D].rearrange("p a d -> p (a d)")
                    done = V.scalar_tensor_tensor(out=res[:, b, g, :], in0=res[:, b, g, :], scalar=mv[:, g, 1:2],
                                                  in1=row, op0=ALU.mult, op1=ALU.add)
                tail_link(done)
                dve.sem_inc(s_res, 1)

            def body(i, b, rows, before):
                s = i * 2 + b
                if before is not None:
                    tail_link = turn([before[0] * 2 + before[1], 1])
                for n in range(UNITS):
                    ef, half = n // 2, n % 2
                    lo, hi = halves[half]
                    dve.wait_ge(s_act, s * UNITS + (4 + n + 1))
                    V.tensor_tensor(hT[:, LOW, ef, lo * P:hi * P], hidden[:, n % 4, 0:(hi - lo) * P],
                                    hT[:, HIGH, ef, lo * P:hi * P].bitcast(F32), ALU.subtract).then_inc(s_low, 1)
                    if n == 0 and rows == P:
                        norm(i + b, 1 - b)
                    if n == 2 and before is not None:
                        tail_statistics(*before, tail_link)
                    if n == 5 and before is not None:
                        tail_center(*before, tail_link)
                    if n == 8 and before is not None:
                        tail_add(*before, tail_link)
                    if n == 6 and before is None:
                        mixture_b2()
                    if n == 12 and before is None:
                        mixture_w2()
                    if n == EARLY and rows == P:
                        yT_lows(i + b, 1 - b, ((0, 0), (0, 1)))
                if rows == P:
                    yT_lows(i + b, 1 - b, ((1, 0), (1, 1)))
                dve.wait_ge(s_yb, s + 1)
                dve.wait_ge(s_stored[b], i * 16 + 16)
                for g in range(SUP + 1):
                    if g < SUP:
                        dve.wait_ge(s_o, s * SUP + (g + 1))
                        V.tensor_tensor(res[:, b, g, :], bank[6 + (b + g) % 2][:, 0:D], y[:, b, g, :], ALU.add
                                        ).then_inc(s_read, 1)
                    if g >= 1:
                        dve.wait_ge(s_read, s * SUP + (g + 2))
                        done = V.bn_stats(bn[:, g - 1, :], res[:, b, g - 1, :])
                done.then_inc(s_tail, 1)
                dve.wait_ge(s_tail, s * TAIL + 1)

            body(0, 0, P, None)
            with dve.Fori(0, last - 1) as i:
                body(i, 1, P, (i, 0))
                body(i + 1, 0, P, (i, 1))
            body(last - 1, 1, P, (last - 1, 0))
            body(last, 0, LAST, (last - 1, 1))
            tail_link = turn([NS - 1, 1])
            tail_statistics(last, 0, tail_link)
            tail_center(last, 0, tail_link)
            tail_add(last, 0, tail_link)

        @block.scalar
        def _(act):
            for n, row in enumerate((1, 6)):
                act.wait_ge(s_e, n + 1)
                nc.scalar.activation(a[:, row, :], a[:, row, :], ACT.Exp).then_inc(s_ee, 1)
            act.wait_ge(s_e, 3)
            nc.scalar.activation(a[:, 7, 0:1], a[:, 7, 0:1], ACT.Exp).then_inc(s_ee, 1)

            def copy_yT(i, b, pieces):
                s = i * 2 + b
                for k, half in pieces:
                    lo, hi = halves[half]
                    act.wait_ge(s_tp, s * 4 + (2 * k + half + 1))
                    nc.scalar.copy(yT[:, b, HIGH, k, lo * P:hi * P], bank[half][:, 0:(hi - lo) * P]).then_inc(s_yT, 1)

            copy_yT(0, 0, ((0, 0), (0, 1), (1, 0), (1, 1)))
            act.wait_ge(s_b1, 16 * 2 * FC)

            def body(i, b, rows, before):
                s = i * 2 + b
                for n in range(UNITS):
                    ef, half = n // 2, n % 2
                    lo, hi = halves[half]
                    unit, bias = bank[2 + n % 4][:, 0:(hi - lo) * P], b1c[:, ef // FC, ef % FC:ef % FC + 1]
                    act.wait_ge(s_h, s * UNITS + (n + 1))
                    if n < 4 and before is None:
                        pass
                    else:
                        act.wait_ge(s_low, s * UNITS + (n - 3))
                    nc.scalar.activation(hidden[:, n % 4, 0:(hi - lo) * P], unit, ACT.Gelu, bias=bias)
                    nc.scalar.activation(hT[:, HIGH, ef, lo * P:hi * P], unit, ACT.Gelu, bias=bias).then_inc(s_act, 1)
                    if n == 3 and before is not None:
                        deviations(*before)
                    if n == EARLY and rows == P:
                        copy_yT(i + b, 1 - b, ((0, 0), (0, 1)))
                if rows == P:
                    copy_yT(i + b, 1 - b, ((1, 0), (1, 1)))

            def deviations(i, b):
                act.wait_ge(s_var, i * 2 + b + 1)
                nc.scalar.activation(mv[:, :, 1], mv[:, :, 1], ACT.Sqrt).then_inc(s_dev, 1)

            body(0, 0, P, None)
            with act.Fori(0, last - 1) as i:
                body(i, 1, P, (i, 0))
                body(i + 1, 0, P, (i, 1))
            body(last - 1, 1, P, (last - 1, 0))
            body(last, 0, LAST, (last - 1, 1))
            deviations(last, 0)

        @block.tensor
        def _(pe):
            for k in range(2):
                done = nc.tensor.matmul(bank[0][:, 0:EX], y_sum[:, k:k + 1].to_broadcast([P, P]), router[:, k, :],
                                        start=(k == 0), stop=(k == 1))
            done.then_inc(s_lg, 1)
            pe.sem_inc(s_act, 4)
            pe.sem_inc(s_read, 2)
            pe.sem_inc(s_yT_low, 2)

            def transposes(i, b, pieces):
                s = i * 2 + b
                pe.wait_ge(s_y, s + 1)
                for k, half in pieces:
                    lo, hi = halves[half]
                    pe.wait_ge(s_yT_low, s * 4 + (2 * k + half + 1))
                    for g in range(lo, hi):
                        done = nc.tensor.transpose(bank[half][:, (g - lo) * P:(g - lo + 1) * P],
                                                   y[:, b, g, k * P:(k + 1) * P], ident[:])
                    done.then_inc(s_tp, 1)

            transposes(0, 0, ((0, 0), (0, 1), (1, 0), (1, 1)))
            pe.wait_ge(s_w1, 1)

            def body(i, b, rows):
                s = i * 2 + b
                pe.wait_ge(s_yT_low, s * 4 + 6)
                for n in range(UNITS):
                    ef, half = n // 2, n % 2
                    lo, hi = halves[half]
                    pe.wait_ge(s_act, s * UNITS + (n + 1))
                    for k in range(2):
                        for m, (wp, yp) in enumerate(PARTS):
                            done = nc.tensor.matmul(bank[2 + n % 4][:, 0:(hi - lo) * P],
                                                    w1[:, wp, ef // FC, k, (ef % FC) * P:(ef % FC + 1) * P],
                                                    yT[:, b, yp, k, lo * P:hi * P], start=(k == 0 and m == 0),
                                                    stop=(k == 1 and m == 2))
                    done.then_inc(s_h, 1)
                    if n == EARLY and rows == P:
                        transposes(i + b, 1 - b, ((0, 0), (0, 1)))
                if rows == P:
                    transposes(i + b, 1 - b, ((1, 0), (1, 1)))
                pe.wait_ge(s_w2, 1)
                for g in range(SUP):
                    pe.wait_ge(s_low, s * UNITS + (UNITS - 1 if g < halves[0][1] else UNITS))
                    pe.wait_ge(s_read, s * SUP + (g + 1))
                    for ef in range(2 * FC):
                        for m, (hp, wp) in enumerate(PARTS):
                            done = nc.tensor.matmul(bank[6 + (b + g) % 2][:, 0:D],
                                                    hT[:, hp, ef, g * P:(g + 1) * P],
                                                    w2[:, wp, ef // FC, ef % FC, :], start=(ef == 0 and m == 0),
                                                    stop=(ef == 2 * FC - 1 and m == 2))
                    done.then_inc(s_o, 1)
            supers(pe, body)


INS = ['x', 'src', 'dst', 'L0_gnn_W', 'L0_gnn_att_src', 'L0_gnn_att_dst', 'L0_gnn_bias', 'L0_gnn_gamma',
       'L0_gnn_beta', 'L0_mix_w_qkv', 'L0_mix_mem_kv', 'L0_mix_w_out', 'L0_mix_b_out', 'L0_mix_g_out',
       'L0_mix_g_pre', 'L0_ffn_Wr', 'L0_ffn_br', 'L0_ffn_W1', 'L0_ffn_b1', 'L0_ffn_W2', 'L0_ffn_b2',
       'L0_ffn_gamma', 'L0_ffn_beta']


def kernel(**inputs):
    import numpy as np
    import concourse.bacc as bacc
    from concourse.bass_utils import run_bass_kernel_spmd

    nc = bacc.Bacc("TRN2", target_bir_lowering=False, num_devices=1)
    arrays, args = {}, []
    for name in INS:
        a = np.ascontiguousarray(inputs[name])
        arrays["in_" + name] = a
        args.append(nc.dram_tensor("in_" + name, a.shape, mybir.dt.from_np(a.dtype), kind="ExternalInput").ap())
    xl_dram = nc.dram_tensor("xl_dram", (N, ROW), F32, kind="Internal").ap()
    base_dram = nc.dram_tensor("base_dram", (N, D), F32, kind="Internal").ap()
    edges_dram = nc.dram_tensor("edges_dram", (GR + 1, 2 * GE), I32, kind="Internal").ap()
    pair_dram = nc.dram_tensor("pair_dram", (PC * P,), I32, kind="Internal").ap()
    out = nc.dram_tensor("out_0", (N, D), F32, kind="ExternalOutput").ap()
    gps_layer(nc, *args, xl_dram, base_dram, edges_dram, pair_dram, out)
    r = run_bass_kernel_spmd(nc, [arrays], core_ids=[0])
    return r.results[0]["out_0"]
```

```python
from contextlib import ExitStack

import concourse.bass as bass
from concourse import mybir

ALU = mybir.AluOpType
ACT = mybir.ActivationFunctionType
F32 = mybir.dt.float32
BF16 = mybir.dt.bfloat16
F32R = mybir.dt.float32r
I32 = mybir.dt.int32
U32 = mybir.dt.uint32
X = mybir.AxisListType.X
DVE = mybir.EngineType.DVE
PE = mybir.EngineType.PE
ds = bass.ds

P = 128
N, D, E = 6250, 256, 200000
H, C = 8, 32
T = -(-N // P)
LAST = N - (T - 1) * P
SUP = 7
NS = T // SUP
ROW = H * C + H
GE = P
GR = -(-E // GE)
PAIRS = GR + T - 1
NOWHERE = T * P
U = 4
QUADS = -(-PAIRS // (4 * U)) * U
PC = -(-(QUADS * 4 + 16) // P)
MH, MD = 4, 32
MHID = MH * MD
NMEM = 4
EX, F = 8, 512
FC = F // P
LN_EPS = 1e-5
SLOPE = 0.2
CAP = float(-(-N * 5 // (4 * EX)))
QKV0 = ROW + H


def flat(ap):
    return ap.rearrange("p a b -> p (a b)")


def gps_layer(nc, x, src, dst, W, att_src, att_dst, gnn_bias, gnn_gamma, gnn_beta, w_qkv, mem_kv, w_out, b_out,
              g_out, g_pre, Wr, br, W1, b1, W2, b2, ffn_gamma, ffn_beta, xl_dram, base_dram, edges_dram,
              pair_dram, out):
    top = ExitStack()

    def alloc(stack):
        return (lambda name, shape, dt=F32: stack.enter_context(nc.sbuf_tensor(name, shape, dt)),
                lambda name: stack.enter_context(nc.semaphore(name)))

    with top:
        top.enter_context(nc.allow_non_contiguous_dma(reason="a few hundred single words, once"))
        sb, _ = alloc(top)
        bank = [top.enter_context(nc.psum_tensor(f"bank{i}", [P, 512], F32)) for i in range(8)]
        acc = sb("acc", [P, T, ROW])
        ident = sb("ident", [P, P])
        stats = sb("stats", [P, T, 2])
        y_sum = sb("y_sum", [P, 2])
        router = sb("router", [P, 3, EX])
        with ExitStack() as attention:
            sa, _ = alloc(attention)
            src_idx = sa("src_idx", [P, PC * P], I32)
            dst_loc = sa("dst_loc", [P, PC * P])
            iota_row = sa("iota_row", [P, P])
            ones = sa("ones", [P, P])
            ones_bf = sa("ones_bf", [P, P], BF16)
            node_logit = sa("node_logit", [P, T, 2 * H])
            pair_tile = sa("pair_tile", [1, PC * P], I32)
            qkv = sa("qkv", [P, T, 3 * MHID + 1])
            with ExitStack() as projection:
                sp, _ = alloc(projection)
                w_part = sp("w_part", [P, 2, 2, QKV0 + 3 * MHID], F32R)
                beta = sp("beta", [P, 1, D])
                xin = sp("xin", [P, 2, SUP, D])
                mv = sp("mv", [P, 2, SUP, 2])
                pair_tables(nc, dst, src, edges_dram, pair_dram, ident, iota_row, ones, ones_bf, src_idx, dst_loc,
                            pair_tile, x, W, att_src, att_dst, w_qkv, g_pre, gnn_beta, w_part, beta, xin, mv, acc,
                            bank)
                project(nc, x, w_part, beta, xin, mv, xl_dram, base_dram, acc, node_logit, qkv, ident, bank)
            edge_phase(nc, mem_kv, w_out, b_out, g_out, xl_dram, base_dram, acc, node_logit, qkv, src_idx, dst_loc,
                       pair_tile, ident, iota_row, ones, bank)
            combine(nc, Wr, br, gnn_bias, gnn_gamma, acc, stats, y_sum, router, qkv, ident, ones, bank)
        experts(nc, W1, b1, W2, b2, ffn_gamma, ffn_beta, acc, stats, y_sum, router, ident, bank, out)


def pair_tables(nc, dst, src, edges_dram, pair_dram, ident, iota_row, ones, ones_bf, src_idx, dst_loc, pair_tile,
                x, W, att_src, att_dst, w_qkv, g_pre, gnn_beta, w_part, beta, xin, mv, acc, bank):
    full = E // GE
    rest = E - full * GE
    with ExitStack() as ctx:
        def sb(name, shape, dt=F32):
            return ctx.enter_context(nc.sbuf_tensor("pt_" + name, shape, dt))

        def sem(name):
            return ctx.enter_context(nc.semaphore(name))

        pad = sb("pad", [1, 4 * GE], I32)
        iota_i = sb("iota_i", [P, P], I32)
        part_i = sb("part_i", [P, 1], I32)
        part_f = sb("part_f", [P, 1])
        first_i = sb("first_i", [P, 2 * PC], I32)
        first_f = sb("first_f", [P, 2 * PC])
        start_i = sb("start_i", [P, T + 1], I32)
        start_f = sb("start_f", [P, T + 1])
        below = sb("below", [P, 2 * PC, T + 1], BF16)
        group_count = sb("group_count", [P, 2, T + 1])
        count = sb("count", [P, T])
        one_t = sb("one_t", [P, T])
        base = sb("base", [P, T + 1])
        shift = sb("shift", [P, T])
        step = sb("step", [P, T])
        pair_i = sb("pair_i", [P, PC], I32)
        pair_f = sb("pair_f", [P, PC])
        reached = sb("reached", [P, PC, T])
        product = sb("product", [P, PC, T])
        tile_f = sb("tile_f", [P, PC])
        tile_i = sb("tile_i", [P, PC], I32)
        tile_node = sb("tile_node", [P, PC])
        row_f = sb("row_f", [P, PC])
        row_i = sb("row_i", [P, PC], I32)
        group = sb("group", [P, PC, 2 * GE], I32)
        whole, taken, buffers = flat(acc[:]), 0, []
        for n, width in ((PC, 2 * GE), (2, QKV0 + 3 * MHID), (2, D), (4, D)):
            buffers.append(whole[:, taken:taken + n * width].rearrange("p (n w) -> p n w", n=n))
            taken += n * width
        group_f, w, att, att_w = buffers
        gp = sb("gp", [P, 2])
        bn = sb("bn", [P, SUP, 6])
        s_w, s_x = sem("s_w"), sem("s_x")
        s_group = [sem(f"s_group{c}") for c in range(PC)]
        s_iota, s_pad, s_edges, s_first = sem("s_iota"), sem("s_pad"), sem("s_edges"), sem("s_first")
        s_below, s_counts, s_row, s_table = (sem("s_below"), sem("s_counts"), sem("s_row"),
                                                      sem("s_table"))
        s_pt, s_gf, s_tr, s_idx, s_chain = sem("s_pt"), sem("s_gf"), sem("s_tr"), sem("s_idx"), sem("s_chain")
        block = ctx.enter_context(nc.Block())
        COPIES = 8

        @block.sync
        def _(sp):
            sp.dma_start(edges_dram[0:full, 0:GE], src[0:full * GE].rearrange("(r w) -> r w", w=GE)).then_inc(s_edges, 16)
            sp.dma_start(edges_dram[0:full, GE:2 * GE], dst[0:full * GE].rearrange("(r w) -> r w", w=GE)).then_inc(s_edges, 16)
            sp.dma_start(edges_dram[full:full + 1, 0:rest], src[full * GE:E].rearrange("(r w) -> r w", r=1)).then_inc(s_edges, 16)
            sp.dma_start(edges_dram[full:full + 1, GE:GE + rest], dst[full * GE:E].rearrange("(r w) -> r w", r=1)).then_inc(s_edges, 16)
            sp.wait_ge(s_pad, 2)
            sp.dma_start(edges_dram[full:full + 1, rest:GE], pad[0:1, 0:GE - rest]).then_inc(s_edges, 16)
            sp.dma_start(edges_dram[full:full + 1, GE + rest:2 * GE], pad[0:1, GE:2 * GE - rest]).then_inc(s_edges, 16)
            sp.dma_start(edges_dram[full + 1:full + 2, 0:GE], pad[0:1, 0:GE]).then_inc(s_edges, 16)
            sp.dma_start(edges_dram[full + 1:full + 2, GE:2 * GE], pad[0:1, GE:2 * GE]).then_inc(s_edges, 16)
            sp.wait_ge(s_table, 1)
            sp.dma_start(pair_dram.rearrange("(c p) -> p c", p=P), tile_i[:]).then_inc(s_pt, 16)
            sp.wait_ge(s_pt, 16)
            sp.dma_start(pair_tile[:], pair_dram.rearrange("(a j) -> a j", a=1)).then_inc(s_pt, 16)
            sp.wait_ge(s_pt, 32)
            sp.wait_ge(s_edges, 16 * COPIES)

        @block.scalar
        def _(act):
            act.wait_ge(s_pad, 3)
            for half, (offset, groups) in enumerate(((0, GR), (GE - 1, full))):
                whole = groups // P
                tail = groups - whole * P
                act.dma_start(first_i[:, half * PC:half * PC + whole],
                              dst[0:whole * P * GE].rearrange("(c p w) -> p c w", p=P, w=GE)[:, :, offset]
                              ).then_inc(s_first, 16)
                if offset:
                    tail_ap = dst[whole * P * GE:(whole * P + tail) * GE].rearrange("(p w) -> p w", w=GE)[:, offset:offset + 1]
                    act.dma_start(first_i[0:tail, half * PC + whole:half * PC + whole + 1], tail_ap).then_inc(s_first, 16)
                else:
                    tail_ap = dst[whole * P * GE:(whole * P + tail - 1) * GE].rearrange("(p w) -> p w", w=GE)[:, 0:1]
                    act.dma_start(first_i[0:tail - 1, whole:whole + 1], tail_ap).then_inc(s_first, 16)
                    act.dma_start(first_i[tail - 1:tail, whole:whole + 1],
                                  dst[full * GE:full * GE + 1].rearrange("(p w) -> p w", w=1)).then_inc(s_first, 16)
            act.dma_start(w[:, :, 0:D], W.rearrange("(k p) n -> p k n", p=P)).then_inc(s_w, 16)
            act.dma_start(w[:, :, QKV0:], w_qkv.rearrange("(k p) n -> p k n", p=P)).then_inc(s_w, 16)
            act.dma_start(gp[:], g_pre.rearrange("(k p) -> p k", p=P)).then_inc(s_w, 16)
            for a, v in enumerate((att_src, att_dst)):
                act.dma_start(att[:, a, :], v.rearrange("h c -> (h c)").partition_broadcast(P)).then_inc(s_w, 16)
            for b in range(2):
                act.dma_start(xin[:, b, :, :], x[b * SUP * P:(b + 1) * SUP * P, :].rearrange("(g p) d -> p g d", p=P)
                              ).then_inc(s_x, 16)
            act.dma_start(beta[:, 0, :], gnn_beta.partition_broadcast(P)).then_inc(s_x, 16)
            for c in range(PC):
                act.wait_ge(s_tr, c + 1)
                t = bank[c % 4]
                nc.scalar.copy(src_idx[:, c * P:(c + 1) * P], t[:, 0:GE])
                nc.scalar.activation(dst_loc[:, c * P:(c + 1) * P], t[:, GE:2 * GE], ACT.Copy, scale=-1.0
                                     ).then_inc(s_idx, 1)

        @block.gpsimd
        def _(pool):
            nc.gpsimd.iota(iota_i[:], pattern=[[1, P]], base=0, channel_multiplier=0)
            nc.gpsimd.iota(part_i[:], pattern=[[0, 1]], base=0, channel_multiplier=1)
            nc.gpsimd.iota(start_i[:], pattern=[[P, T + 1]], base=0, channel_multiplier=0)
            nc.gpsimd.iota(pair_i[:], pattern=[[P, PC]], base=0, channel_multiplier=1).then_inc(s_iota, 1)
            pool.wait_ge(s_row, 1)
            pool.wait_ge(s_edges, 16 * COPIES)
            for c in range(PC):
                nc.gpsimd.indirect_dma_start(out=group[:, c, :], out_offset=None, in_=edges_dram,
                                             in_offset=bass.IndirectOffsetOnAxis(ap=row_i[:, c:c + 1], axis=0)
                                             ).then_inc(s_group[c], 16)
            for c in range(PC):
                pool.wait_ge(s_group[c], 16)

        @block.vector
        def _(dve):
            links = [0]

            def link(ins):
                links[0] += 1
                ins.then_inc(s_chain, 1)
                dve.wait_ge(s_chain, links[0])

            nc.vector.memset(pad[:, 0:GE], 0).then_inc(s_pad, 1)
            nc.vector.memset(pad[:, GE:], NOWHERE).then_inc(s_pad, 1)
            nc.vector.memset(first_i[:], NOWHERE).then_inc(s_pad, 1)
            nc.vector.memset(ones[:], 1.0)
            nc.vector.memset(ones_bf[:], 1.0)
            nc.vector.memset(one_t[:], 1.0)
            nc.vector.memset(base[:, 0:1], 0.0)
            dve.wait_ge(s_iota, 1)
            nc.vector.tensor_copy(iota_row[:], iota_i[:])
            nc.vector.tensor_copy(pair_f[:], pair_i[:])
            nc.vector.tensor_copy(start_f[:], start_i[:])
            link(nc.vector.tensor_copy(part_f[:], part_i[:]))
            nc.vector.tensor_scalar(ident[:], iota_row[:], part_f[:, 0:1], None, ALU.is_equal)
            dve.wait_ge(s_first, 16 * 5)
            link(nc.vector.tensor_copy(first_f[:], first_i[:]))
            nc.vector.tensor_tensor(below[:], first_f[:].unsqueeze(2).to_broadcast([P, 2 * PC, T + 1]),
                                    start_f[:].unsqueeze(1).to_broadcast([P, 2 * PC, T + 1]), ALU.is_lt
                                    ).then_inc(s_below, 1)
            dve.wait_ge(s_counts, 1)
            link(nc.vector.tensor_copy(flat(group_count[:]), bank[0][:, 0:2 * (T + 1)]))
            begun, ended = group_count[:, 0, :], group_count[:, 1, :]
            link(nc.vector.tensor_tensor(count[:], begun[:, 1:T + 1], ended[:, 0:T], ALU.subtract))
            link(nc.vector.tensor_tensor_scan(base[:, 1:T + 1], one_t[:], count[:], 0.0, ALU.mult, ALU.add))
            link(nc.vector.tensor_tensor(shift[:], ended[:, 0:T], base[:, 0:T], ALU.subtract))
            link(nc.vector.tensor_copy(step[:, 0:1], shift[:, 0:1]))
            link(nc.vector.tensor_tensor(step[:, 1:T], shift[:, 1:T], shift[:, 0:T - 1], ALU.subtract))
            pairs = pair_f[:].unsqueeze(2).to_broadcast([P, PC, T])
            link(nc.vector.tensor_tensor(reached[:], base[:, 1:T + 1].unsqueeze(1).to_broadcast([P, PC, T]), pairs,
                                         ALU.is_le))
            link(nc.vector.tensor_reduce(tile_f[:], reached[:], X, ALU.add))
            link(nc.vector.tensor_scalar(tile_f[:], tile_f[:], float(T - 1), None, ALU.min))
            nc.vector.tensor_copy(tile_i[:], tile_f[:]).then_inc(s_table, 1)
            nc.vector.tensor_scalar(tile_node[:], tile_f[:], float(P), None, ALU.mult)
            link(nc.vector.tensor_tensor(reached[:], base[:, 0:T].unsqueeze(1).to_broadcast([P, PC, T]), pairs,
                                         ALU.is_le))
            link(nc.vector.tensor_tensor(product[:], reached[:], step[:].unsqueeze(1).to_broadcast([P, PC, T]),
                                         ALU.mult))
            link(nc.vector.tensor_reduce(row_f[:], product[:], X, ALU.add))
            link(nc.vector.tensor_tensor(row_f[:], row_f[:], pair_f[:], ALU.add))
            link(nc.vector.tensor_scalar(row_f[:], row_f[:], float(full + 1), 0.0, ALU.min, ALU.max))
            nc.vector.tensor_copy(row_i[:], row_f[:]).then_inc(s_row, 1)

            dve.wait_ge(s_w, 16 * 5)
            for k in range(2):
                for a in range(2):
                    done = nc.vector.tensor_tensor(att_w[:, 2 * k + a, :], w[:, k, 0:D], att[:, a, :], ALU.mult)
            link(done)
            for k in range(2):
                for a in range(2):
                    nc.vector.tensor_reduce(w[:, k, D + a * H:D + (a + 1) * H],
                                            att_w[:, 2 * k + a, :].rearrange("p (h c) -> p h c", c=C), X, ALU.add)
            for k in range(2):
                done = nc.vector.tensor_scalar(w[:, k, QKV0:], w[:, k, QKV0:], gp[:, k:k + 1], None, ALU.mult)
            link(done)
            link(nc.vector.tensor_copy(w_part[:, 0, :, :], w[:]))
            nc.vector.tensor_tensor(w_part[:, 1, :, :], w[:], w_part[:, 0, :, :].bitcast(F32), ALU.subtract)
            dve.wait_ge(s_x, 16 * 3)
            for g in range(SUP):
                done = nc.vector.bn_stats(bn[:, g, :], xin[:, 0, g, :])
            link(done)
            for g in range(SUP):
                done = nc.vector.bn_aggr(mv[:, 0, g, :], bn[:, g, :])
            for c in range(PC):
                dve.wait_ge(s_group[c], 16)
                nc.vector.tensor_copy(group_f[:, c, 0:GE], group[:, c, 0:GE])
                nc.vector.tensor_scalar(group_f[:, c, GE:], group[:, c, GE:], tile_node[:, c:c + 1], None,
                                        ALU.subtract).then_inc(s_gf, 1)

        @block.tensor
        def _(pe):
            pe.wait_ge(s_below, 1)
            for half in range(2):
                for c in range(PC):
                    last = nc.tensor.matmul(bank[0][:, half * (T + 1):(half + 1) * (T + 1)], ones_bf[:],
                                            below[:, half * PC + c, :], start=(c == 0), stop=(c == PC - 1))
            last.then_inc(s_counts, 1)
            for c in range(PC):
                pe.wait_ge(s_gf, c + 1)
                if c >= 4:
                    pe.wait_ge(s_idx, c - 3)
                for kind in range(2):
                    last = nc.tensor.transpose(bank[c % 4][:, kind * GE:(kind + 1) * GE],
                                               group_f[:, c, kind * GE:(kind + 1) * GE], ident[:])
                last.then_inc(s_tr, 1)


def project(nc, x, w_part, beta, xin, mv, xl_dram, base_dram, acc, node_logit, qkv, ident, bank):
    with ExitStack() as ctx:
        def sb(name, shape, dt=F32):
            return ctx.enter_context(nc.sbuf_tensor("pj_" + name, shape, dt))

        def sem(name):
            return ctx.enter_context(nc.semaphore(name))

        xn = sb("xn", [P, 2, SUP, D])
        xnT = sb("xnT", [P, SUP, 2, 2, P], F32R)
        bn = sb("bn", [P, 2, SUP, 6])
        rstd = sb("rstd", [P, 2, SUP])
        sumsq = sb("sumsq", [P, 2, SUP])
        rnorm = sb("rnorm", [P, 2, SUP])
        s_var, s_dev, s_squared, s_sum = (sem("pj_" + n) for n in ("var", "dev", "squared", "sum"))
        s_low, s_chain, s_xn, s_sq, s_rn, s_tp, s_xt, s_mm, s_xl, s_base, s_xls, s_fence = (
            sem(n) for n in ("s_low", "s_chain", "s_xn", "s_sq", "s_rn", "s_tp", "s_xt", "s_mm", "s_xl",
                             "s_base", "s_xls", "s_fence"))
        s_x = [sem("s_x_even"), sem("s_x_odd")]
        s_stored = [sem("s_stored_even"), sem("s_stored_odd")]
        block = ctx.enter_context(nc.Block())
        HIGH, LOW = 0, 1
        PARTS = ((LOW, HIGH), (HIGH, LOW), (HIGH, HIGH))
        A0 = 4
        LINKS = 6

        AHEAD = 2

        def ahead(i, b, g, rows):
            if g + AHEAD < SUP:
                return [(i, b, g + AHEAD)]
            return [(i + b, 1 - b, g + AHEAD - SUP)] if rows == P else []

        def supers(eng, body):
            last = (NS - 1) // 2
            with eng.Fori(0, last - 1) as i:
                for b in range(2):
                    body(i, b, P)
            for b in range(2):
                body(last - 1, b, P)
            body(last, 0, LAST)

        def node_rows(dram, s, rows):
            if rows == P:
                return [(dram[ds(s * (SUP * P), SUP * P), :].rearrange("(g p) d -> p g d", p=P), slice(0, SUP), P)]
            whole = s * SUP * P + (SUP - 1) * P
            return [(dram[s * SUP * P:whole, :].rearrange("(g p) d -> p g d", p=P), slice(0, SUP - 1), P),
                    (dram[whole:whole + rows, :].unsqueeze(1), slice(SUP - 1, SUP), rows)]

        @block.sync
        def _(sp):
            for b in range(2):
                sp.sem_inc(s_stored[b], 16)
                sp.sem_inc(s_x[b], 16)

            def load(i, b, rows):
                sp.wait_ge(s_stored[b], i * 16 + 16)
                for dram, g, r in node_rows(x, i * 2 + b, rows):
                    sp.dma_start(xin[0:r, b, g, :], dram).then_inc(s_x[b], 16)

            def store_base(i, b, rows):
                s = i * 2 + b
                sp.wait_ge(s_base, s + 1)
                for dram, g, r in node_rows(base_dram, s, rows):
                    sp.dma_start(dram, xin[0:r, b, g, :]).then_inc(s_stored[b], 16)

            def store_xl(i, b, rows):
                s = i * 2 + b
                for dram, g, r in node_rows(xl_dram, s, rows):
                    sp.wait_ge(s_xl, s * SUP + (g.stop + 2))
                    sp.dma_start(dram, acc[0:r, ds(s * SUP + g.start, g.stop - g.start), :]).then_inc(s_xls, 16)

            last = (NS - 1) // 2
            with sp.Fori(0, last - 1) as i:
                for b in range(2):
                    store_base(i, b, P)
                    load(i + 1, b, P)
                    store_xl(i, b, P)
            store_base(last - 1, 0, P)
            load(last, 0, LAST)
            store_xl(last - 1, 0, P)
            store_base(last - 1, 1, P)
            store_xl(last - 1, 1, P)
            store_base(last, 0, LAST)
            store_xl(last, 0, LAST)
            sp.wait_ge(s_stored[0], 16 + 16 * (last + 2))
            sp.wait_ge(s_stored[1], 16 + 16 * last)
            sp.wait_ge(s_xls, 16 * (NS + 1))

        @block.gpsimd
        def _(pool):
            def body(i, b, rows):
                s = i * 2 + b
                pool.wait_ge(s_xn, s + 1)
                pool.sem_inc(s_fence, 1)
                nc.gpsimd.tensor_tensor(flat(xin[:, b, :, :]), flat(xin[:, b, :, :]), flat(xn[:, b, :, :]),
                                        ALU.add).then_inc(s_sum, 1)
                pool.wait_ge(s_sum, s + 1)
                pool.sem_inc(s_fence, 1)
                nc.gpsimd.tensor_tensor(xin[:, b, :, :], xin[:, b, :, :], beta[:].to_broadcast([P, SUP, D]), ALU.add
                                        ).then_inc(s_base, 1)
            supers(pool, body)

        @block.vector
        def _(dve):
            links = [0]

            def link(ins, s=None):
                links[0] += 1
                ins.then_inc(s_chain, 1)
                dve.wait_ge(s_chain, links[0] if s is None else s * LINKS + (A0 + links[0]))

            nc.vector.memset(qkv[:, :, 3 * MHID:], 1.0)

            def variance_of(i, b, full, tiles):
                if tiles.start == 0:
                    dve.wait_ge(s_x[b], i * 16 + (16 if full else 32))
                for g in range(tiles.start, tiles.stop):
                    last = nc.vector.bn_stats(bn[:, b, g, :], xin[:, b, g, :])
                return last

            def variance(i, b, s_at):
                if s_at is not None:
                    dve.sem_inc(s_fence, 1)
                    for g in range(SUP):
                        last = nc.vector.bn_aggr(mv[:, b, g, :], bn[:, b, g, :])
                    link(last, s_at)
                nc.vector.tensor_scalar(rstd[:, b, :], mv[:, b, :, 1], LN_EPS, None, ALU.add).then_inc(s_var, 1)

            def scales(i, b, s_at=None):
                dve.wait_ge(s_dev, i * 2 + b + 1)
                link(nc.vector.reciprocal(rstd[:, b, :], rstd[:, b, :]), s_at)
                link(nc.vector.scalar_tensor_tensor(out=sumsq[:, b, :], in0=mv[:, b, :, 1], scalar=float(D),
                                                    in1=rstd[:, b, :], op0=ALU.mult, op1=ALU.mult), s_at)
                nc.vector.tensor_tensor(sumsq[:, b, :], sumsq[:, b, :], rstd[:, b, :], ALU.mult).then_inc(s_squared, 1)

            def norms(i, b, s_at=None):
                dve.wait_ge(s_sq, i * 2 + b + 1)
                link(nc.vector.tensor_scalar(rnorm[:, b, :], sumsq[:, b, :], 1e-12, None, ALU.max), s_at)
                link(nc.vector.reciprocal(rnorm[:, b, :], rnorm[:, b, :]), s_at)
                nc.vector.tensor_scalar(rnorm[:, b, :], rnorm[:, b, :], float(D) ** 0.5, None, ALU.mult
                                        ).then_inc(s_rn, 1)

            def normalize(b, tiles):
                for g in range(tiles.start, tiles.stop):
                    last = nc.vector.tensor_scalar(xn[:, b, g, :], xin[:, b, g, :], mv[:, b, g, 0:1],
                                                   rstd[:, b, g:g + 1], ALU.subtract, ALU.mult)
                return last

            first, rest = slice(0, 4), slice(4, SUP)
            variance(0, 0, None)
            scales(0, 0)
            normalize(0, slice(0, SUP)).then_inc(s_xn, 1)
            norms(0, 0)
            assert links[0] == A0

            def body(i, b, rows):
                s = i * 2 + b
                links[0] = 0
                n = (i + b, 1 - b)
                for g in range(SUP):
                    a = (b + g) % 2
                    dve.wait_ge(s_xt, s * SUP + (g + 1))
                    nc.vector.tensor_tensor(flat(xnT[:, g, LOW, :, :]), bank[a][:, 0:2 * P],
                                            flat(xnT[:, g, HIGH, :, :]).bitcast(F32), ALU.subtract).then_inc(s_low, 1)
                    if rows != P:
                        continue
                    if g == 0:
                        variance_of(*n, not (isinstance(i, int) and b == 1), first)
                    if g == 1:
                        link(variance_of(*n, True, rest), s)
                    if g == 2:
                        variance(*n, s)
                    if g == 3:
                        scales(*n, s)
                        normalize(n[1], first)
                    if g == 4:
                        normalize(n[1], rest).then_inc(s_xn, 1)
                    if g == 5:
                        norms(*n, s)
            supers(dve, body)

        @block.tensor
        def _(pe):
            pe.sem_inc(s_low, 2)
            pe.sem_inc(s_xl, 2)

            def transposes(i, b, g):
                s = i * 2 + b
                t = bank[(b + g) % 2]
                pe.wait_ge(s_xn, s + 1)
                pe.wait_ge(s_low, s * SUP + (g + 1))
                for k in range(2):
                    last = nc.tensor.transpose(t[:, k * P:(k + 1) * P], xn[:, b, g, k * P:(k + 1) * P], ident[:])
                last.then_inc(s_tp, 1)

            for g in range(AHEAD):
                transposes(0, 0, g)

            def body(i, b, rows):
                s = i * 2 + b
                for g in range(SUP):
                    a = (b + g) % 2
                    for tile in ahead(i, b, g, rows):
                        transposes(*tile)
                    pe.wait_ge(s_low, s * SUP + (g + 3))
                    pe.wait_ge(s_xl, s * SUP + (g + 1))
                    for out, columns in ((bank[2 + a], slice(0, QKV0)), (bank[4 + a], slice(QKV0, QKV0 + 3 * MHID))):
                        for k in range(2):
                            for m, (xp, wp) in enumerate(PARTS):
                                last = nc.tensor.matmul(out[:, 0:columns.stop - columns.start], xnT[:, g, xp, k, :],
                                                        w_part[:, wp, k, columns], start=(k == 0 and m == 0),
                                                        stop=(k == 1 and m == 2))
                    last.then_inc(s_mm, 1)
            supers(pe, body)

        @block.scalar
        def _(act):
            def deviations(i, b):
                act.wait_ge(s_var, i * 2 + b + 1)
                nc.scalar.activation(rstd[:, b, :], rstd[:, b, :], ACT.Sqrt).then_inc(s_dev, 1)

            def norms(i, b):
                act.wait_ge(s_squared, i * 2 + b + 1)
                nc.scalar.activation(sumsq[:, b, :], sumsq[:, b, :], ACT.Sqrt).then_inc(s_sq, 1)

            def copy_xnT(i, b, g):
                act.wait_ge(s_tp, (i * 2 + b) * SUP + (g + 1))
                nc.scalar.copy(flat(xnT[:, g, HIGH, :, :]), bank[(b + g) % 2][:, 0:2 * P]).then_inc(s_xt, 1)

            deviations(0, 0)
            norms(0, 0)
            for g in range(AHEAD):
                copy_xnT(0, 0, g)

            def body(i, b, rows):
                s = i * 2 + b
                for g in range(SUP):
                    for tile in ahead(i, b, g, rows):
                        copy_xnT(*tile)
                    if g == 0:
                        act.wait_ge(s_rn, s + 1)
                    if g == 2 and rows == P:
                        deviations(i + b, 1 - b)
                    if g == 4 and rows == P:
                        norms(i + b, 1 - b)
                    act.wait_ge(s_mm, s * SUP + (g + 1))
                    a = (b + g) % 2
                    nc.scalar.copy(acc[:, ds(s * SUP + g, 1), :].rearrange("p a d -> p (a d)"),
                                   bank[2 + a][:, 0:ROW])
                    nc.scalar.copy(node_logit[:, ds(s * SUP + g, 1), 0:H].rearrange("p a h -> p (a h)"),
                                   bank[2 + a][:, ROW:ROW + H])
                    nc.scalar.activation(qkv[:, ds(s * SUP + g, 1), 0:3 * MHID].rearrange("p a d -> p (a d)"),
                                         bank[4 + a][:, 0:3 * MHID], ACT.Copy, scale=rnorm[:, b, g:g + 1]
                                         ).then_inc(s_xl, 1)
            supers(act, body)


def edge_phase(nc, mem_kv, w_out, b_out, g_out, xl_dram, base_dram, acc, node_logit, qkv, src_idx, dst_loc,
               pair_tile, ident, iota_row, ones, bank):
    with ExitStack() as ctx:
        def sb(name, shape, dt=F32):
            return ctx.enter_context(nc.sbuf_tensor("ed_" + name, shape, dt))

        def sem(name):
            return ctx.enter_context(nc.semaphore("e_" + name))

        rows = sb("rows", [P, U * 4, ROW])
        hot = sb("hot", [P, U, 4, P])
        hotT = sb("hotT", [P, U, 4 * P])
        apart = sb("apart", [P, 4, P])
        idx = sb("idx", [P, U * 4], I32)
        logit = sb("logit", [P, 2, 4, H])
        s_rows = [sem(f"rows{u}") for u in range(U)]
        (s_idx, s_hot, s_tr, s_hotT, s_node, s_logit, s_exp, s_scaled, s_sum, s_added, s_chain, s_fence) = (
            sem(n) for n in ("idx", "hot", "tr", "hotT", "node", "logit", "exp", "scaled", "sum", "added", "chain",
                             "fence"))

        s_apart = sem("apart")

        top_logit = sb("top_logit", [P, H])
        top_col = sb("top_col", [P, 1])
        self_z = sb("self_z", [P, T, H])
        s_lmax, s_ltp, s_lcol, s_lbc, s_bound, s_self, s_self_w = (
            sem(n) for n in ("lmax", "ltp", "lcol", "lbc", "bound", "self", "self_w"))

        mem = sb("mem", [P, 2, NMEM])
        mem_k = sb("mem_k", [NMEM, P])
        mem_v = sb("mem_v", [NMEM, MHID + 1])
        mem_e = sb("mem_e", [P, NMEM])
        wout = sb("wout", [P, D])
        bout = sb("bout", [1, D])
        gout = sb("gout", [P, D])
        top_keys = sb("top_keys", [P, 4, MHID])
        top_key = sb("top_key", [P, MHID])
        kcol = sb("kcol", [P, 3])
        key_max = sb("key_max", [P, MHID])
        key_exp = sb("key_exp", [P, SUP, MHID])
        qmax = sb("qmax", [P, SUP, MH])
        qsum = sb("qsum", [P, SUP, MH])
        ctx_n = sb("ctx_n", [P, MHID])
        ctx_b = sb("ctx_b", [P, MHID])
        ctx_t = sb("ctx_t", [P, MHID])
        rden = sb("rden", [P, 1])
        mix_w = sb("mix_w", [P, D])
        q_two = sb("q_two", [P, 2, MHID])
        qT = sb("qT", [P, 2 * P])
        junk = sb("junk", [P, 2, D])
        sumsq = sb("sumsq", [P, T])
        base = sb("base", [P, 2, D])
        (s_in, s_kmax, s_ktp, s_kcol, s_kneg, s_kbc, s_kready, s_meme, s_memt, s_mem, s_side) = (
            sem(n) for n in ("in", "kmax", "ktp", "kcol", "kneg", "kbc", "kready", "meme", "memt", "mem", "side"))
        (s_kd, s_ke, s_kfree, s_ctx, s_qd, s_qe, s_qchain, s_qs, s_ctxn, s_ctxt, s_ctxT, s_mw, s_wd) = (
            sem(n) for n in ("kd", "ke", "kfree", "ctx", "qd", "qe", "qchain", "qs", "ctxn", "ctxt", "ctxT", "mw",
                             "wd"))
        (s_mq, s_mt, s_mqT, s_mo, s_mread, s_msq, s_rm, s_radd) = (
            sem(n) for n in ("mq", "mt", "mqT", "mo", "mread", "msq", "rm", "radd"))
        s_base = sem("base")
        keys = qkv[:, :, MHID:2 * MHID]

        TURNS = QUADS // U
        LINKS = 3
        TWOS = T // 2
        segments, at = [], 0
        for kind, turns in (("self loops", 1), ("more self loops", 1), ("last self loops", 1), ("key parts", 1), ("more key parts", 1), ("key maximum", 1), ("keys", NS - 1), ("last keys", 1), ("query maxima", NS), ("queries", NS), ("context", 1),
                            ("mix", TWOS), ("last mix", 1), ("norms", 1), ("rest", TWOS), ("last rest", 1)):
            segments.append((kind, at, turns))
            at += turns
        segments.append(("", at, TURNS - 1 - at))
        block = ctx.enter_context(nc.Block())

        def run(eng, turn):
            for kind, first, turns in segments:
                if turns == 1:
                    turn(first, kind, 0)
                else:
                    with eng.Fori(first, first + turns) as i:
                        turn(i, kind, i - first)
            turn(TURNS - 1, "", 0, True)

        def tiles_of(which, at):
            _, values = nc.values_load_multi_w_load_instructions(
                pair_tile[0:1, ds(at, 8)], engines=(which,), min_val=0, max_val=T - 1,
                skip_runtime_bounds_check_because="pair_tables clamps the tiles")
            return values

        @block.sync
        def _(sp):
            sp.dma_start(mem[:], mem_kv.rearrange("a h d m -> (h d) a m")).then_inc(s_in, 16)
            sp.dma_start(wout[:], w_out).then_inc(s_in, 16)
            sp.dma_start(bout[:], b_out.rearrange("(a d) -> a d", a=1)).then_inc(s_in, 16)
            sp.dma_start(gout[:], g_out.partition_broadcast(P)).then_inc(s_in, 16)
            sp.sem_inc(s_radd, 1)
            with sp.Fori(0, TWOS) as j:
                sp.wait_ge(s_radd, j + 1)
                sp.dma_start(base[:], base_dram[ds(j * (2 * P), 2 * P), :].rearrange("(g p) d -> p g d", p=P)
                             ).then_inc(s_base, 16)
            sp.wait_ge(s_radd, TWOS + 1)
            sp.dma_start(base[0:LAST, 0, :], base_dram[(T - 1) * P:N, :]).then_inc(s_base, 16)

        @block.gpsimd
        def _(pool):
            def gather(u):
                for k in range(4):
                    m = 4 * u + k
                    nc.gpsimd.indirect_dma_start(out=rows[:, m, :], out_offset=None, in_=xl_dram,
                                                 in_offset=bass.IndirectOffsetOnAxis(ap=idx[:, m:m + 1], axis=0)
                                                 ).then_inc(s_rows[u], 16)

            pool.wait_ge(s_idx, U)
            for u in range(U):
                gather(u)
            with pool.Fori(0, TURNS - 1) as i:
                for u in range(U):
                    q = i * U + u
                    pool.wait_ge(s_sum, q * 4 + 4)
                    pool.wait_ge(s_idx, q + (U + 1))
                    pool.sem_inc(s_fence, 1)
                    gather(u)

        @block.scalar
        def _(act):
            def side(kind, j, u):
                if kind == "key maximum" and u == 2:
                    act.wait_ge(s_kneg, 1)
                    nc.scalar.activation(mem_e[:], mem[:, 0, :], ACT.Exp, bias=kcol[:, 2:3]).then_inc(s_meme, 1)
                elif kind in ("keys", "last keys") and u == 1:
                    j = j if kind == "keys" else NS - 1
                    act.wait_ge(s_kd, j + 1)
                    act.wait_ge(s_kfree, j + 1)
                    nc.scalar.activation(key_exp[:], keys[:, ds(j * SUP, SUP), :], ACT.Exp).then_inc(s_ke, 1)
                elif kind == "query maxima" and u == 2:
                    act.wait_ge(s_qd, j + 2)
                    q = qkv[:, ds(j * SUP, SUP), 0:MHID]
                    nc.scalar.activation(q, q, ACT.Exp).then_inc(s_qe, 1)
                elif kind in ("mix", "last mix"):
                    j, n = (j, 2) if kind == "mix" else (TWOS, 1)
                    if u == 0:
                        nc.scalar.copy(q_two[:, 0:n, :], qkv[:, ds(j * 2, n), 0:MHID]).then_inc(s_mq, 1)
                    elif u == 1:
                        act.wait_ge(s_mt, j + 1)
                        nc.scalar.copy(qT[:, 0:n * P], bank[6][:, 0:n * P]).then_inc(s_mqT, 1)
                    elif u == 3:
                        act.wait_ge(s_mo, j + 1)
                        act.wait_ge(s_mread, j + 1)
                        for g in range(n):
                            nc.scalar.activation(junk[:, g, :], bank[7][:, g * D:(g + 1) * D], ACT.Square,
                                                 accum_out=sumsq[:, ds(j * 2 + g, 1)])
                        nc.scalar.copy(qkv[:, ds(j * 2, n), MHID:3 * MHID],
                                       bank[7][:, 0:n * D].rearrange("p (g d) -> p g d", d=D)).then_inc(s_mread, 1)
                elif kind == "norms" and u == 0:
                    act.wait_ge(s_mread, TWOS + 2)
                    nc.scalar.activation(sumsq[:], sumsq[:], ACT.Sqrt).then_inc(s_msq, 1)

            def copy_indices(q, u):
                nc.scalar.copy(idx[:, 4 * u:4 * u + 4],
                               src_idx[:, ds(q * 4, 4)]).then_inc(s_idx, 1)

            def copy_hotT(q, u):
                act.wait_ge(s_tr, q + 1)
                nc.scalar.copy(hotT[:, u, :], bank[2 + u % 2][:]).then_inc(s_hotT, 1)

            def exps(q, u):
                act.wait_ge(s_logit, q + 1)
                nc.scalar.activation(rows[:, 4 * u:4 * u + 4, D:ROW], logit[:, u % 2, :, :], ACT.Exp
                                     ).then_inc(s_exp, 1)

            def one_hots(q, u):
                if not (isinstance(q, int) and q == 0):
                    act.wait_ge(s_hot, q)
                for k in range(4):
                    done = nc.scalar.activation(apart[:, k, :], iota_row[:], ACT.Square,
                                                bias=dst_loc[:, ds(q * 4 + k, 1)])
                done.then_inc(s_apart, 1)
                act.wait_ge(s_apart, q + 1)
                nc.scalar.activation(hot[:, u, :, :], apart[:], ACT.Relu, bias=1.0, scale=-1.0).then_inc(s_hot, 1)

            act.sem_inc(s_mread, 1)
            for u in range(U):
                copy_indices(u, u)
            for u in range(2):
                one_hots(u, u)
            copy_hotT(0, 0)
            act.wait_ge(s_self, 1)
            nc.scalar.activation(acc[:, :, D:ROW], self_z[:], ACT.Exp).then_inc(s_self_w, 1)
            one_hots(2, 2)
            for u in range(1, 3):
                copy_hotT(u, u)
            exps(0, 0)

            def turn(i, kind, j, last=False):
                for u in range(U):
                    q = i * U + u
                    if not last:
                        copy_indices(q + U, u)
                    if not (last and u > 0):
                        if not (kind == "self loops" and u == 0):
                            act.wait_ge(s_sum, q * 4)
                        one_hots(q + 3, (u + 3) % U)
                    if not (last and u == U - 1):
                        exps(q + 1, (u + 1) % U)
                    if not (last and u > 0):
                        copy_hotT(q + 3, (u + 3) % U)
                    side(kind, j, u)

            run(act, turn)

        @block.vector
        def _(dve):
            V = nc.vector
            links = [0]
            side_links = [0]

            def link(ins, i):
                links[0] += 1
                ins.then_inc(s_chain, 1)
                return i * (LINKS * U) + (LINKS + links[0])

            def then(ins):
                side_links[0] += 1
                ins.then_inc(s_side, 1)
                dve.wait_ge(s_side, side_links[0])

            SELF = list(range(0, 4 * (T // 4), 4)) + [T]
            QUARTER = (T - 1) // 4

            def scale_self(n):
                part = acc[:, SELF[n]:SELF[n + 1], :]
                f = part[:, :, 0:D].rearrange("p t (h c) -> p t h c", c=C)
                then(V.tensor_tensor(f, f, part[:, :, D:ROW].unsqueeze(3).to_broadcast(
                    [P, SELF[n + 1] - SELF[n], H, C]), ALU.mult))

            def side(kind, j, u):
                if kind in ("self loops", "more self loops", "last self loops"):
                    n = 1 + u + U * ("self loops", "more self loops", "last self loops").index(kind)
                    if n < len(SELF) - 1:
                        scale_self(n)
                elif kind in ("key parts", "more key parts"):
                    if u % 2 == 0:
                        n = u // 2 + (2 if kind == "more key parts" else 0)
                        part = keys[:, n * QUARTER:(n + 1) * QUARTER, :]
                        then(V.tensor_reduce(top_keys[:, n, :], part.rearrange("p t d -> p d t"), X, ALU.max))
                elif kind == "key maximum":
                    if u == 0:
                        then(V.tensor_reduce(top_key[:], top_keys[:].rearrange("p t d -> p d t"), X, ALU.max))
                        V.tensor_tensor(top_key[0:LAST, :], top_key[0:LAST, :], keys[0:LAST, T - 1, :], ALU.max
                                        ).then_inc(s_kmax, 1)
                    elif u == 1:
                        dve.wait_ge(s_ktp, 1)
                        V.tensor_reduce(kcol[:, 0:1], bank[6][:, 0:P], X, ALU.max)
                        dve.wait_ge(s_in, 64)
                        then(V.tensor_reduce(kcol[:, 1:2], mem[:, 0, :], X, ALU.max))
                        V.tensor_tensor(kcol[:, 1:2], kcol[:, 0:1], kcol[:, 1:2], ALU.max).then_inc(s_kcol, 1)
                        dve.wait_ge(s_kcol, 1)
                        V.tensor_scalar(kcol[:, 2:3], kcol[:, 1:2], -1.0, None, ALU.mult).then_inc(s_kneg, 1)
                    elif u == 2:
                        dve.wait_ge(s_kbc, 1)
                        V.tensor_copy(key_max[:], bank[7][:, 0:P]).then_inc(s_kready, 1)
                    else:
                        dve.wait_ge(s_memt, 1)
                        V.tensor_copy(mem_k[:], bank[6][0:NMEM, 0:P])
                        V.tensor_copy(mem_v[:, 0:MHID], bank[6][0:NMEM, P:2 * P]).then_inc(s_mem, 1)
                elif kind in ("keys", "last keys") and u == 0:
                    k = keys[:, ds((j if kind == "keys" else NS - 1) * SUP, SUP), :]
                    dve.wait_ge(s_kready, 1)
                    V.tensor_tensor(k, k, key_max[:].unsqueeze(1).to_broadcast([P, SUP, MHID]), ALU.subtract
                                    ).then_inc(s_kd, 1)
                elif kind in ("query maxima", "queries"):
                    q = qkv[:, ds(j * SUP, SUP), 0:MHID].rearrange("p t (h d) -> p t h d", d=MD)
                    wide = [P, SUP, MH, MD]
                    if kind == "query maxima" and u == 0:
                        dve.wait_ge(s_qd, j + 1)
                        dve.sem_inc(s_fence, 1)
                        V.tensor_reduce(qmax[:], q, X, ALU.max).then_inc(s_qchain, 1)
                    elif kind == "query maxima" and u == 1:
                        dve.wait_ge(s_qchain, j + 1)
                        V.tensor_tensor(q, q, qmax[:].unsqueeze(3).to_broadcast(wide), ALU.subtract
                                        ).then_inc(s_qd, 1)
                    elif kind == "queries" and u == 0:
                        dve.wait_ge(s_qe, j + 1)
                        dve.wait_ge(s_qs, j + 1)
                        dve.sem_inc(s_fence, 1)
                        V.tensor_reduce(qsum[:], q, X, ALU.add).then_inc(s_qchain, 1)
                    elif kind == "queries" and u == 1:
                        dve.wait_ge(s_qchain, j * 2 + (NS + 1))
                        V.reciprocal(qsum[:], qsum[:]).then_inc(s_qchain, 1)
                    elif kind == "queries" and u == 2:
                        dve.wait_ge(s_qchain, j * 2 + (NS + 2))
                        V.tensor_tensor(q, q, qsum[:].unsqueeze(3).to_broadcast(wide), ALU.mult).then_inc(s_qs, 1)
                elif kind == "context":
                    if u == 0:
                        dve.wait_ge(s_ctx, 1)
                        then(V.reciprocal(rden[:], bank[6][:, MHID:MHID + 1]))
                        then(V.tensor_scalar(ctx_n[:], bank[6][:, 0:MHID], rden[:, 0:1], float(MD) ** -0.5, ALU.mult,
                                             ALU.mult))
                        for h in range(MH):
                            blk = slice(h * MD, (h + 1) * MD)
                            done = V.tensor_copy(ctx_b[blk, blk], ctx_n[blk, blk])
                        done.then_inc(s_ctxn, 1)
                    elif u == 1:
                        dve.wait_ge(s_ctxt, 1)
                        V.tensor_copy(ctx_t[:], bank[7][:, 0:P]).then_inc(s_ctxT, 1)
                    elif u == 3:
                        dve.wait_ge(s_mw, 1)
                        V.tensor_copy(mix_w[:], bank[6][:, 0:D]).then_inc(s_wd, 1)
                elif kind == "norms" and u == 1:
                    dve.wait_ge(s_msq, 1)
                    then(V.tensor_scalar(sumsq[:], sumsq[:], 1e-12, None, ALU.max))
                    then(V.reciprocal(sumsq[:], sumsq[:]))
                    then(V.tensor_scalar(sumsq[:], sumsq[:], float(D) ** 0.5, None, ALU.mult))
                elif kind in ("rest", "last rest"):
                    j, n = (j, 2) if kind == "rest" else (TWOS, 1)
                    if u == 0:
                        for g in range(n):
                            o = qkv[:, ds(j * 2 + g, 1), MHID:3 * MHID].rearrange("p a d -> p (a d)")
                            done = V.scalar_tensor_tensor(out=o, in0=o, scalar=sumsq[:, ds(j * 2 + g, 1)], in1=gout[:],
                                                          op0=ALU.mult, op1=ALU.mult)
                        done.then_inc(s_rm, 1)
                    elif u == 2:
                        dve.wait_ge(s_rm, j + 1)
                        rest = qkv[:, ds(j * 2, n), MHID:3 * MHID]
                        dve.wait_ge(s_base, j * 16 + 16)
                        V.tensor_tensor(rest, rest, base[:, 0:n, :], ALU.add).then_inc(s_radd, 1)

            def edge_logits(i, turn, q, u, between):
                own = bank[4 + u % 2][:, 0:8 * H].rearrange("p (k h) -> p k h", k=4)
                z = logit[:, u % 2, :, :]
                dve.wait_ge(s_rows[u], turn * 64 + 64)
                dve.wait_ge(s_node, q + 1)
                at = link(V.tensor_tensor(z, rows[:, 4 * u:4 * u + 4, D:ROW], own[:, :, 0:H], ALU.add), i)
                between(0)
                dve.wait_ge(s_chain, at)
                at = link(V.scalar_tensor_tensor(out=z, in0=z, scalar=SLOPE, in1=z, op0=ALU.mult, op1=ALU.max), i)
                between(1)
                dve.wait_ge(s_chain, at)
                at = link(V.tensor_tensor(z, z, own[:, :, H:], ALU.subtract), i)
                between(2)
                dve.wait_ge(s_chain, at)
                V.tensor_scalar(z, z, 0.0, None, ALU.min).then_inc(s_logit, 1)

            def scale(q, u, a):
                r = rows[:, 4 * u + 2 * a:4 * u + 2 * a + 2, :]
                f = r[:, :, 0:D].rearrange("p k (h c) -> p k h c", c=C)
                V.tensor_tensor(f, f, r[:, :, D:ROW].unsqueeze(3).to_broadcast([P, 2, H, C]), ALU.mult
                                ).then_inc(s_scaled, 1)

            def add(q, m, tile):
                dve.wait_ge(s_sum, q * 4 + (m + 1))
                dve.wait_ge(s_added, q * 4 + (m + 2))
                into = acc[:, ds(tile, 1), :].rearrange("p a d -> p (a d)")
                V.tensor_tensor(into, into, bank[m % 2][:, 0:ROW], ALU.add).then_inc(s_added, 1)

            then(V.tensor_reduce(top_logit[:], acc[:, 0:T - 1, D:ROW].rearrange("p t h -> p h t"), X, ALU.max))
            V.tensor_tensor(top_logit[0:LAST, :], top_logit[0:LAST, :], acc[0:LAST, T - 1, D:ROW], ALU.max
                            ).then_inc(s_lmax, 1)
            own_logit, bound = node_logit[:, :, 0:H], node_logit[:, :, H:]
            then(V.tensor_tensor(self_z[:], acc[:, :, D:ROW], own_logit, ALU.add))
            then(V.scalar_tensor_tensor(out=self_z[:], in0=self_z[:], scalar=SLOPE, in1=self_z[:], op0=ALU.mult,
                                        op1=ALU.max))
            dve.wait_ge(s_ltp, 1)
            V.tensor_reduce(top_col[0:H, :], bank[6][0:H, 0:P], X, ALU.max).then_inc(s_lcol, 1)
            dve.wait_ge(s_lbc, 1)
            then(V.tensor_tensor(bound, own_logit, bank[6][:, 0:H].unsqueeze(1).to_broadcast([P, T, H]), ALU.add))
            then(V.scalar_tensor_tensor(out=bound, in0=bound, scalar=SLOPE, in1=bound, op0=ALU.mult, op1=ALU.max))
            dve.sem_inc(s_bound, 1)
            then(V.tensor_tensor(self_z[:], self_z[:], bound, ALU.subtract))
            V.tensor_scalar(self_z[:], self_z[:], 0.0, None, ALU.min).then_inc(s_self, 1)
            V.memset(ctx_b[:], 0.0)
            then(V.memset(mem_v[:, MHID:], 1.0))
            dve.sem_inc(s_qs, 1)
            dve.sem_inc(s_qd, 1)
            dve.sem_inc(s_added, 2)
            links[0] = -LINKS
            edge_logits(0, 0, 0, 0, lambda n: None)
            dve.wait_ge(s_self_w, 1)
            scale_self(0)

            def turn(i, kind, j, last=False):
                links[0] = 0
                begin = kind == "self loops"
                for u in range(U):
                    q = i * U + u
                    end = last and u == U - 1
                    if u % 2 == 0:
                        first = begin and u == 0
                        tiles = tiles_of(DVE, 0 if first else i * (4 * U) + (4 * u - 2))
                    at = 4 * (u % 2) - (2 if first else 0)

                    def add_last(m):
                        if not (first and u == 0):
                            add(q - 1, m, tiles[at + m - 2])

                    def between(n):
                        if n == 0:
                            add_last(2)
                        elif n == 1:
                            add_last(3)
                            scale(q, u, 1)
                        else:
                            add(q, 0, tiles[at + 2])

                    dve.wait_ge(s_exp, q + 1)
                    scale(q, u, 0)
                    if end:
                        for n in range(3):
                            between(n)
                    else:
                        edge_logits(i, i + (u + 1) // U, q + 1, (u + 1) % U, between)
                    add(q, 1, tiles[at + 3])
                    side(kind, j, u)
                if last:
                    tiles = tiles_of(DVE, (QUADS - 1) * 4)
                    for m in (2, 3):
                        add(QUADS - 1, m, tiles[m])

            run(dve, turn)

        @block.tensor
        def _(pe):
            def side(kind, j, u):
                if kind == "key maximum":
                    if u == 0:
                        pe.wait_ge(s_kmax, 1)
                        nc.tensor.transpose(bank[6][:, 0:P], top_key[:], ident[:]).then_inc(s_ktp, 1)
                    elif u == 1:
                        pe.wait_ge(s_kcol, 1)
                        nc.tensor.matmul(bank[7][:, 0:P], kcol[:, 1:2].to_broadcast([P, P]), ident[:], start=True,
                                         stop=True).then_inc(s_kbc, 1)
                    elif u == 2:
                        pe.wait_ge(s_meme, 1)
                        nc.tensor.transpose(bank[6][0:NMEM, 0:P], mem_e[:], ident[:])
                        nc.tensor.transpose(bank[6][0:NMEM, P:2 * P], mem[:, 1, :], ident[:]).then_inc(s_memt, 1)
                    else:
                        pe.wait_ge(s_mem, 1)
                        nc.tensor.matmul(bank[6][:, 0:MHID + 1], mem_k[:], mem_v[:], start=True, stop=False)
                        pe.sem_inc(s_kfree, 1)
                elif kind in ("keys", "last keys") and u == 2:
                    end = kind == "last keys"
                    j = NS - 1 if end else j
                    pe.wait_ge(s_ke, j + 1)
                    for g in range(SUP):
                        r = LAST if end and g == SUP - 1 else P
                        done = nc.tensor.matmul(bank[6][:, 0:MHID + 1], key_exp[0:r, g, :],
                                                qkv[0:r, ds(j * SUP + g, 1), 2 * MHID:].rearrange("p a d -> p (a d)"),
                                                start=False, stop=end and g == SUP - 1)
                    done.then_inc(s_ctx if end else s_kfree, 1)
                elif kind == "context":
                    if u == 0:
                        pe.wait_ge(s_ctxn, 1)
                        nc.tensor.transpose(bank[7][:, 0:P], ctx_b[:], ident[:]).then_inc(s_ctxt, 1)
                    elif u == 2:
                        pe.wait_ge(s_ctxT, 1)
                        nc.tensor.matmul(bank[6][:, 0:D], ctx_t[:], wout[:], start=True, stop=True).then_inc(s_mw, 1)
                elif kind in ("mix", "last mix"):
                    j, n = (j, 2) if kind == "mix" else (TWOS, 1)
                    if u == 0:
                        pe.wait_ge(s_wd, 1)
                        pe.wait_ge(s_mq, j + 1)
                        for g in range(n):
                            done = nc.tensor.transpose(bank[6][:, g * P:(g + 1) * P], q_two[:, g, :], ident[:])
                        done.then_inc(s_mt, 1)
                    elif u == 2:
                        pe.wait_ge(s_mqT, j + 1)
                        pe.wait_ge(s_mread, j + 1)
                        for g in range(n):
                            o = bank[7][:, g * D:(g + 1) * D]
                            nc.tensor.matmul(o, qT[:, g * P:(g + 1) * P], mix_w[:], start=True, stop=False)
                            done = nc.tensor.matmul(o, ones[0:1, :], bout[:], start=False, stop=True)
                        done.then_inc(s_mo, 1)

            def transposes(q, u):
                pe.wait_ge(s_hot, q + 1)
                for k in range(4):
                    last = nc.tensor.transpose(bank[2 + u % 2][:, k * P:(k + 1) * P], hot[:, u, k, :], ident[:])
                last.then_inc(s_tr, 1)

            def node_rows(q, u, tiles):
                pe.wait_ge(s_hotT, q + 1)
                for k in range(4):
                    last = nc.tensor.matmul(bank[4 + u % 2][:, 2 * H * k:2 * H * (k + 1)],
                                            hotT[:, u, k * P:(k + 1) * P],
                                            node_logit[:, ds(tiles[k], 1), :].rearrange("p a h -> p (a h)"),
                                            start=True, stop=True)
                last.then_inc(s_node, 1)

            def sums(q, u, m):
                pe.wait_ge(s_scaled, q * 2 + (m // 2 + 1))
                pe.wait_ge(s_added, q * 4 + (m + 1))
                nc.tensor.matmul(bank[m % 2][:, 0:ROW], hot[:, u, m, :], rows[:, 4 * u + m, :], start=True, stop=True
                                 ).then_inc(s_sum, 1)

            first = tiles_of(PE, 0)
            pe.wait_ge(s_lmax, 1)
            nc.tensor.transpose(bank[6][0:H, 0:P], top_logit[:], ident[:]).then_inc(s_ltp, 1)
            pe.wait_ge(s_lcol, 1)
            nc.tensor.matmul(bank[6][:, 0:H], top_col[0:H, 0:1].to_broadcast([H, P]), ident[0:H, 0:H], start=True,
                             stop=True).then_inc(s_lbc, 1)
            transposes(0, 0)
            transposes(1, 1)
            pe.wait_ge(s_bound, 1)
            node_rows(0, 0, first[0:4])
            transposes(2, 2)
            node_rows(1, 1, first[4:8])

            def turn(i, kind, j, last=False):
                for u in range(U):
                    q = i * U + u
                    if u % 2 == 0 and not (last and u > 1):
                        tiles = tiles_of(PE, i * (4 * U) + (4 * u + 8))
                    for m in range(2):
                        sums(q, u, m)
                    if not (last and u > 1):
                        node_rows(q + 2, (u + 2) % U, tiles[4 * (u % 2):4 * (u % 2) + 4])
                    for m in range(2, 4):
                        sums(q, u, m)
                    if not (last and u > 0):
                        transposes(q + 3, (u + 3) % U)
                    side(kind, j, u)

            run(pe, turn)


def combine(nc, Wr, br, gnn_bias, gnn_gamma, acc, stats, y_sum, router, qkv, ident, ones, bank):
    with ExitStack() as ctx:
        def sb(name, shape, dt=F32):
            return ctx.enter_context(nc.sbuf_tensor("cb_" + name, shape, dt))

        def sem(name):
            return ctx.enter_context(nc.semaphore("m_" + name))

        gain = sb("gain", [P, 2, D])
        zero2 = sb("zero2", [P, 2])
        shift_sum = sb("shift_sum", [P, 1])
        mixed = sb("mixed", [P, 2, SUP, D])
        rden = sb("rden", [P, T, H])
        bn = sb("bn", [P, 2, SUP, 6])
        mv = sb("mv", [P, T, 2, 2])
        shift = sb("shift", [P, T, 2])
        (s_par, s_chain, s_zero, s_den, s_biased, s_var, s_dev, s_shift, s_normed, s_scaled, s_z, s_ysum, s_router) = (
            sem(n) for n in ("par", "chain", "zero", "den", "biased", "var", "dev", "shift", "normed", "scaled", "z",
                             "ysum", "router"))
        block = ctx.enter_context(nc.Block())

        def tiles(s):
            return slice(s * SUP, (s + 1) * SUP)

        turns = [(s, n) for t in range(NS + 1) for s, n in ((t, 0), (t - 1, 1)) if 0 <= s < NS]
        place = {turn: n + 1 for n, turn in enumerate(turns)}

        @block.sync
        def _(sp):
            for n, v in enumerate((gnn_bias, gnn_gamma)):
                sp.dma_start(gain[:, n, :], v.partition_broadcast(P)).then_inc(s_par, 16)
            sp.dma_start(router[:, 0:2, :], Wr.rearrange("(k p) e -> p k e", p=P)).then_inc(s_router, 16)
            sp.dma_start(router[:, 2, :], br.partition_broadcast(P)).then_inc(s_router, 16)
            sp.wait_ge(s_router, 32)

        @block.vector
        def _(dve):
            V = nc.vector
            links = [0]

            def link(ins):
                links[0] += 1
                ins.then_inc(s_chain, 1)
                dve.wait_ge(s_chain, links[0])

            def divide(s):
                z = acc[:, tiles(s), 0:D].rearrange("p t (h c) -> p t h c", c=C)
                V.tensor_tensor(z, z, rden[:, tiles(s), :].unsqueeze(3).to_broadcast([P, SUP, H, C]), ALU.mult
                                ).then_inc(s_den, 1)

            def variance(s, n):
                view = mixed[:, s % 2, :, :] if n == 0 else acc[:, tiles(s), 0:D]
                for g in range(SUP):
                    done = V.bn_stats(bn[:, n, g, :], view[:, g, :])
                link(done)
                for g in range(SUP):
                    done = V.bn_aggr(mv[:, s * SUP + g, n, :], bn[:, n, g, :])
                link(done)
                var = mv[:, tiles(s), n, 1]
                V.tensor_scalar(var, var, LN_EPS, None, ALU.add).then_inc(s_var, 1)

            def scale_shift(s, n):
                m, r = mv[:, tiles(s), n, 0], mv[:, tiles(s), n, 1]
                dve.wait_ge(s_dev, place[s, n])
                link(V.reciprocal(r, r))
                if n == 1:
                    V.tensor_copy(stats[:, tiles(s), :], mv[:, tiles(s), 1, :])
                V.scalar_tensor_tensor(out=shift[:, tiles(s), n], in0=m, scalar=-1.0, in1=r, op0=ALU.mult,
                                       op1=ALU.mult).then_inc(s_shift, 1)

            V.memset(zero2[:], 0.0).then_inc(s_zero, 1)
            link(V.reciprocal(rden[:, tiles(0), :], acc[:, tiles(0), D:ROW]))
            divide(0)
            link(V.reciprocal(rden[:, SUP:, :], acc[:, SUP:, D:ROW]))
            divide(1)
            dve.wait_ge(s_par, 32)
            for s in range(NS + 1):
                if s < NS:
                    dve.wait_ge(s_biased, s + 1)
                    variance(s, 0)
                    if s + 2 < NS:
                        divide(s + 2)
                    scale_shift(s, 0)
                if s >= 1:
                    dve.wait_ge(s_z, s)
                    variance(s - 1, 1)
                    scale_shift(s - 1, 1)
                if s < NS:
                    dve.wait_ge(s_normed, s + 1)
                    V.tensor_tensor(mixed[:, s % 2, :, :], mixed[:, s % 2, :, :],
                                    gain[:, 1:2, :].to_broadcast([P, SUP, D]), ALU.mult).then_inc(s_scaled, 1)
                if s == NS - 1:
                    dve.wait_ge(s_scaled, NS)
                    V.tensor_tensor(acc[:, tiles(s), 0:D], mixed[:, s % 2, :, :], qkv[:, tiles(s), MHID:3 * MHID],
                                    ALU.add).then_inc(s_z, 1)
            dve.wait_ge(s_ysum, 1)
            link(V.tensor_reduce(shift_sum[:], bank[3][:, 0:T], X, ALU.add))
            V.tensor_scalar(y_sum[:, 0:2], bank[2][:, 0:2], shift_sum[:, 0:1], 1.0 / N, ALU.add, ALU.mult
                            ).then_inc(s_zero, 1)

        @block.gpsimd
        def _(pool):
            pool.wait_ge(s_par, 32)

            def bias(s):
                pool.wait_ge(s_den, s + 1)
                nc.gpsimd.tensor_tensor(mixed[:, s % 2, :, :], acc[:, tiles(s), 0:D],
                                        gain[:, 0:1, :].to_broadcast([P, SUP, D]), ALU.add).then_inc(s_biased, 1)

            bias(0)
            bias(1)
            for s in range(NS - 1):
                pool.wait_ge(s_scaled, s + 1)
                nc.gpsimd.tensor_tensor(acc[:, tiles(s), 0:D], mixed[:, s % 2, :, :],
                                        qkv[:, tiles(s), MHID:3 * MHID], ALU.add).then_inc(s_z, 1)
                if s + 2 < NS:
                    pool.wait_ge(s_z, s + 1)
                    bias(s + 2)

        @block.scalar
        def _(act):
            for s, n in turns:
                var = mv[:, tiles(s), n, 1]
                act.wait_ge(s_var, place[s, n])
                nc.scalar.activation(var, var, ACT.Sqrt).then_inc(s_dev, 1)
                act.wait_ge(s_shift, place[s, n])
                if n == 0:
                    for g in range(SUP):
                        t = s * SUP + g
                        done = nc.scalar.activation(mixed[:, s % 2, g, :], mixed[:, s % 2, g, :], ACT.Identity,
                                                    bias=shift[:, t, 0:1], scale=mv[:, t, 0, 1:2])
                    done.then_inc(s_normed, 1)

        @block.tensor
        def _(pe):
            pe.wait_ge(s_zero, 1)
            nc.tensor.matmul(bank[2][:, 0:2], ident[:], zero2[:], start=True, stop=False)
            for s in range(NS):
                pe.wait_ge(s_shift, place[s, 1])
                for g in range(SUP):
                    t = s * SUP + g
                    r = LAST if t == T - 1 else P
                    for k in range(2):
                        nc.tensor.matmul(bank[2][:, k:k + 1], acc[0:r, t, k * P:(k + 1) * P], mv[0:r, t, 1, 1:2],
                                         start=False, stop=t == T - 1 and k == 1)
            nc.tensor.matmul(bank[3][:, 0:T - 1], ones[:], shift[:, 0:T - 1, 1], start=True, stop=True)
            nc.tensor.matmul(bank[3][:, T - 1:T], ones[0:LAST, :], shift[0:LAST, T - 1, 1:2], start=True, stop=True
                             ).then_inc(s_ysum, 1)


def experts(nc, W1, b1, W2, b2, ffn_gamma, ffn_beta, acc, stats, y_sum, router, ident, bank, out):
    with ExitStack() as ctx:
        def sb(name, shape, dt=F32):
            return ctx.enter_context(nc.sbuf_tensor("ex_" + name, shape, dt))

        def sem(name):
            return ctx.enter_context(nc.semaphore("f_" + name))

        HIGH, LOW = 0, 1
        PARTS = ((LOW, HIGH), (HIGH, LOW), (HIGH, HIGH))
        off_i = sb("off_i", [P, FC], I32)
        off_f = sb("off_f", [P, FC])
        a = sb("a", [P, 8, EX])
        top8 = sb("top8", [P, 8])
        top8_i = sb("top8_i", [P, 8], U32)
        which = sb("which", [P, 2])
        scaled = sb("scaled", [P, 2, 2])
        idx_f = sb("idx_f", [P, 2, 2 + FC])
        idx_i = sb("idx_i", [P, 2, 2 + FC], I32)
        one_i = sb("one_i", [P, 2], I32)
        w1 = sb("w1", [P, 2, 2, 2, F], F32R)
        w2 = sb("w2", [P, 2, 2, FC, D], F32R)
        b1c = sb("b1c", [P, 2, FC])
        b2r = sb("b2r", [P, 1, D])
        gain = sb("gain", [P, 2, D])
        y = sb("y", [P, 2, SUP, D])
        yT = sb("yT", [P, 2, 2, 2, SUP * P], F32R)
        hidden = sb("hidden", [P, 4, 4 * P])
        hT = sb("hT", [P, 2, 2 * FC, SUP * P], F32R)
        bn = sb("bn", [P, SUP, 6])
        mv = sb("mv", [P, SUP, 2])
        res = sb("res", [P, 2, SUP, D])
        w1_in = flat(hidden[:]).rearrange("p (e k f) -> p e k f", e=2, k=2)
        w2_in = res[:].rearrange("p b g d -> p (b g) d")[:, 0:2 * FC, :].rearrange("p (e f) d -> p e f d", e=2)
        b2_in = res[:].rearrange("p b g d -> p (b g) d")[:, 2 * FC:2 * FC + 2, :]
        (s_par, s_chain, s_fence, s_lg, s_e, s_ee, s_idx, s_off, s_w1_in, s_w1_high, s_w1, s_b1, s_b2_in, s_b2, s_w2_in, s_w2,
         s_y, s_tp, s_yT, s_yT_low, s_h, s_act, s_low, s_o, s_read, s_yb, s_xb, s_res, s_var, s_dev, s_tail) = (
            sem(n) for n in ("par", "chain", "fence", "lg", "e", "ee", "idx", "off", "w1_in", "w1_high", "w1", "b1", "b2_in",
                             "b2", "w2_in", "w2", "y", "tp", "yT", "yT_low", "h", "act", "low", "o", "read", "yb",
                             "xb", "res", "var", "dev", "tail"))
        s_stored = [sem("stored_even"), sem("stored_odd")]
        block = ctx.enter_context(nc.Block())
        last = (NS - 1) // 2
        PART = 4
        UNITS = 4 * FC

        def supers(eng, body):
            with eng.Fori(0, last) as i:
                for b in range(2):
                    body(i, b, P)
            body(last, 0, LAST)

        halves = ((0, 4), (4, SUP))
        EARLY = UNITS - 5

        @block.sync
        def _(sp):
            sp.dma_start(gain[:, 0, :], ffn_gamma.partition_broadcast(P)).then_inc(s_par, 16)
            sp.dma_start(gain[:, 1, :], ffn_beta.partition_broadcast(P)).then_inc(s_par, 16)
            for b in range(2):
                sp.sem_inc(s_stored[b], 16)

            def body(i, b, rows):
                s = i * 2 + b
                sp.wait_ge(s_res, s + 1)
                if rows == P:
                    sp.dma_start(out[ds(s * (SUP * P), SUP * P), :].rearrange("(g p) d -> p g d", p=P),
                                 res[:, b, :, :]).then_inc(s_stored[b], 16)
                else:
                    split, at = (s * SUP + PART) * P, (T - 1) * P
                    sp.dma_start(out[s * SUP * P:split, :].rearrange("(g p) d -> p g d", p=P),
                                 res[:, b, 0:PART, :]).then_inc(s_stored[b], 16)
                    sp.wait_ge(s_res, s + 2)
                    sp.dma_start(out[split:at, :].rearrange("(g p) d -> p g d", p=P),
                                 res[:, b, PART:SUP - 1, :]).then_inc(s_stored[b], 16)
                    sp.dma_start(out[at:at + rows, :], res[0:rows, b, SUP - 1, :]).then_inc(s_stored[b], 16)
            supers(sp, body)
            sp.wait_ge(s_stored[0], 16 * (last + 4))
            sp.wait_ge(s_stored[1], 16 * (last + 1))

        @block.gpsimd
        def _(pool):
            nc.gpsimd.iota(off_i[:], pattern=[[P, FC]], base=0, channel_multiplier=1).then_inc(s_off, 1)
            pool.wait_ge(s_idx, 1)
            w1_rows = W1.rearrange("e d f -> (e d) f")
            w2_rows = W2.rearrange("e f d -> (e f) d")
            b1_rows = b1.rearrange("e (f a) -> (e f) a", a=1)

            def gather(dest, table, index, signal):
                nc.gpsimd.indirect_dma_start(out=dest, out_offset=None, in_=table,
                                             in_offset=bass.IndirectOffsetOnAxis(ap=index, axis=0)
                                             ).then_inc(signal, 16)

            for e in range(2):
                for k in range(2):
                    gather(w1_in[:, e, k, :], w1_rows, idx_i[:, e, k:k + 1], s_w1_in)
            for e in range(2):
                for f in range(FC):
                    gather(b1c[:, e, f:f + 1], b1_rows, idx_i[:, e, 2 + f:3 + f], s_b1)
            for e in range(2):
                gather(b2_in[:, e, :], b2, one_i[:, e:e + 1], s_b2_in)
            for e in range(2):
                for f in range(FC):
                    gather(w2_in[:, e, f, :], w2_rows, idx_i[:, e, 2 + f:3 + f], s_w2_in)
            pool.wait_ge(s_par, 32)
            pool.wait_ge(s_b2, 1)

            def body(i, b, rows):
                s = i * 2 + b
                x2 = acc[:, ds(s * SUP, SUP), 0:D]
                pool.wait_ge(s_y, s + 1)
                pool.sem_inc(s_fence, 1)
                nc.gpsimd.tensor_tensor(x2, x2, gain[:, 1:2, :].to_broadcast([P, SUP, D]), ALU.add).then_inc(s_xb, 1)
                pool.wait_ge(s_tp, s * 4 + 4)
                pool.sem_inc(s_fence, 1)
                nc.gpsimd.tensor_tensor(y[:, b, :, :], y[:, b, :, :], b2r[:].to_broadcast([P, SUP, D]),
                                        ALU.add).then_inc(s_yb, 1)
            supers(pool, body)

        @block.vector
        def _(dve):
            links = [0]

            def link(ins):
                links[0] += 1
                ins.then_inc(s_chain, 1)
                dve.wait_ge(s_chain, links[0])

            V = nc.vector
            dve.wait_ge(s_off, 1)
            link(V.tensor_copy(off_f[:], off_i[:]))
            dve.wait_ge(s_lg, 1)
            link(V.tensor_tensor(a[:, 0, :], bank[0][:, 0:EX], router[:, 2, :], ALU.add))

            def softmax(src, dst, n):
                link(V.tensor_reduce(top8[:, 0:1], src, X, ALU.max))
                V.tensor_scalar(dst, src, top8[:, 0:1], None, ALU.subtract).then_inc(s_e, 1)
                dve.wait_ge(s_ee, n)
                link(V.tensor_reduce(top8[:, 0:1], dst, X, ALU.add))
                link(V.reciprocal(top8[:, 0:1], top8[:, 0:1]))
                link(V.tensor_scalar(dst, dst, top8[:, 0:1], None, ALU.mult))

            softmax(a[:, 0, :], a[:, 1, :], 1)
            link(V.tensor_scalar(a[:, 2, :], a[:, 1, :], float(N), None, ALU.mult))
            link(V.tensor_scalar(a[:, 3, :], a[:, 2, :], CAP, None, ALU.max))
            link(V.reciprocal(a[:, 4, :], a[:, 3, :]))
            link(V.tensor_scalar(a[:, 4, :], a[:, 4, :], CAP, None, ALU.mult))
            link(V.tensor_tensor(a[:, 5, :], a[:, 1, :], a[:, 4, :], ALU.mult))
            softmax(a[:, 5, :], a[:, 6, :], 2)
            link(V.max(top8[:], a[:, 6, :]))
            link(V.max_index(top8_i[:], top8[:], a[:, 6, :]))
            V.tensor_tensor(a[:, 7, 0:1], top8[:, 1:2], top8[:, 0:1], ALU.subtract).then_inc(s_e, 1)
            link(V.tensor_copy(which[:], top8_i[:, 0:2]))
            V.tensor_copy(one_i[:], which[:])
            V.tensor_scalar(scaled[:, 0, :], which[:], float(D), None, ALU.mult)
            link(V.tensor_scalar(scaled[:, 1, :], which[:], float(F), None, ALU.mult))
            for e in range(2):
                V.tensor_scalar(idx_f[:, e, 0:2], off_f[:, 0:2], scaled[:, 0, e:e + 1], None, ALU.add)
                done = V.tensor_scalar(idx_f[:, e, 2:], off_f[:], scaled[:, 1, e:e + 1], None, ALU.add)
            link(done)
            V.tensor_copy(idx_i[:], idx_f[:]).then_inc(s_idx, 1)

            def norm(i, b):
                s = i * 2 + b
                for g in range(SUP):
                    row = acc[:, ds(s * SUP + g, 1), 0:D].rearrange("p a d -> p (a d)")
                    done = V.tensor_scalar(y[:, b, g, :], row, stats[:, ds(s * SUP + g, 1), 0],
                                           stats[:, ds(s * SUP + g, 1), 1], ALU.subtract, ALU.mult)
                done.then_inc(s_y, 1)

            def yT_lows(i, b, pieces):
                s = i * 2 + b
                for k, half in pieces:
                    lo, hi = halves[half]
                    dve.wait_ge(s_yT, s * 4 + (2 * k + half + 1))
                    V.tensor_tensor(yT[:, b, LOW, k, lo * P:hi * P], bank[half][:, 0:(hi - lo) * P],
                                    yT[:, b, HIGH, k, lo * P:hi * P].bitcast(F32), ALU.subtract).then_inc(s_yT_low, 1)

            norm(0, 0)
            dve.wait_ge(s_ee, 3)
            link(V.tensor_scalar(a[:, 7, 1:2], a[:, 7, 0:1], 1.0, None, ALU.add))
            link(V.reciprocal(a[:, 7, 2:3], a[:, 7, 1:2]))
            link(V.tensor_tensor(a[:, 7, 3:4], a[:, 7, 0:1], a[:, 7, 2:3], ALU.mult))
            yT_lows(0, 0, ((0, 0), (0, 1), (1, 0), (1, 1)))
            for e in range(2):
                dve.wait_ge(s_w1_high, e + 1)
                V.tensor_tensor(w1[:, LOW, e, :, :], w1_in[:, e, :, :], w1[:, HIGH, e, :, :].bitcast(F32),
                                ALU.subtract).then_inc(s_w1, 1)

            def mixture_b2():
                dve.wait_ge(s_b2_in, 16 * 2)
                for e in range(2):
                    done = V.tensor_scalar(b2_in[:, e, :], b2_in[:, e, :], a[:, 7, 2 + e:3 + e], None, ALU.mult)
                link(done)
                V.tensor_tensor(b2r[:, 0, :], b2_in[:, 0, :], b2_in[:, 1, :], ALU.add).then_inc(s_b2, 1)

            def mixture_w2():
                dve.wait_ge(s_w2_in, 16 * 2 * FC)
                for e in range(2):
                    done = V.tensor_scalar(w2_in[:, e, :, :], w2_in[:, e, :, :], a[:, 7, 2 + e:3 + e], None, ALU.mult)
                link(done)
                link(V.tensor_copy(w2[:, HIGH, :, :, :], w2_in))
                done = V.tensor_tensor(w2[:, LOW, :, :, :], w2_in, w2[:, HIGH, :, :, :].bitcast(F32), ALU.subtract)
                link(done)
                dve.sem_inc(s_w2, 1)

            TAIL = 5

            def tail_links(s, made):
                count = [made]

                def tail_link(ins):
                    count[0] += 1
                    ins.then_inc(s_tail, 1)
                    dve.wait_ge(s_tail, s * TAIL + count[0])
                return tail_link

            def tail_statistics(i, b, tail_link, lo=0, hi=SUP):
                dve.sem_inc(s_fence, 1)
                for g in range(lo, hi):
                    done = V.bn_aggr(mv[:, g, :], bn[:, g, :])
                tail_link(done)
                V.tensor_scalar(mv[:, lo:hi, 1], mv[:, lo:hi, 1], LN_EPS, None, ALU.add).then_inc(s_var, 1)

            def tail_center(i, b, tail_link, lo=0, hi=SUP, more=0):
                dve.wait_ge(s_dev, i * 2 + b + (1 + more))
                tail_link(V.reciprocal(mv[:, lo:hi, 1], mv[:, lo:hi, 1]))
                for g in range(lo, hi):
                    done = V.scalar_tensor_tensor(out=res[:, b, g, :], in0=res[:, b, g, :], scalar=mv[:, g, 0:1],
                                                  in1=gain[:, 0, :], op0=ALU.subtract, op1=ALU.mult)
                tail_link(done)

            def tail_add(i, b, tail_link, lo=0, hi=SUP):
                s = i * 2 + b
                dve.wait_ge(s_xb, s + 1)
                dve.sem_inc(s_fence, 1)
                for g in range(lo, hi):
                    row = acc[:, ds(s * SUP + g, 1), 0:D].rearrange("p a d -> p (a d)")
                    done = V.scalar_tensor_tensor(out=res[:, b, g, :], in0=res[:, b, g, :], scalar=mv[:, g, 1:2],
                                                  in1=row, op0=ALU.mult, op1=ALU.add)
                tail_link(done)
                dve.sem_inc(s_res, 1)

            def body(i, b, rows, before):
                s = i * 2 + b
                if before is not None:
                    tail_link = tail_links(before[0] * 2 + before[1], 1)
                for n in range(UNITS):
                    ef, half = n // 2, n % 2
                    lo, hi = halves[half]
                    dve.wait_ge(s_act, s * UNITS + (4 + n + 1))
                    V.tensor_tensor(hT[:, LOW, ef, lo * P:hi * P], hidden[:, n % 4, 0:(hi - lo) * P],
                                    hT[:, HIGH, ef, lo * P:hi * P].bitcast(F32), ALU.subtract).then_inc(s_low, 1)
                    if n == 0 and rows == P:
                        norm(i + b, 1 - b)
                    if n == 2 and before is not None:
                        tail_statistics(*before, tail_link)
                    if n == 5 and before is not None:
                        tail_center(*before, tail_link)
                    if n == 8 and before is not None:
                        tail_add(*before, tail_link)
                    if n == 6 and before is None:
                        mixture_b2()
                    if n == 12 and before is None:
                        mixture_w2()
                    if n == EARLY and rows == P:
                        yT_lows(i + b, 1 - b, ((0, 0), (0, 1)))
                if rows == P:
                    yT_lows(i + b, 1 - b, ((1, 0), (1, 1)))
                dve.wait_ge(s_yb, s + 1)
                dve.wait_ge(s_stored[b], i * 16 + 16)
                if rows != P:
                    own_link = tail_links(s, 0)
                for g in range(SUP + 1):
                    if rows != P and g == PART + 1:
                        own_link(done)
                        tail_statistics(i, b, own_link, 0, PART)
                        tail_center(i, b, own_link, 0, PART)
                        tail_add(i, b, own_link, 0, PART)
                    if g < SUP:
                        dve.wait_ge(s_o, s * SUP + (g + 1))
                        V.tensor_tensor(res[:, b, g, :], bank[6 + (b + g) % 2][:, 0:D], y[:, b, g, :], ALU.add
                                        ).then_inc(s_read, 1)
                    if g >= 1:
                        dve.wait_ge(s_read, s * SUP + (g + 2))
                        done = V.bn_stats(bn[:, g - 1, :], res[:, b, g - 1, :])
                if rows == P:
                    done.then_inc(s_tail, 1)
                    dve.wait_ge(s_tail, s * TAIL + 1)
                else:
                    own_link(done)
                    tail_statistics(i, b, own_link, PART)
                    tail_center(i, b, own_link, PART, more=1)
                    tail_add(i, b, own_link, PART)

            body(0, 0, P, None)
            with dve.Fori(0, last - 1) as i:
                body(i, 1, P, (i, 0))
                body(i + 1, 0, P, (i, 1))
            body(last - 1, 1, P, (last - 1, 0))
            body(last, 0, LAST, (last - 1, 1))

        @block.scalar
        def _(act):
            for n, row in enumerate((1, 6)):
                act.wait_ge(s_e, n + 1)
                nc.scalar.activation(a[:, row, :], a[:, row, :], ACT.Exp).then_inc(s_ee, 1)
            act.wait_ge(s_e, 3)
            nc.scalar.activation(a[:, 7, 0:1], a[:, 7, 0:1], ACT.Exp).then_inc(s_ee, 1)

            def copy_yT(i, b, pieces):
                s = i * 2 + b
                for k, half in pieces:
                    lo, hi = halves[half]
                    act.wait_ge(s_tp, s * 4 + (2 * k + half + 1))
                    nc.scalar.copy(yT[:, b, HIGH, k, lo * P:hi * P], bank[half][:, 0:(hi - lo) * P]).then_inc(s_yT, 1)

            copy_yT(0, 0, ((0, 0), (0, 1), (1, 0), (1, 1)))
            act.wait_ge(s_w1_in, 16 * 4)
            for e in range(2):
                nc.scalar.copy(w1[:, HIGH, e, :, :], w1_in[:, e, :, :]).then_inc(s_w1_high, 1)
            act.wait_ge(s_b1, 16 * 2 * FC)

            def body(i, b, rows, before):
                s = i * 2 + b
                for n in range(UNITS):
                    ef, half = n // 2, n % 2
                    lo, hi = halves[half]
                    unit, bias = bank[2 + n % 4][:, 0:(hi - lo) * P], b1c[:, ef // FC, ef % FC:ef % FC + 1]
                    act.wait_ge(s_h, s * UNITS + (n + 1))
                    if n < 4 and before is None:
                        if n == 2:
                            act.wait_ge(s_w1, 2)
                    else:
                        act.wait_ge(s_low, s * UNITS + (n - 3))
                    nc.scalar.activation(hidden[:, n % 4, 0:(hi - lo) * P], unit, ACT.Gelu, bias=bias)
                    nc.scalar.activation(hT[:, HIGH, ef, lo * P:hi * P], unit, ACT.Gelu, bias=bias).then_inc(s_act, 1)
                    if n == 3 and before is not None:
                        deviations(*before)
                    if n == EARLY and rows == P:
                        copy_yT(i + b, 1 - b, ((0, 0), (0, 1)))
                if rows == P:
                    copy_yT(i + b, 1 - b, ((1, 0), (1, 1)))

            def deviations(i, b, lo=0, hi=SUP, more=0):
                act.wait_ge(s_var, i * 2 + b + (1 + more))
                nc.scalar.activation(mv[:, lo:hi, 1], mv[:, lo:hi, 1], ACT.Sqrt).then_inc(s_dev, 1)

            body(0, 0, P, None)
            with act.Fori(0, last - 1) as i:
                body(i, 1, P, (i, 0))
                body(i + 1, 0, P, (i, 1))
            body(last - 1, 1, P, (last - 1, 0))
            body(last, 0, LAST, (last - 1, 1))
            deviations(last, 0, 0, PART)
            deviations(last, 0, PART, SUP, 1)

        @block.tensor
        def _(pe):
            for k in range(2):
                done = nc.tensor.matmul(bank[0][:, 0:EX], y_sum[:, k:k + 1].to_broadcast([P, P]), router[:, k, :],
                                        start=(k == 0), stop=(k == 1))
            done.then_inc(s_lg, 1)
            pe.sem_inc(s_act, 4)
            pe.sem_inc(s_read, 2)
            pe.sem_inc(s_yT_low, 2)

            def transposes(i, b, pieces):
                s = i * 2 + b
                pe.wait_ge(s_y, s + 1)
                for k, half in pieces:
                    lo, hi = halves[half]
                    pe.wait_ge(s_yT_low, s * 4 + (2 * k + half + 1))
                    for g in range(lo, hi):
                        done = nc.tensor.transpose(bank[half][:, (g - lo) * P:(g - lo + 1) * P],
                                                   y[:, b, g, k * P:(k + 1) * P], ident[:])
                    done.then_inc(s_tp, 1)

            transposes(0, 0, ((0, 0), (0, 1), (1, 0), (1, 1)))
            pe.wait_ge(s_w1, 1)

            def body(i, b, rows):
                s = i * 2 + b
                pe.wait_ge(s_yT_low, s * 4 + 6)
                for n in range(UNITS):
                    ef, half = n // 2, n % 2
                    lo, hi = halves[half]
                    if n == UNITS // 2:
                        pe.wait_ge(s_w1, 2)
                    pe.wait_ge(s_act, s * UNITS + (n + 1))
                    for k in range(2):
                        for m, (wp, yp) in enumerate(PARTS):
                            done = nc.tensor.matmul(bank[2 + n % 4][:, 0:(hi - lo) * P],
                                                    w1[:, wp, ef // FC, k, (ef % FC) * P:(ef % FC + 1) * P],
                                                    yT[:, b, yp, k, lo * P:hi * P], start=(k == 0 and m == 0),
                                                    stop=(k == 1 and m == 2))
                    done.then_inc(s_h, 1)
                    if n == EARLY and rows == P:
                        transposes(i + b, 1 - b, ((0, 0), (0, 1)))
                if rows == P:
                    transposes(i + b, 1 - b, ((1, 0), (1, 1)))
                pe.wait_ge(s_w2, 1)
                for g in range(SUP):
                    pe.wait_ge(s_low, s * UNITS + (UNITS - 1 if g < halves[0][1] else UNITS))
                    pe.wait_ge(s_read, s * SUP + (g + 1))
                    for ef in range(2 * FC):
                        for m, (hp, wp) in enumerate(PARTS):
                            done = nc.tensor.matmul(bank[6 + (b + g) % 2][:, 0:D],
                                                    hT[:, hp, ef, g * P:(g + 1) * P],
                                                    w2[:, wp, ef // FC, ef % FC, :], start=(ef == 0 and m == 0),
                                                    stop=(ef == 2 * FC - 1 and m == 2))
                    done.then_inc(s_o, 1)
            supers(pe, body)


INS = ['x', 'src', 'dst', 'L0_gnn_W', 'L0_gnn_att_src', 'L0_gnn_att_dst', 'L0_gnn_bias', 'L0_gnn_gamma',
       'L0_gnn_beta', 'L0_mix_w_qkv', 'L0_mix_mem_kv', 'L0_mix_w_out', 'L0_mix_b_out', 'L0_mix_g_out',
       'L0_mix_g_pre', 'L0_ffn_Wr', 'L0_ffn_br', 'L0_ffn_W1', 'L0_ffn_b1', 'L0_ffn_W2', 'L0_ffn_b2',
       'L0_ffn_gamma', 'L0_ffn_beta']


def kernel(**inputs):
    import numpy as np
    import concourse.bacc as bacc
    from concourse.bass_utils import run_bass_kernel_spmd

    nc = bacc.Bacc("TRN2", target_bir_lowering=False, num_devices=1)
    arrays, args = {}, []
    for name in INS:
        a = np.ascontiguousarray(inputs[name])
        arrays["in_" + name] = a
        args.append(nc.dram_tensor("in_" + name, a.shape, mybir.dt.from_np(a.dtype), kind="ExternalInput").ap())
    xl_dram = nc.dram_tensor("xl_dram", (N, ROW), F32, kind="Internal").ap()
    base_dram = nc.dram_tensor("base_dram", (N, D), F32, kind="Internal").ap()
    edges_dram = nc.dram_tensor("edges_dram", (GR + 1, 2 * GE), I32, kind="Internal").ap()
    pair_dram = nc.dram_tensor("pair_dram", (PC * P,), I32, kind="Internal").ap()
    out = nc.dram_tensor("out_0", (N, D), F32, kind="ExternalOutput").ap()
    gps_layer(nc, *args, xl_dram, base_dram, edges_dram, pair_dram, out)
    r = run_bass_kernel_spmd(nc, [arrays], core_ids=[0])
    return r.results[0]["out_0"]
```
